# Optimizing a Trainium2 kernel written in Bass

```python
import numpy as np
import jax
import jax.numpy as jnp

def _softmax(x, axis=-1):
    return jax.nn.softmax(x, axis=axis)

def _gelu(x):
    return jax.nn.gelu(x, approximate=True)

def _silu(x):
    return jax.nn.silu(x)

def _sigmoid(x):
    return jax.nn.sigmoid(x)

def _layernorm(x, axis=-1, eps=1e-05):
    m = jnp.mean(x, axis=axis, keepdims=True)
    v = jnp.var(x, axis=axis, keepdims=True)
    return (x - m) / jnp.sqrt(v + eps)

def _scatter_add(tgt, idx, src, axis=0):
    return tgt.at[idx].add(src)

def _segment_sum(src, seg, n):
    return jax.ops.segment_sum(src, seg, n)
kernel_name = 'mk_macaron_d2_jaxref_r8_2f3a3f'

def setup_inputs(seed: int=0):
    np.random.seed(seed)
    _w = jnp.asarray

    def _L0_attn_setup():
        import jax, jax.numpy as jnp
        import numpy as np
        B, SQ, HIDDEN = (2, 256, 256)
        HEADS, GROUPS, KVC = (16, 4, 128)
        HPG = HEADS // GROUPS
        LAYER_INDEX = 1
        SCALE = KVC ** (-0.5)
        key = jax.random.key(seed)
        k1, k2, k3, k4 = jax.random.split(key, 4)
        return {'x': jax.random.normal(k1, (B, SQ, HIDDEN), jnp.float32), 'w_q': jax.random.normal(k2, (HIDDEN, HEADS * KVC), jnp.float32) * 0.02, 'w_kv': jax.random.normal(k3, (HIDDEN, 2 * GROUPS * KVC), jnp.float32) * 0.02, 'w_dense': jax.random.normal(k4, (HEADS * KVC, HIDDEN), jnp.float32) * 0.02}
    _L0_attn_in = _L0_attn_setup()

    def _L0_ffn_setup():
        import jax, jax.numpy as jnp
        import numpy as np
        BLOCK_SIZE = 32
        HIDDEN_SIZE = 256
        MLP_DIM = 2048
        NVFP4_LUT = jnp.array([0.0, 0.5, 1.0, 1.5, 2.0, 3.0, 4.0, 6.0, 0.0, -0.5, -1.0, -1.5, -2.0, -3.0, -4.0, -6.0], dtype=jnp.float32)

        def dequant_nvfp4(W_packed, scales, block=BLOCK_SIZE):
            N = W_packed.shape[0]
            low = W_packed & 15
            high = W_packed >> 4 & 15
            idx = jnp.stack([low, high], axis=-1).reshape(N, -1)
            vals = NVFP4_LUT[idx]
            K = vals.shape[1]
            vals = vals.reshape(N, K // block, block) * scales[:, :, None]
            return vals.reshape(N, K)
        key = jax.random.key(seed)
        ks = jax.random.split(key, 7)
        x = jax.random.normal(ks[0], (4, 32, HIDDEN_SIZE), dtype=jnp.float32)
        gate_W_packed = jax.random.randint(ks[1], (MLP_DIM, HIDDEN_SIZE // 2), 0, 32, dtype=jnp.int32)
        gate_scales = jax.random.uniform(ks[2], (MLP_DIM, HIDDEN_SIZE // BLOCK_SIZE), dtype=jnp.float32) * 0.1 + 0.001
        up_W_packed = jax.random.randint(ks[3], (MLP_DIM, HIDDEN_SIZE // 2), 0, 32, dtype=jnp.int32)
        up_scales = jax.random.uniform(ks[4], (MLP_DIM, HIDDEN_SIZE // BLOCK_SIZE), dtype=jnp.float32) * 0.1 + 0.001
        down_W_packed = jax.random.randint(ks[5], (HIDDEN_SIZE, MLP_DIM // 2), 0, 32, dtype=jnp.int32)
        down_scales = jax.random.uniform(ks[6], (HIDDEN_SIZE, MLP_DIM // BLOCK_SIZE), dtype=jnp.float32) * 0.1 + 0.001
        return {'x': x, 'gate_W_packed': gate_W_packed, 'gate_scales': gate_scales, 'up_W_packed': up_W_packed, 'up_scales': up_scales, 'down_W_packed': down_W_packed, 'down_scales': down_scales}
    _L0_ffn_in = _L0_ffn_setup()

    def _L1_attn_setup():
        import math
        import jax, jax.numpy as jnp
        import numpy as np
        H, D = (16, 128)
        INNER = H * D
        QUERY_DIM = 256
        EPS = 1e-06
        NUM_SEQ_SHIFTS = 16
        MAX_SEQ_LEN = 256
        CHANNEL_SHIFTS = [1, 2, 4, 8]

        def compute_seq_shifts(num_shifts, max_len=256):
            if num_shifts <= 1:
                return [0]
            half = (num_shifts - 1 + 1) // 2
            max_s = max(max_len // 2, 2)
            if half <= 1:
                positive = [1]
            else:
                positive = sorted(set((max(1, round(math.exp(math.log(max_s) * i / (half - 1)))) for i in range(half))))
                while len(positive) < half:
                    new_vals = []
                    for i in range(len(positive) - 1):
                        mid = (positive[i] + positive[i + 1]) // 2
                        if mid not in positive and mid not in new_vals:
                            new_vals.append(mid)
                        if len(positive) + len(new_vals) >= half:
                            break
                    if not new_vals:
                        v = positive[-1] + 1
                        while len(positive) + len(new_vals) < half and v <= max_s:
                            new_vals.append(v)
                            v += 1
                    positive = sorted(set(positive + new_vals))[:half]
            shifts = [0]
            for s in positive:
                shifts.append(s)
                shifts.append(-s)
            return shifts[:num_shifts]
        SEQ_SHIFTS = compute_seq_shifts(NUM_SEQ_SHIFTS, MAX_SEQ_LEN)

        def _rmsnorm(x, g, eps=EPS):
            return x * jax.lax.rsqrt(jnp.mean(x * x, axis=-1, keepdims=True) + eps) * g
        key = jax.random.key(seed)
        ks = jax.random.split(key, 12)
        s = 0.02
        return {'x': jax.random.normal(ks[0], (2, 256, QUERY_DIM), dtype=jnp.float32), 'wq': jax.random.normal(ks[1], (INNER, QUERY_DIM), dtype=jnp.float32) * s, 'bq': jnp.zeros((INNER,), jnp.float32), 'wk': jax.random.normal(ks[2], (INNER, QUERY_DIM), dtype=jnp.float32) * s, 'bk': jnp.zeros((INNER,), jnp.float32), 'wv': jax.random.normal(ks[3], (INNER, QUERY_DIM), dtype=jnp.float32) * s, 'bv': jnp.zeros((INNER,), jnp.float32), 'gq': jnp.ones((INNER,), jnp.float32), 'gk': jnp.ones((INNER,), jnp.float32), 'w_mix': jax.random.normal(ks[4], (1, 1 + len(CHANNEL_SHIFTS)), dtype=jnp.float32) * 0.4, 'wo': jax.random.normal(ks[5], (QUERY_DIM, INNER), dtype=jnp.float32) * s, 'bo': jnp.zeros((QUERY_DIM,), jnp.float32)}
    _L1_attn_in = _L1_attn_setup()

    def _L1_ffn_setup():
        import jax, jax.numpy as jnp
        import numpy as np
        H = 256
        M = 176
        E = 32
        TOPK = 6
        G = 8
        TOPK_G = 4
        SH = 2
        B, S = (1, 128)
        key = jax.random.key(seed)
        ks = jax.random.split(key, 9)
        sc = 0.02
        return {'x': jax.random.normal(ks[0], (B, S, H), dtype=jnp.float32), 'w_router': jax.random.normal(ks[1], (H, E), dtype=jnp.float32) * sc, 'corr_bias': jax.random.normal(ks[2], (E,), dtype=jnp.float32) * 0.1, 'gate_w': jax.random.normal(ks[3], (E, H, M), dtype=jnp.float32) * sc, 'up_w': jax.random.normal(ks[4], (E, H, M), dtype=jnp.float32) * sc, 'down_w': jax.random.normal(ks[5], (E, M, H), dtype=jnp.float32) * sc, 'sh_gate_w': jax.random.normal(ks[6], (H, M * SH), dtype=jnp.float32) * sc, 'sh_up_w': jax.random.normal(ks[7], (H, M * SH), dtype=jnp.float32) * sc, 'sh_down_w': jax.random.normal(ks[8], (M * SH, H), dtype=jnp.float32) * sc}
    _L1_ffn_in = _L1_ffn_setup()
    _d = {'L0_attn_x': _L0_attn_in['x'], 'L0_attn_w_q': _L0_attn_in['w_q'], 'L0_attn_w_kv': _L0_attn_in['w_kv'], 'L0_attn_w_dense': _L0_attn_in['w_dense'], 'L0_ffn_gate_W_packed': _L0_ffn_in['gate_W_packed'], 'L0_ffn_gate_scales': _L0_ffn_in['gate_scales'], 'L0_ffn_up_W_packed': _L0_ffn_in['up_W_packed'], 'L0_ffn_up_scales': _L0_ffn_in['up_scales'], 'L0_ffn_down_W_packed': _L0_ffn_in['down_W_packed'], 'L0_ffn_down_scales': _L0_ffn_in['down_scales'], 'L1_attn_wq': _L1_attn_in['wq'], 'L1_attn_bq': _L1_attn_in['bq'], 'L1_attn_wk': _L1_attn_in['wk'], 'L1_attn_bk': _L1_attn_in['bk'], 'L1_attn_wv': _L1_attn_in['wv'], 'L1_attn_bv': _L1_attn_in['bv'], 'L1_attn_gq': _L1_attn_in['gq'], 'L1_attn_gk': _L1_attn_in['gk'], 'L1_attn_w_mix': _L1_attn_in['w_mix'], 'L1_attn_wo': _L1_attn_in['wo'], 'L1_attn_bo': _L1_attn_in['bo'], 'L1_ffn_w_router': _L1_ffn_in['w_router'], 'L1_ffn_corr_bias': _L1_ffn_in['corr_bias'], 'L1_ffn_gate_w': _L1_ffn_in['gate_w'], 'L1_ffn_up_w': _L1_ffn_in['up_w'], 'L1_ffn_down_w': _L1_ffn_in['down_w'], 'L1_ffn_sh_gate_w': _L1_ffn_in['sh_gate_w'], 'L1_ffn_sh_up_w': _L1_ffn_in['sh_up_w'], 'L1_ffn_sh_down_w': _L1_ffn_in['sh_down_w']}
    _x0 = _d['L0_attn_x']
    _d['L0_attn_x'] = jax.random.normal(jax.random.fold_in(jax.random.key(seed), 1), (8, 256, 256), dtype=_x0.dtype)
    del _x0
    return _d

def reference(L0_attn_x, L0_attn_w_q, L0_attn_w_kv, L0_attn_w_dense, L0_ffn_gate_W_packed, L0_ffn_gate_scales, L0_ffn_up_W_packed, L0_ffn_up_scales, L0_ffn_down_W_packed, L0_ffn_down_scales, L1_attn_wq, L1_attn_bq, L1_attn_wk, L1_attn_bk, L1_attn_wv, L1_attn_bv, L1_attn_gq, L1_attn_gk, L1_attn_w_mix, L1_attn_wo, L1_attn_bo, L1_ffn_w_router, L1_ffn_corr_bias, L1_ffn_gate_w, L1_ffn_up_w, L1_ffn_down_w, L1_ffn_sh_gate_w, L1_ffn_sh_up_w, L1_ffn_sh_down_w):

    def _L0_attn_ref(x, w_q, w_kv, w_dense):
        import jax, jax.numpy as jnp
        import numpy as np
        B, SQ, HIDDEN = (2, 256, 256)
        HEADS, GROUPS, KVC = (16, 4, 128)
        HPG = HEADS // GROUPS
        LAYER_INDEX = 1
        SCALE = KVC ** (-0.5)
        b, sq, _ = x.shape
        sk = sq
        q = jnp.einsum('bsh,he->bse', x, w_q).reshape(b, sq, GROUPS, HPG, KVC)
        kv = jnp.einsum('bsh,he->bse', x, w_kv)
        k, v = jnp.split(kv, 2, axis=-1)
        k = k.reshape(b, sk, GROUPS, KVC)
        v = v.reshape(b, sk, GROUPS, KVC)
        scores = jnp.einsum('bqgpd,bkgd->bgqpk', q, k) * (SCALE / LAYER_INDEX)
        scores = scores.astype(jnp.float32) * LAYER_INDEX
        causal = jnp.arange(sq)[:, None] >= jnp.arange(sk)[None, :]
        scores = jnp.where(causal[None, None, :, None, :], scores, -jnp.inf)
        probs = jax.nn.softmax(scores, axis=-1).astype(x.dtype)
        ctx = jnp.einsum('bgqpk,bkgd->bqgpd', probs, v).reshape(b, sq, HEADS * KVC)
        return jnp.einsum('bse,eh->bsh', ctx, w_dense)

    def _L0_ffn_ref(x, gate_W_packed, gate_scales, up_W_packed, up_scales, down_W_packed, down_scales):
        import jax, jax.numpy as jnp
        import numpy as np
        BLOCK_SIZE = 32
        HIDDEN_SIZE = 256
        MLP_DIM = 2048
        NVFP4_LUT = jnp.array([0.0, 0.5, 1.0, 1.5, 2.0, 3.0, 4.0, 6.0, 0.0, -0.5, -1.0, -1.5, -2.0, -3.0, -4.0, -6.0], dtype=jnp.float32)

        def dequant_nvfp4(W_packed, scales, block=BLOCK_SIZE):
            N = W_packed.shape[0]
            low = W_packed & 15
            high = W_packed >> 4 & 15
            idx = jnp.stack([low, high], axis=-1).reshape(N, -1)
            vals = NVFP4_LUT[idx]
            K = vals.shape[1]
            vals = vals.reshape(N, K // block, block) * scales[:, :, None]
            return vals.reshape(N, K)
        B, S, H = x.shape
        xt = x.reshape(B * S, H)
        Wg = dequant_nvfp4(gate_W_packed, gate_scales)
        Wu = dequant_nvfp4(up_W_packed, up_scales)
        Wd = dequant_nvfp4(down_W_packed, down_scales)
        gate = jnp.einsum('th,nh->tn', xt, Wg)
        up = jnp.einsum('th,nh->tn', xt, Wu)
        gelu = jnp.tanh(0.7978845608028654 * (gate + 0.044715 * gate ** 3)) * gate * 0.5 + gate * 0.5
        inter = gelu * up
        out = jnp.einsum('tn,hn->th', inter, Wd)
        return out.reshape(B, S, H)

    def _L1_attn_ref(x, wq, bq, wk, bk, wv, bv, gq, gk, w_mix, wo, bo):
        import math
        import jax, jax.numpy as jnp
        import numpy as np
        H, D = (16, 128)
        INNER = H * D
        QUERY_DIM = 256
        EPS = 1e-06
        NUM_SEQ_SHIFTS = 16
        MAX_SEQ_LEN = 256
        CHANNEL_SHIFTS = [1, 2, 4, 8]

        def compute_seq_shifts(num_shifts, max_len=256):
            if num_shifts <= 1:
                return [0]
            half = (num_shifts - 1 + 1) // 2
            max_s = max(max_len // 2, 2)
            if half <= 1:
                positive = [1]
            else:
                positive = sorted(set((max(1, round(math.exp(math.log(max_s) * i / (half - 1)))) for i in range(half))))
                while len(positive) < half:
                    new_vals = []
                    for i in range(len(positive) - 1):
                        mid = (positive[i] + positive[i + 1]) // 2
                        if mid not in positive and mid not in new_vals:
                            new_vals.append(mid)
                        if len(positive) + len(new_vals) >= half:
                            break
                    if not new_vals:
                        v = positive[-1] + 1
                        while len(positive) + len(new_vals) < half and v <= max_s:
                            new_vals.append(v)
                            v += 1
                    positive = sorted(set(positive + new_vals))[:half]
            shifts = [0]
            for s in positive:
                shifts.append(s)
                shifts.append(-s)
            return shifts[:num_shifts]
        SEQ_SHIFTS = compute_seq_shifts(NUM_SEQ_SHIFTS, MAX_SEQ_LEN)

        def _rmsnorm(x, g, eps=EPS):
            return x * jax.lax.rsqrt(jnp.mean(x * x, axis=-1, keepdims=True) + eps) * g
        B, L, _ = x.shape
        scale = D ** (-0.5)
        q = _rmsnorm(x @ wq.T + bq, gq).reshape(B, L, H, D)
        k = _rmsnorm(x @ wk.T + bk, gk).reshape(B, L, H, D)
        v = (x @ wv.T + bv).reshape(B, L, H, D)
        shifts = np.asarray(SEQ_SHIFTS)
        idx = (np.arange(L)[None, :] - shifts[:, None]) % L
        k_sh = k[:, idx]
        v_sh = v[:, idx]
        q_all = jnp.stack([q] + [jnp.roll(q, c, axis=-1) for c in CHANNEL_SHIFTS], axis=0)
        scores = jnp.einsum('cblhd,bslhd->blhsc', q_all, k_sh) * scale
        mixed = jnp.einsum('blhsc,c->blhs', scores, w_mix[0])
        attn = jax.nn.softmax(mixed, axis=-1)
        out = jnp.einsum('blhs,bslhd->blhd', attn, v_sh).reshape(B, L, H * D)
        return out @ wo.T + bo

    def _L1_ffn_ref(x, w_router, corr_bias, gate_w, up_w, down_w, sh_gate_w, sh_up_w, sh_down_w):
        import jax, jax.numpy as jnp
        import numpy as np
        H = 256
        M = 176
        E = 32
        TOPK = 6
        G = 8
        TOPK_G = 4
        SH = 2
        B, S = (1, 128)
        b, s, h = x.shape
        xf = x.reshape(-1, h)
        T = xf.shape[0]
        logits = xf @ w_router
        scores = jax.nn.sigmoid(logits)
        sfc = scores + corr_bias
        grp = sfc.reshape(T, G, E // G)
        top2, _ = jax.lax.top_k(grp, 2)
        group_scores = top2.sum(-1)
        _, gidx = jax.lax.top_k(group_scores, TOPK_G)
        group_mask = jax.nn.one_hot(gidx, G, dtype=jnp.float32).sum(axis=1) > 0
        score_mask = jnp.repeat(group_mask, E // G, axis=1)
        masked = jnp.where(score_mask, sfc, -jnp.inf)
        _, topk_idx = jax.lax.top_k(masked, TOPK)
        topk_w = jnp.take_along_axis(scores, topk_idx, axis=1)
        combine = jnp.zeros((T, E), dtype=x.dtype).at[jnp.arange(T)[:, None], topk_idx].add(topk_w)
        g = jnp.einsum('th,ehm->etm', xf, gate_w)
        u = jnp.einsum('th,ehm->etm', xf, up_w)
        eo = jnp.einsum('etm,emh->eth', jax.nn.silu(g) * u, down_w)
        routed = jnp.einsum('te,eth->th', combine, eo)
        shared = jax.nn.silu(xf @ sh_gate_w) * (xf @ sh_up_w) @ sh_down_w
        return (routed + shared).reshape(b, s, h)
    x = L0_attn_x
    x = x + 0.5 * _L0_ffn_ref(_layernorm(x, axis=-1), L0_ffn_gate_W_packed, L0_ffn_gate_scales, L0_ffn_up_W_packed, L0_ffn_up_scales, L0_ffn_down_W_packed, L0_ffn_down_scales)
    x = x + _L0_attn_ref(_layernorm(x, axis=-1), L0_attn_w_q, L0_attn_w_kv, L0_attn_w_dense)
    x = x + 0.5 * _L0_ffn_ref(_layernorm(x, axis=-1), L0_ffn_gate_W_packed, L0_ffn_gate_scales, L0_ffn_up_W_packed, L0_ffn_up_scales, L0_ffn_down_W_packed, L0_ffn_down_scales)
    x = x + 0.5 * _L1_ffn_ref(_layernorm(x, axis=-1), L1_ffn_w_router, L1_ffn_corr_bias, L1_ffn_gate_w, L1_ffn_up_w, L1_ffn_down_w, L1_ffn_sh_gate_w, L1_ffn_sh_up_w, L1_ffn_sh_down_w)
    x = x + _L1_attn_ref(_layernorm(x, axis=-1), L1_attn_wq, L1_attn_bq, L1_attn_wk, L1_attn_bk, L1_attn_wv, L1_attn_bv, L1_attn_gq, L1_attn_gk, L1_attn_w_mix, L1_attn_wo, L1_attn_bo)
    x = x + 0.5 * _L1_ffn_ref(_layernorm(x, axis=-1), L1_ffn_w_router, L1_ffn_corr_bias, L1_ffn_gate_w, L1_ffn_up_w, L1_ffn_down_w, L1_ffn_sh_gate_w, L1_ffn_sh_up_w, L1_ffn_sh_down_w)
    return x

_drawn_inputs = setup_inputs


def setup_inputs(seed=0):
    import zlib

    import numpy as np

    out = dict(_drawn_inputs(seed))
    spreads = {'L1_attn_bq': (0.0, 0.8),
     'L1_attn_bk': (0.0, 2.0),
     'L1_attn_bv': (0.0, 0.8),
     'L1_attn_gq': (1.0, 0.6),
     'L1_attn_gk': (1.0, 0.6),
     'L1_attn_bo': (0.0, 0.8)}
    factors = {'L0_attn_w_q': 8.0,
     'L0_attn_w_kv': 7.085,
     'L0_attn_w_dense': 7.016,
     'L1_attn_wq': 8.0,
     'L1_attn_wk': 8.0,
     'L1_attn_wv': 5.707,
     'L1_attn_w_mix': 8.0,
     'L1_attn_wo': 4.297,
     'L1_ffn_w_router': 8.0,
     'L1_ffn_corr_bias': 8.0,
     'L1_ffn_gate_w': 8.0,
     'L1_ffn_up_w': 8.0,
     'L1_ffn_down_w': 8.0,
     'L1_ffn_sh_gate_w': 8.0,
     'L1_ffn_sh_up_w': 8.0,
     'L1_ffn_sh_down_w': 8.0}
    for name, (base, spread) in spreads.items():
        noise = np.random.default_rng([zlib.crc32(name.encode()), seed]).standard_normal(out[name].shape)
        drawn = base * np.exp(spread * noise) if base else spread * noise
        out[name] = jnp.asarray(drawn.astype(out[name].dtype))
    for name, factor in factors.items():
        out[name] = (out[name] * factor).astype(out[name].dtype)
    return out
```

```python
from contextlib import ExitStack

import numpy as np

import concourse.bass as bass
from concourse import mybir

F32 = mybir.dt.float32
F32R = mybir.dt.float32r
I32 = mybir.dt.int32
BF16 = mybir.dt.bfloat16
ALU = mybir.AluOpType
ACT = mybir.ActivationFunctionType
AX_X = mybir.AxisListType.X



P = 128
HID = 256
KT = HID // P
BATCH, SEQ = 8, 256
TOK = BATCH * SEQ
CH = 512
NCH = TOK // CH
MLP = 2048
T0 = MLP // P
NE, MI, SHARED = 32, 176, 352
ROUTED = NE * MI
T1 = -(-(ROUTED + SHARED) // P)
NG, TOPG, TOPK = 8, 4, 6
WCOL = 3 * HID
BIG = 1.0e30
HEADS, D = 16, 128
GROUPS = 4
CHANNEL_SHIFTS = (1, 2, 4, 8)
SEQ_SHIFTS = (0, 1, -1, 2, -2, 4, -4, 8, -8, 16, -16, 32, -32, 64, -64, 128)


class Core:

    def __init__(self, nc, ctx):
        self.nc, self.ctx, self.named, self.passes, self.route_steps, self.tiles_run, self.primed = nc, ctx, {}, {}, 0, (0, 0), set()

    def sem(self, name):
        if name not in self.named:
            self.named[name] = self.ctx.enter_context(self.nc.semaphore(name))
        return self.named[name]

    def again(self, stage):
        self.passes[stage] = self.passes.get(stage, -1) + 1
        return self.passes[stage]

    def sems(self, name, n=2):
        return [self.sem(f"{name}{i}") for i in range(n)]

    def prime(self, sp, *groups):
        for group in groups:
            for sem in group if isinstance(group, list) else [group]:
                if sem.name not in self.primed:
                    self.primed.add(sem.name)
                    sp.sem_inc(sem, 1)


def load_constants(nc, k, x_t, gather_mats):
    x_in, ones_set = k.sem("x_in"), k.sem("ones_set")
    block = k.nc.Block()
    with block:
        @block.sync
        def _(sp):
            sp.dma_start(k.x[:], x_t).then_inc(x_in, 16)
            sp.dma_start(k.ident[:], gather_mats["ident"]).then_inc(x_in, 16)
            sp.wait_ge(x_in, 32)

        @block.vector
        def _(dve):
            nc.vector.memset(k.mean_mat[:], 1.0 / HID).then_inc(ones_set, 1)
            nc.vector.memset(k.eps[:], 1e-5).then_inc(ones_set, 1)
            dve.wait_ge(ones_set, 2)


def dequantise(nc, k, packed, scales, w_out):
    units = T0 // 2
    with ExitStack() as ctx:
        sb = lambda name, shape, dt: ctx.enter_context(nc.sbuf_tensor(name, shape, dt))
        codes = sb("dq_codes", [P, 2, WCOL], I32)
        scale = sb("dq_scale", [P, 2, WCOL], F32)
        mag = sb("dq_mag", [P, 2, WCOL], I32)
        bit = sb("dq_bit", [P, 2, WCOL], I32)
        steep = sb("dq_steep", [P, 2, WCOL], F32)
        sign = sb("dq_sign", [P, 2, WCOL], F32)
        value = sb("dq_value", [P, 2, WCOL], F32)
        done = sb("dq_done", [P, 2, 2, WCOL], F32)
        codes_in, scale_in, bits_done = k.sems("codes_in"), k.sems("scale_in"), k.sem("bits_done")
        steep_done, sign_done, signed_done = k.sem("steep_done"), k.sem("sign_done"), k.sem("signed_done")
        step, unit_done, stored = k.sem("dq_step"), k.sem("unit_done"), k.sems("dq_stored")
        block = nc.Block()
        with block:
            @block.sync
            def _(sp):
                for u in range(units):
                    b = u % 2
                    if u >= 2:
                        sp.wait_ge(unit_done, u - 1)
                    sp.dma_start(codes[:, b], packed[u]).then_inc(codes_in[b], 16)
                    for g in range(8):
                        sp.dma_start(scale[16 * g:16 * g + 16, b], scales[u, g:g + 1].to_broadcast([16, WCOL])
                                     ).then_inc(scale_in[b], 16)

            @block.scalar
            def _(act):
                for u in range(units):
                    b = u % 2
                    act.wait_ge(bits_done, u + 1)
                    if u:
                        act.wait_ge(unit_done, u)
                    nc.scalar.activation(steep[:], mag[:], ACT.Copy, bias=-8.0, scale=2.0).then_inc(steep_done, 1)
                    nc.scalar.activation(sign[:], bit[:], ACT.Copy, bias=1.0, scale=-0.25).then_inc(sign_done, 1)
                    act.wait_ge(unit_done, u + 1)
                    act.dma_start(w_out[2 * u:2 * u + 2].rearrange("t p c -> p t c"), done[:, b]
                                  ).then_inc(stored[b], 16)
                for b in range(2):
                    act.wait_ge(stored[b], 16 * (units // 2))

            @block.vector
            def _(dve):
                steps = 0
                for u in range(units):
                    b = u % 2
                    dve.wait_ge(codes_in[b], 16 * (u // 2 + 1))
                    if u:
                        dve.wait_ge(sign_done, u)
                    for nib in range(2):
                        if nib:
                            nc.vector.tensor_scalar(mag[:, 1], codes[:, b], 4, 7, ALU.logical_shift_right,
                                                    ALU.bitwise_and)
                            nc.vector.tensor_scalar(bit[:, 1], codes[:, b], 4, 8, ALU.logical_shift_right,
                                                    ALU.bitwise_and).then_inc(bits_done, 1)
                        else:
                            nc.vector.tensor_scalar(mag[:, 0], codes[:, b], 7, None, ALU.bitwise_and)
                            nc.vector.tensor_scalar(bit[:, 0], codes[:, b], 8, None, ALU.bitwise_and)
                    dve.wait_ge(bits_done, u + 1)
                    dve.wait_ge(steep_done, u + 1)
                    nc.vector.scalar_tensor_tensor(out=value[:], in0=mag[:], scalar=-2.0, in1=steep[:],
                                                   op0=ALU.add, op1=ALU.max).then_inc(step, 1)
                    dve.wait_ge(step, steps + 1)
                    nc.vector.scalar_tensor_tensor(out=value[:], in0=mag[:], scalar=0.5, in1=value[:],
                                                   op0=ALU.mult, op1=ALU.max).then_inc(step, 1)
                    dve.wait_ge(step, steps + 2)
                    dve.wait_ge(sign_done, u + 1)
                    nc.vector.tensor_tensor(value[:], value[:], sign[:], ALU.mult).then_inc(step, 1)
                    dve.wait_ge(step, steps + 3)
                    dve.wait_ge(scale_in[b], 128 * (u // 2 + 1))
                    if u >= 2:
                        dve.wait_ge(stored[b], 16 * (u // 2))
                    for nib in range(2):
                        nc.vector.tensor_tensor(
                            done[:, b, :, 0:2 * HID].rearrange("p t (w k c) -> p w t k c", w=2, k=2)[:, :, :, nib],
                            value[:, nib, 0:2 * HID].rearrange("p (w t c) -> p w t c", w=2, t=2),
                            scale[:, b, 0:2 * HID].rearrange("p (w t c) -> p w t c", w=2, t=2), ALU.mult)
                        last = nc.vector.tensor_tensor(done[:, b, nib, 2 * HID:], value[:, nib, 2 * HID:],
                                                       scale[:, b, 2 * HID:], ALU.mult)
                    last.then_inc(unit_done, 1)
                    steps += 3


def layernorm(nc, k, tag, split):
    with ExitStack() as ctx:
        sb = lambda name, shape, dt: ctx.enter_context(nc.sbuf_tensor(f"{name}_{tag}", shape, dt))
        centred = sb("centred", [P, 2, KT, CH], F32)
        square = sb("square", [P, 2, KT, CH], F32)
        root = sb("root", [P, 2, CH], F32)
        rstd = sb("rstd", [P, 2, CH], F32)
        scaled = sb("scaled", [P, 2, KT, CH], F32) if split else None
        mean_done, var_done = k.sem("mean_done"), k.sem("var_done")
        centred_done, square_done = k.sem("centred_done"), k.sem("square_done")
        root_done, rstd_done, scaled_done = k.sem("root_done"), k.sem("rstd_done"), k.sem("scaled_done")
        if split:
            high_done, low_done = k.sem("xn_high_done"), k.sem("xn_low_done")
        C0, S0 = NCH * k.again("layernorm"), NCH * k.again("split") if split else 0
        mean = [k.bank[0], k.bank[1]]
        var = [k.bank[2], k.bank[3]]
        chunk = lambda c: slice(c * CH, (c + 1) * CH)

        def out_of(c):
            return scaled[:, c % 2] if split else k.xn[:, :, chunk(c)]

        block = nc.Block()
        with block:
            @block.tensor
            def _(pe):
                def sum_mean(c):
                    if c >= 2:
                        pe.wait_ge(centred_done, C0 + c - 1)
                    for kt in range(KT):
                        last = nc.tensor.matmul(mean[c % 2][:], k.mean_mat[:], k.x[:, kt, chunk(c)],
                                                start=kt == 0, stop=kt == KT - 1)
                    last.then_inc(mean_done, 1)

                def sum_var(c):
                    pe.wait_ge(square_done, C0 + c + 1)
                    if c >= 2:
                        pe.wait_ge(root_done, C0 + c - 1)
                    for kt in range(KT):
                        last = nc.tensor.matmul(var[c % 2][:], k.mean_mat[:], square[:, c % 2, kt],
                                                start=kt == 0, stop=kt == KT - 1)
                    last.then_inc(var_done, 1)

                sum_mean(0)
                for c in range(NCH):
                    if c + 1 < NCH:
                        sum_mean(c + 1)
                    sum_var(c)

            @block.scalar
            def _(act):
                def take_square(c):
                    act.wait_ge(centred_done, C0 + c + 1)
                    if c >= 2:
                        act.wait_ge(var_done, C0 + c - 1)
                    nc.scalar.activation(square[:, c % 2], centred[:, c % 2], ACT.Square).then_inc(square_done, 1)

                take_square(0)
                for c in range(NCH):
                    if c + 1 < NCH:
                        take_square(c + 1)
                    act.wait_ge(var_done, C0 + c + 1)
                    if c >= 2:
                        act.wait_ge(rstd_done, C0 + c - 1)
                    nc.scalar.activation(root[:, c % 2], var[c % 2][:], ACT.Sqrt, bias=k.eps[:, 0:1]
                                         ).then_inc(root_done, 1)
                    if split:
                        act.wait_ge(scaled_done, C0 + c + 1)
                        nc.scalar.activation(k.xn_high[:, :, chunk(c)], scaled[:, c % 2], ACT.Copy
                                             ).then_inc(high_done, 1)

            @block.vector
            def _(dve):
                def centre(c):
                    dve.wait_ge(mean_done, C0 + c + 1)
                    if c >= 2:
                        dve.wait_ge(square_done, C0 + c - 1)
                        dve.wait_ge(scaled_done, C0 + c - 1)
                    nc.vector.tensor_tensor(centred[:, c % 2], k.x[:, :, chunk(c)],
                                            mean[c % 2][:].unsqueeze(1).to_broadcast([P, KT, CH]), ALU.subtract
                                            ).then_inc(centred_done, 1)

                def low(c):
                    dve.wait_ge(high_done, S0 + c + 1)
                    nc.vector.tensor_tensor(k.xn_low[:, :, chunk(c)], scaled[:, c % 2],
                                            k.xn_high[:, :, chunk(c)].bitcast(F32), ALU.subtract).then_inc(low_done, 1)

                centre(0)
                for c in range(NCH):
                    if c + 1 < NCH:
                        centre(c + 1)
                    dve.wait_ge(root_done, C0 + c + 1)
                    if c >= 2:
                        dve.wait_ge(scaled_done, C0 + c - 1)
                    nc.vector.reciprocal(rstd[:, c % 2], root[:, c % 2]).then_inc(rstd_done, 1)
                    if split and c:
                        low(c - 1)
                    dve.wait_ge(rstd_done, C0 + c + 1)
                    if split and c >= 2:
                        dve.wait_ge(low_done, S0 + c - 1)
                    nc.vector.tensor_tensor(out_of(c), centred[:, c % 2],
                                            rstd[:, c % 2].unsqueeze(1).to_broadcast([P, KT, CH]), ALU.mult
                                            ).then_inc(scaled_done, 1)
                if split:
                    low(NCH - 1)


def feed_forward(nc, k, tag, tiles, w_dram, func, combine=None):
    uses = [(tiles + 1) // 2, tiles // 2]
    C0, base = NCH * k.again("feed_forward"), list(k.tiles_run)
    k.tiles_run = [base[b] + NCH * uses[b] for b in range(2)]
    turn = lambda b, c, h: 1 + base[b] + c * uses[b] + h
    W0 = NCH * k.again("weighed") if combine is not None else C0
    weigh_turn = (lambda b, c, h: 1 + (c + W0) * uses[b] + h) if combine is not None else turn
    pairs = tiles // 2
    gu_cols = 2 * HID + (P if combine is not None else 0)
    with ExitStack() as ctx:
        sb = lambda name, shape, dt: [ctx.enter_context(nc.sbuf_tensor(f"{name}{i}_{tag}", shape, dt)) for i in range(2)]
        gu_raw, gu_high, gu_low = sb("gu_raw", [P, gu_cols], F32), sb("gu_high", [P, gu_cols], F32R), sb("gu_low", [P, 2 * HID], F32R)
        dn_raw, dn_high, dn_low = sb("dn_raw", [P, HID], F32), sb("dn_high", [P, HID], F32R), sb("dn_low", [P, HID], F32R)
        acted, prod = sb("acted", [P, CH], F32), sb("prod", [P, CH], F32)
        weighed = sb("weighed", [P, CH], F32) if combine is not None else prod
        h_high, h_low = sb("h_high", [P, CH], F32R), sb("h_low", [P, CH], F32R)
        y = [k.bank[0], k.bank[1]]
        gate, up, spread = [k.bank[2], k.bank[3]], [k.bank[4], k.bank[5]], [k.bank[6], k.bank[7]]
        gu_in, dn_in = k.sems("gu_in"), k.sems("dn_in")
        gu_high_done, gu_split = k.sems("gu_high_done"), k.sems("gu_split")
        dn_high_done, dn_split = k.sems("dn_high_done"), k.sems("dn_split")
        gu_done, acted_done = k.sems("gu_done"), k.sems("acted_done")
        prod_done = k.sems("prod_done")
        weighed_done = k.sems("weighed_done") if combine is not None else prod_done
        h_high_done, h_split, down_done = k.sems("h_high_done"), k.sems("h_split"), k.sems("down_done")
        y_added = k.sem("y_added")

        block = nc.Block()
        with block:
            @block.sync
            def _(sp):
                k.prime(sp, gu_high_done, gu_split, dn_high_done, dn_split, gu_done, acted_done, prod_done, weighed_done,
                        h_high_done, h_split, down_done, y_added)

                def load(c, t, h, b):
                    n = turn(b, c, h)
                    sp.wait_ge(gu_split[b], n)
                    sp.dma_start(gu_raw[b][:], w_dram[t, :, 0:gu_cols]).then_inc(gu_in[b], 16)
                    sp.wait_ge(dn_split[b], n)
                    sp.dma_start(dn_raw[b][:], w_dram[t, :, gu_cols:gu_cols + HID]).then_inc(dn_in[b], 16)

                with sp.Fori(0, NCH) as c:
                    with sp.Fori(0, pairs) as h:
                        load(c, 2 * h, h, 0)
                        load(c, 2 * h + 1, h, 1)
                    if tiles % 2:
                        load(c, tiles - 1, pairs, 0)

            @block.gpsimd
            def _(pool):
                def gu_low_part(c, h, b):
                    pool.wait_ge(gu_high_done[b], turn(b, c, h) + 1)
                    nc.gpsimd.tensor_tensor(gu_low[b][:], gu_raw[b][:, 0:2 * HID], gu_high[b][:, 0:2 * HID].bitcast(F32),
                                            ALU.subtract).then_inc(gu_split[b], 1)

                def dn_low_part(c, h, b):
                    pool.wait_ge(dn_high_done[b], turn(b, c, h) + 1)
                    nc.gpsimd.tensor_tensor(dn_low[b][:], dn_raw[b][:], dn_high[b][:].bitcast(F32),
                                            ALU.subtract).then_inc(dn_split[b], 1)

                with pool.Fori(0, NCH) as c:
                    gu_low_part(c, 0, 0)
                    gu_low_part(c, 0, 1)
                    with pool.Fori(0, pairs - 1) as h:
                        for b in range(2):
                            dn_low_part(c, h, b)
                            gu_low_part(c, h + 1, b)
                    dn_low_part(c, pairs - 1, 0)
                    if tiles % 2:
                        gu_low_part(c, pairs, 0)
                    dn_low_part(c, pairs - 1, 1)
                    if tiles % 2:
                        dn_low_part(c, pairs, 0)

            @block.tensor
            def _(pe):
                def gate_up(c, h, b):
                    n = turn(b, c, h)
                    pe.wait_ge(gu_split[b], n + 1)
                    pe.wait_ge(weighed_done[b], weigh_turn(b, c, h))
                    cols = bass.ts(c, CH)
                    for out, at in ((gate[b], 0), (up[b], HID)):
                        for kt in range(KT):
                            w = slice(at + kt * P, at + kt * P + P)
                            nc.tensor.matmul(out[:], gu_high[b][:, w], k.xn_high[:, kt, cols], start=kt == 0, stop=False)
                            nc.tensor.matmul(out[:], gu_high[b][:, w], k.xn_low[:, kt, cols], start=False, stop=False)
                            last = nc.tensor.matmul(out[:], gu_low[b][:, w], k.xn_high[:, kt, cols], start=False,
                                                    stop=kt == KT - 1)
                    if combine is not None:
                        sel = gu_high[b][0:NE + 1, 2 * HID:]
                        nc.tensor.matmul(spread[b][:], sel, combine[0][:, cols], start=True, stop=False)
                        last = nc.tensor.matmul(spread[b][:], sel, combine[1][:, cols], start=False, stop=True)
                    last.then_inc(gu_done[b], 1)

                def down(c, h, b, first=False, final=False):
                    n = turn(b, c, h)
                    if first:
                        pe.wait_ge(y_added, c + C0 + 1)
                    pe.wait_ge(dn_split[b], n + 1)
                    pe.wait_ge(h_split[b], n + 1)
                    for kt in range(KT):
                        w = slice(kt * P, kt * P + P)
                        nc.tensor.matmul(y[kt][:], dn_high[b][:, w], h_high[b][:], start=first, stop=False)
                        nc.tensor.matmul(y[kt][:], dn_high[b][:, w], h_low[b][:], start=False, stop=False)
                        last = nc.tensor.matmul(y[kt][:], dn_low[b][:, w], h_high[b][:], start=False, stop=final)
                    last.then_inc(down_done[b], 1)

                with pe.Fori(0, NCH) as c:
                    gate_up(c, 0, 0)
                    gate_up(c, 0, 1)
                    for b in range(2):
                        gate_up(c, 1, b)
                        down(c, 0, b, first=b == 0)
                    with pe.Fori(1, pairs - 1) as h:
                        for b in range(2):
                            gate_up(c, h + 1, b)
                            down(c, h, b)
                    if tiles % 2:
                        gate_up(c, pairs, 0)
                    down(c, pairs - 1, 0)
                    down(c, pairs - 1, 1, final=tiles % 2 == 0)
                    if tiles % 2:
                        down(c, pairs, 0, final=True)

            @block.scalar
            def _(act):
                def gu_high_part(c, h, b):
                    n = turn(b, c, h)
                    act.wait_ge(gu_in[b], 16 * n)
                    act.wait_ge(gu_done[b], n)
                    nc.scalar.activation(gu_high[b][:], gu_raw[b][:], ACT.Copy).then_inc(gu_high_done[b], 1)

                def dn_high_part(c, h, b):
                    n = turn(b, c, h)
                    act.wait_ge(dn_in[b], 16 * n)
                    act.wait_ge(down_done[b], n)
                    nc.scalar.activation(dn_high[b][:], dn_raw[b][:], ACT.Copy).then_inc(dn_high_done[b], 1)

                def values(c, h, b):
                    n = turn(b, c, h)
                    act.wait_ge(gu_done[b], n + 1)
                    act.wait_ge(prod_done[b], n)
                    nc.scalar.activation(acted[b][:], gate[b][:], func).then_inc(acted_done[b], 1)
                    dn_high_part(c, h, b)
                    act.wait_ge(weighed_done[b], weigh_turn(b, c, h) + 1)
                    nc.scalar.activation(h_high[b][:], weighed[b][:], ACT.Copy).then_inc(h_high_done[b], 1)

                with act.Fori(0, NCH) as c:
                    gu_high_part(c, 0, 0)
                    gu_high_part(c, 0, 1)
                    with act.Fori(0, pairs - 1) as h:
                        for b in range(2):
                            values(c, h, b)
                            gu_high_part(c, h + 1, b)
                    values(c, pairs - 1, 0)
                    if tiles % 2:
                        gu_high_part(c, pairs, 0)
                    values(c, pairs - 1, 1)
                    if tiles % 2:
                        values(c, pairs, 0)

            @block.vector
            def _(dve):
                def product(c, h, b):
                    n = turn(b, c, h)
                    dve.wait_ge(acted_done[b], n + 1)
                    dve.wait_ge(h_split[b], n)
                    nc.vector.tensor_tensor(prod[b][:], acted[b][:], up[b][:], ALU.mult).then_inc(prod_done[b], 1)
                    if combine is not None:
                        dve.wait_ge(prod_done[b], n + 1)
                        nc.vector.tensor_tensor(weighed[b][:], prod[b][:], spread[b][:], ALU.mult
                                                ).then_inc(weighed_done[b], 1)
                    dve.wait_ge(h_high_done[b], n + 1)
                    nc.vector.tensor_tensor(h_low[b][:], weighed[b][:], h_high[b][:].bitcast(F32), ALU.subtract
                                            ).then_inc(h_split[b], 1)

                with dve.Fori(0, NCH) as c:
                    with dve.Fori(0, pairs) as h:
                        product(c, h, 0)
                        product(c, h, 1)
                    if tiles % 2:
                        product(c, pairs, 0)
                    last = (tiles - 1) % 2
                    dve.wait_ge(down_done[last], turn(last, c, (tiles - 1) // 2) + 1)
                    for kt in range(KT):
                        add = nc.vector.scalar_tensor_tensor(
                            out=k.x[:, kt, bass.ts(c, CH)], in0=y[kt][:], scalar=0.5, in1=k.x[:, kt, bass.ts(c, CH)],
                            op0=ALU.mult, op1=ALU.add)
                    add.then_inc(y_added, 1)


def route(nc, k, tag, w_router, bias, comb):
    NT = TOK // P
    with ExitStack() as ctx:
        sb = lambda name, shape, dt=F32: ctx.enter_context(nc.sbuf_tensor(f"{name}_{tag}", shape, dt))
        w_raw, w_high, w_low = sb("rw_raw", [P, KT, NE]), sb("rw_high", [P, KT, NE], F32R), sb("rw_low", [P, KT, NE], F32R)
        bias_row = sb("bias_row", [P, NE])
        half_tanh = sb("half_tanh", [NE, TOK])
        score, sfc, masked, weight = sb("score", [P, NT, NE]), sb("sfc", [P, NT, NE]), sb("masked", [P, NT, NE]), sb("weight", [P, NT, NE])
        best2 = sb("best2", [P, NT, NG])
        pair_a, pair_b = sb("pair_a", [P, NT, NG, 2]), sb("pair_b", [P, NT, NG, 2])
        keep = sb("keep", [P, NT, NG])
        chosen = sb("chosen", [P, NT, NE])
        top8 = sb("top8", [P, NT, 8])
        above, equal = sb("above", [P, NT, NE]), sb("equal", [P, NT, NE])
        count = sb("count", [P, NT])
        PAD = 16
        run = [sb(f"run{i}", [P, NT, PAD + NE]) for i in range(2)]
        w_in, bias_in = k.sem("rw_in"), k.sem("rbias_in")
        step, tanh_done, logits_done = k.sem("rstep"), k.sem("tanh_done"), k.sem("logits_done")
        w_ready, turned, weight_done = k.sem("rw_ready"), k.sem("rturned"), k.sem("rweight")
        back, high_done, low_done = k.sem("rback"), k.sem("rhigh"), k.sem("rlow")
        R = k.again("route")
        chunk = lambda c: slice(c * CH, (c + 1) * CH)
        logit_bank = [k.bank[c] for c in range(NCH)]
        turn_bank = k.bank[4]
        block = nc.Block()
        with block:
            @block.sync
            def _(sp):
                sp.dma_start(w_raw[:], w_router).then_inc(w_in, 16)
                sp.dma_start(bias_row[:], bias.to_broadcast([P, NE])).then_inc(bias_in, 16)
                sp.wait_ge(bias_in, 16 * R + 16)

            @block.tensor
            def _(pe):
                pe.wait_ge(w_ready, 2 * R + 2)
                for c in range(NCH):
                    for kt in range(KT):
                        out = logit_bank[c][0:NE, :]
                        nc.tensor.matmul(out, w_high[:, kt], k.xn_high[:, kt, chunk(c)], start=kt == 0, stop=False)
                        nc.tensor.matmul(out, w_high[:, kt], k.xn_low[:, kt, chunk(c)], start=False, stop=False)
                        last = nc.tensor.matmul(out, w_low[:, kt], k.xn_high[:, kt, chunk(c)], start=False, stop=kt == KT - 1)
                    last.then_inc(logits_done, 1)
                for c in range(NCH):
                    pe.wait_ge(tanh_done, NCH * R + c + 1)
                    for t in range(4 * c, 4 * c + 4):
                        last = nc.tensor.transpose(turn_bank[:, t * NE:(t + 1) * NE], half_tanh[:, t * P:(t + 1) * P],
                                                   k.ident[0:NE, 0:NE])
                last.then_inc(turned, 1)
                pe.wait_ge(weight_done, R + 1)
                for c in range(NCH):
                    for t in range(4 * c, 4 * c + 4):
                        last = nc.tensor.transpose(logit_bank[c][0:NE, t % 4 * P:t % 4 * P + P], weight[:, t], k.ident[:])
                    last.then_inc(back, 1)

            @block.scalar
            def _(act):
                for c in range(NCH):
                    act.wait_ge(logits_done, NCH * R + c + 1)
                    nc.scalar.activation(half_tanh[:, chunk(c)], logit_bank[c][0:NE, :], ACT.Tanh, scale=0.5
                                         ).then_inc(tanh_done, 1)
                for c in range(NCH):
                    act.wait_ge(back, NCH * R + c + 1)
                    nc.scalar.activation(comb[0][0:NE, chunk(c)], logit_bank[c][0:NE, :], ACT.Copy).then_inc(high_done, 1)

            @block.vector
            def _(dve):
                steps = [k.route_steps]

                def link(ins):
                    steps[0] += 1
                    ins.then_inc(step, 1)
                    dve.wait_ge(step, steps[0])

                def tt(out, a, b, op):
                    return nc.vector.tensor_tensor(out, a, b, op)

                def choose(mask, values, n, many):
                    for t in range(NT):
                        last = nc.vector.max(top8[:, t], values[:, t])
                    link(last)
                    least = top8[:, :, many - 1:many].to_broadcast([P, NT, n])
                    a, e = above[:, :, 0:n], equal[:, :, 0:n]
                    tt(a, values, least, ALU.is_gt)
                    tt(e, values, least, ALU.is_equal)
                    link(tt(run[0][:, :, PAD:PAD + n], values, least, ALU.is_equal))
                    link(nc.vector.tensor_reduce(count[:], a, AX_X, ALU.add))
                    at, by = 0, 1
                    while by < n:
                        link(tt(run[1 - at][:, :, PAD:PAD + n], run[at][:, :, PAD:PAD + n],
                                run[at][:, :, PAD - by:PAD - by + n], ALU.add))
                        at, by = 1 - at, 2 * by
                    ran = run[at][:, :, PAD:PAD + n]
                    link(tt(ran, ran, count[:].unsqueeze(2).to_broadcast([P, NT, n]), ALU.add))
                    link(nc.vector.scalar_tensor_tensor(out=e, in0=ran, scalar=float(many), in1=e,
                                                        op0=ALU.is_le, op1=ALU.mult))
                    link(tt(mask, a, e, ALU.add))

                nc.vector.memset(comb[0][NE:NE + 1, :].bitcast(F32), 1.0)
                nc.vector.memset(comb[1][NE:NE + 1, :].bitcast(F32), 0.0)
                nc.vector.memset(run[0][:], 0.0)
                link(nc.vector.memset(run[1][:], 0.0))
                dve.wait_ge(w_in, 16 * R + 16)
                nc.vector.tensor_copy(w_high[:], w_raw[:]).then_inc(w_ready, 1)
                dve.wait_ge(w_ready, 2 * R + 1)
                nc.vector.tensor_tensor(w_low[:], w_raw[:], w_high[:].bitcast(F32), ALU.subtract).then_inc(w_ready, 1)
                dve.wait_ge(turned, R + 1)
                link(nc.vector.tensor_scalar(score[:].rearrange("p t e -> p (t e)"), turn_bank[:], 0.5, 0.5,
                                             ALU.mult, ALU.add))
                dve.wait_ge(bias_in, 16 * R + 16)
                link(tt(sfc[:], score[:], bias_row[:].unsqueeze(1).to_broadcast([P, NT, NE]), ALU.add))
                quad = sfc[:].rearrange("p t (g x y) -> p (t g) x y", x=2, y=2)
                a, b = quad[:, :, :, 0], quad[:, :, :, 1]
                sums, maxs = [z[:].rearrange("p t g x -> p (t g) x") for z in (pair_a, pair_b)]
                best = best2[:].rearrange("p t g -> p (t g)")
                tt(sums, a, b, ALU.add)
                link(tt(maxs, a, b, ALU.max))
                link(tt(best, maxs[:, :, 0], maxs[:, :, 1], ALU.add))
                link(tt(best, best, sums[:, :, 0], ALU.max))
                link(tt(best, best, sums[:, :, 1], ALU.max))
                choose(keep[:], best2[:], NG, TOPG)
                kept = keep[:].rearrange("p t g -> p (t g)").unsqueeze(2).to_broadcast([P, NT * NG, NE // NG])
                m4 = masked[:].rearrange("p t (g x) -> p (t g) x", x=NE // NG)
                s4 = sfc[:].rearrange("p t (g x) -> p (t g) x", x=NE // NG)
                link(tt(m4, s4, kept, ALU.mult))
                link(nc.vector.tensor_scalar(keep[:], keep[:], BIG, -BIG, ALU.mult, ALU.add))
                link(tt(m4, m4, kept, ALU.add))
                choose(chosen[:], masked[:], NE, TOPK)
                tt(weight[:], chosen[:], score[:], ALU.mult).then_inc(weight_done, 1)
                for c in range(NCH):
                    dve.wait_ge(high_done, NCH * R + c + 1)
                    last = nc.vector.tensor_tensor(comb[1][0:NE, chunk(c)], logit_bank[c][0:NE, :],
                                                   comb[0][0:NE, chunk(c)].bitcast(F32), ALU.subtract)
                last.then_inc(low_done, 1)
                dve.wait_ge(low_done, R + 1)
                k.route_steps = steps[0]


def attention(nc, k, tag, a, mix):
    MH = HEADS // 2
    C0 = NCH * k.again("attention")
    turn = lambda c, m: 1 + (c + C0) * MH + m
    own = lambda c, m: 1 + c * MH + m
    with ExitStack() as ctx:
        one = lambda name, shape, dt=F32: ctx.enter_context(nc.sbuf_tensor(f"{name}_{tag}", shape, dt))
        two = lambda name, shape, dt=F32: [one(f"{name}{i}", shape, dt) for i in range(2)]
        xc = one("xc", [P, KT, CH])
        mask = one("mask", [P, 2, SEQ])
        qT, kT = two("qT", [P, CH]), two("kT", [P, CH])
        vs = two("vs", [P, 4, D])
        probs, pT, oT = two("probs", [P, 4, SEQ]), two("pT", [P, 2, 2, SEQ]), two("oT", [P, CH])
        peak, shift, total, inverse = two("peak", [P, 4]), two("shift", [P, 4]), two("total", [P, 4]), two("inverse", [P, 4])
        w_out = two("w_out", [P, HID])
        if mix:
            q_all, k_all = one("q_all", [P, HEADS, CH]), one("k_all", [P, HEADS, CH])
            w_qk = two("w_qk", [P, 2 * HID])
            w_val = two("w_val", [P, HID])
            vec = one("vec", [P, 5, HEADS])
            shifts = one("shifts", [P, 1 + len(CHANNEL_SHIFTS), P])
            w_mix = one("w_mix", [P, 1 + len(CHANNEL_SHIFTS)])
            circ = one("circ", [P, P])
            circ_g = two("circ_g", [P, P])
            sq_q, sq_k = two("sq_q", [P, CH]), two("sq_k", [P, CH])
            acc = one("acc", [P, 2, CH])
            rms = one("rms", [P, 2, CH])
            inv_rms = one("inv_rms", [P, 2, CH])
            eps6, b_out = one("eps6", [P, 1]), one("b_out", [P, KT])
        else:
            w_q = two("w_q", [P, HID])
            w_kv = one("w_kv", [P, 2, KT, GROUPS * D])
            k_all = one("k_all", [P, GROUPS, CH])
            v_all = one("v_all", [P, 4, GROUPS * D])
        y = [k.bank[0], k.bank[1]]
        proj, ctx_bank = k.bank[2], k.bank[7]
        s_ps, t_ps = k.pair[0], k.pair[1]
        n = lambda s: f"{s}_{tag}"
        xc_ready, const_in, setup = k.sem("attn_xc_ready"), k.sem(n("const_in")), k.sem(n("setup"))
        head_in, wo_in = k.sems("head_in"), k.sems("wo_in")
        q_proj, q_ready, k_ready = k.sems("attn_q_proj"), k.sems("attn_q_ready"), k.sems(n("k_ready"))
        v_proj, v_ready = k.sems(n("v_proj")), k.sems("attn_v_ready")
        scored, masked, peaked, shifted = k.sems("attn_scored"), k.sems("attn_masked"), k.sems("attn_peaked"), k.sems("attn_shifted")
        exped, inverted, normed = k.sems("attn_exped"), k.sems("attn_inverted"), k.sems("attn_normed")
        turned, pt_ready, ctx_done, o_ready, y_done = (k.sems("attn_turned"), k.sems("attn_pt_ready"), k.sems("attn_ctx_done"),
                                                       k.sems("attn_o_ready"), k.sems("attn_y_done"))
        y_added = k.sem("attn_y_added")
        if mix:
            qk_in, qk_proj, qk_biased = k.sems(n("qk_in")), k.sems(n("qk_proj")), k.sems(n("qk_biased"))
            summed = k.sems(n("summed"))
            acc_zero, sums_done, rms_done, inv_done = k.sem(n("acc_zero")), k.sem(n("sums_done")), k.sem(n("rms_done")), k.sem(n("inv_done"))
            circ_ready = k.sems(n("circ_ready"))
        else:
            kv_proj, kv_ready = k.sem(n("kv_proj")), k.sem(n("kv_ready"))

        def before(sems, b, t):
            return (sems[1], t) if b == 0 else (sems[0], t + 1)

        def steps(eng, c, step):
            step(0, 0, True, 0)
            step(0, 1, False, 0)
            with eng.Fori(1, MH - 1) as m:
                step(m, 0, False, 0)
                step(m, 1, False, 0)
            step(MH - 1, 0, False, 1)
            step(MH - 1, 1, False, 2)

        block = nc.Block()
        with block:
            @block.sync
            def _(sp):
                k.prime(sp, q_proj, q_ready, v_ready, scored, masked, peaked, shifted, exped, inverted, normed, turned,
                        pt_ready, ctx_done, o_ready, y_done, y_added, v_proj, k_ready)
                if mix:
                    k.prime(sp, qk_proj, qk_biased, summed, circ_ready)
                sp.dma_start(mask[:], a["near_mask" if mix else "causal_mask"]).then_inc(const_in, 16)
                if mix:
                    sp.dma_start(vec[:], a["attn1_vec"]).then_inc(const_in, 16)
                    sp.dma_start(b_out[:], a["attn1_bo"]).then_inc(const_in, 16)
                    sp.dma_start(shifts[:], a["shift_mats"]).then_inc(const_in, 16)
                    sp.dma_start(w_mix[:], a["w_mix"].to_broadcast([P, 1 + len(CHANNEL_SHIFTS)])).then_inc(const_in, 16)
                else:
                    sp.dma_start(w_kv[:], a["attn0_kv"]).then_inc(const_in, 16)

                def load_in(c, m):
                    for b in range(2):
                        if mix:
                            sp.wait_ge(v_proj[b], own(c, m))
                            sp.dma_start(w_val[b][:], a["attn1_v"][2 * m + b]).then_inc(head_in[b], 16)
                        else:
                            sp.wait_ge(q_proj[b], turn(c, m))
                            sp.dma_start(w_q[b][:], a["attn0_q"][2 * m + b]).then_inc(head_in[b], 16)

                def load_out(c, m):
                    for b in range(2):
                        sp.wait_ge(y_done[b], turn(c, m))
                        sp.dma_start(w_out[b][:], a["attn1_o" if mix else "attn0_o"][2 * m + b]).then_inc(wo_in[b], 16)

                with sp.Fori(0, NCH) as c:
                    if mix:
                        with sp.Fori(0, MH) as m:
                            for b in range(2):
                                sp.wait_ge(qk_proj[b], own(c, m))
                                sp.dma_start(w_qk[b][:], a["attn1_qk"][2 * m + b]).then_inc(qk_in[b], 16)
                    load_in(c, 0)
                    with sp.Fori(1, MH) as m:
                        load_in(c, m)
                        load_out(c, m - 1)
                    load_out(c, MH - 1)

            @block.tensor
            def _(pe):
                def query_key(c, m, b):
                    t = turn(c, m)
                    pe.wait_ge(xc_ready, c + C0 + 1)
                    pe.wait_ge(qk_in[b], 16 * own(c, m))
                    pe.wait_ge(qk_biased[b], own(c, m))
                    for out, at in ((s_ps[:, b], 0), (t_ps[:, b], HID)):
                        for kt in range(KT):
                            last = nc.tensor.matmul(out, w_qk[b][:, at + kt * P:at + kt * P + P], xc[:, kt],
                                                    start=kt == 0, stop=kt == KT - 1)
                    last.then_inc(qk_proj[b], 1)

                def queries(c, m, b, first=False):
                    t = turn(c, m)
                    pe.wait_ge(*before(q_ready, b, t))
                    if mix:
                        pe.wait_ge(v_ready[b], t)
                        if first:
                            pe.wait_ge(v_ready[1], t)
                        pe.wait_ge(circ_ready[b], own(c, m) + 1)
                        last = nc.tensor.matmul(proj[:], circ_g[b][:], q_all[:, 2 * m + b], start=True, stop=True)
                    else:
                        pe.wait_ge(head_in[b], 16 * t)
                        for kt in range(KT):
                            last = nc.tensor.matmul(proj[:], w_q[b][:, kt * P:kt * P + P], xc[:, kt],
                                                    start=kt == 0, stop=kt == KT - 1)
                    last.then_inc(q_proj[b], 1)

                def values(c, m, b, last_head=False):
                    t = turn(c, m)
                    pe.wait_ge(head_in[b], 16 * t)
                    if not last_head:
                        pe.wait_ge(q_ready[1 - b], t + 1 + b)
                    pe.wait_ge(*before(v_ready, b, t))
                    for i in range(4):
                        for kt in range(KT):
                            last = nc.tensor.matmul(proj[:, i * D:(i + 1) * D], xc[:, kt, i * P:(i + 1) * P],
                                                    w_val[b][:, kt * P:kt * P + P], start=kt == 0, stop=kt == KT - 1)
                    last.then_inc(v_proj[b], 1)

                def scores(c, m, b):
                    t = turn(c, m)
                    pe.wait_ge(q_ready[b], t + 1)
                    if mix:
                        pe.wait_ge(k_ready[b], own(c, m) + 1)
                    pe.wait_ge(*before(masked, b, t))
                    for s in range(2):
                        for i in range(2):
                            at = s * SEQ
                            keys = kT[b][:, at:at + SEQ] if mix else k_all[:, m // 2, at:at + SEQ]
                            last = nc.tensor.matmul(s_ps[:, s, i * SEQ:(i + 1) * SEQ], qT[b][:, at + i * P:at + i * P + P],
                                                    keys, start=True, stop=True)
                    last.then_inc(scored[b], 1)

                def turn_probs(c, m, b):
                    t = turn(c, m)
                    pe.wait_ge(normed[b], t + 1)
                    pe.wait_ge(*before(pt_ready, b, t))
                    for s in range(2):
                        for j in range(2):
                            for i in range(2):
                                last = nc.tensor.transpose(t_ps[:, s, j * SEQ + i * P:j * SEQ + i * P + P],
                                                           probs[b][:, 2 * s + i, j * P:(j + 1) * P], k.ident[:])
                    last.then_inc(turned[b], 1)

                def context(c, m, b):
                    t = turn(c, m)
                    pe.wait_ge(pt_ready[b], t + 1)
                    pe.wait_ge(v_ready[b], t + 1)
                    pe.wait_ge(*before(o_ready, b, t))
                    for s in range(2):
                        for j in range(2):
                            last = nc.tensor.matmul(ctx_bank[:, s * SEQ:(s + 1) * SEQ], vs[b][:, 2 * s + j], pT[b][:, s, j],
                                                    start=j == 0, stop=j == 1)
                    last.then_inc(ctx_done[b], 1)

                def project_out(c, m, b, first, final):
                    t = turn(c, m)
                    if first:
                        pe.wait_ge(y_added, c + C0 + 1)
                    pe.wait_ge(wo_in[b], 16 * t)
                    pe.wait_ge(o_ready[b], t + 1)
                    for kt in range(KT):
                        last = nc.tensor.matmul(y[kt][:], w_out[b][:, kt * P:kt * P + P], oT[b][:], start=first, stop=final)
                    last.then_inc(y_done[b], 1)

                pe.wait_ge(setup, 2 if mix else 1)
                with pe.Fori(0, NCH) as c:
                    if mix:
                        with pe.Fori(0, MH) as m:
                            query_key(c, m, 0)
                            query_key(c, m, 1)
                        pe.wait_ge(summed[1], own(c, MH - 1) + 1)
                        for i in range(2):
                            last = nc.tensor.matmul(s_ps[:, i], k.mean_mat[:], acc[:, i], start=True, stop=True)
                        last.then_inc(sums_done, 1)
                    else:
                        pe.wait_ge(xc_ready, c + C0 + 1)
                        for i in range(8):
                            bank = s_ps[:, i % 2]
                            if i >= 2:
                                pe.wait_ge(kv_ready, c * 8 + i - 1)
                            for kt in range(KT):
                                if i < GROUPS:
                                    w, z = w_kv[:, 0, kt, i * D:(i + 1) * D], xc[:, kt]
                                else:
                                    w, z = xc[:, kt, (i - 4) * P:(i - 3) * P], w_kv[:, 1, kt]
                                last = nc.tensor.matmul(bank, w, z, start=kt == 0, stop=kt == KT - 1)
                            last.then_inc(kv_proj, 1)
                        pe.wait_ge(kv_ready, c * 8 + 8)
                    queries(c, 0, 0, first=True)
                    if mix:
                        queries(c, 0, 1)
                        values(c, 0, 0)
                    scores(c, 0, 0)
                    if not mix:
                        queries(c, 0, 1)

                    def step(m, b, first, last):
                        nxt = (m, 1) if b == 0 else (m + 1, 0)
                        if last < 2:
                            scores(c, *nxt)
                        turn_probs(c, m, b)
                        if last == 0:
                            queries(c, m + 1, b)
                        if not first:
                            prev = (m, 0) if b == 1 else (m - 1, 1)
                            project_out(c, *prev, first=isinstance(m, int) and m == 0, final=False)
                        if mix and last < 2:
                            values(c, *nxt, last_head=last == 1)
                        context(c, m, b)

                    steps(pe, c, step)
                    project_out(c, MH - 1, 1, first=False, final=True)

            @block.scalar
            def _(act):
                def bias_qk(c, m, b):
                    t = turn(c, m)
                    act.wait_ge(qk_proj[b], own(c, m) + 1)
                    act.wait_ge(summed[b], own(c, m))
                    h = 2 * m + b
                    nc.scalar.activation(q_all[:, h], s_ps[:, b], ACT.Identity, bias=vec[:, 0, bass.ds(h, 1)])
                    nc.scalar.activation(k_all[:, h], t_ps[:, b], ACT.Identity, bias=vec[:, 1, bass.ds(h, 1)])
                    nc.scalar.activation(sq_q[b][:], s_ps[:, b], ACT.Square, bias=vec[:, 0, bass.ds(h, 1)])
                    nc.scalar.activation(sq_k[b][:], t_ps[:, b], ACT.Square, bias=vec[:, 1, bass.ds(h, 1)]
                                         ).then_inc(qk_biased[b], 1)

                def take_queries(c, m, b):
                    t = turn(c, m)
                    if mix:
                        act.wait_ge(q_proj[b], t)
                        h = 2 * m + b
                        nc.scalar.activation(circ_g[b][:], circ[:], ACT.Copy, scale=vec[:, 3, bass.ds(h, 1)]
                                             ).then_inc(circ_ready[b], 1)
                    else:
                        act.wait_ge(q_proj[b], t + 1)
                        act.wait_ge(scored[b], t)
                        nc.scalar.activation(qT[b][:], proj[:], ACT.Copy).then_inc(q_ready[b], 1)

                def take_values(c, m, b):
                    t = turn(c, m)
                    act.wait_ge(ctx_done[b], t)
                    if mix:
                        act.wait_ge(v_proj[b], own(c, m) + 1)
                        src = proj[:].rearrange("p (i d) -> p i d", i=4)
                    else:
                        src = v_all[:, :, bass.ds(m // 2 * D, D)]
                    nc.scalar.activation(vs[b][:], src, ACT.Copy).then_inc(v_ready[b], 1)

                def take_turned(c, m, b):
                    t = turn(c, m)
                    act.wait_ge(turned[b], t + 1)
                    act.wait_ge(ctx_done[b], t)
                    nc.scalar.activation(pT[b][:].rearrange("p s j q -> p (s j q)"), t_ps[:].rearrange("p s c -> p (s c)"),
                                         ACT.Copy).then_inc(pt_ready[b], 1)

                def exponentials(c, m, b):
                    t = turn(c, m)
                    act.wait_ge(shifted[b], t + 1)
                    for i in range(4):
                        last = nc.scalar.activation(probs[b][:, i], probs[b][:, i], ACT.Exp, bias=shift[b][:, i:i + 1],
                                                    scale=D ** -0.5, accum_out=total[b][:, i:i + 1])
                    last.then_inc(exped[b], 1)

                def take_context(c, m, b):
                    t = turn(c, m)
                    act.wait_ge(ctx_done[b], t + 1)
                    act.wait_ge(y_done[b], t)
                    nc.scalar.activation(oT[b][:], ctx_bank[:], ACT.Identity, bias=vec[:, 2, bass.ds(2 * m + b, 1)]
                                         ).then_inc(o_ready[b], 1)

                act.wait_ge(setup, 2 if mix else 1)
                with act.Fori(0, NCH) as c:
                    act.wait_ge(y_added, c + C0 + 1)
                    nc.scalar.activation(xc[:], k.xn[:, :, bass.ts(c, CH)], ACT.Copy).then_inc(xc_ready, 1)
                    if mix:
                        with act.Fori(0, MH) as m:
                            bias_qk(c, m, 0)
                            bias_qk(c, m, 1)
                        act.wait_ge(sums_done, c + 1)
                        nc.scalar.activation(rms[:], s_ps[:], ACT.Sqrt, bias=eps6[:, 0:1], scale=HID / (HEADS * D)
                                             ).then_inc(rms_done, 1)
                    else:
                        for i in range(8):
                            act.wait_ge(kv_proj, c * 8 + i + 1)
                            dst = k_all[:, i] if i < GROUPS else v_all[:, i - 4]
                            nc.scalar.activation(dst, s_ps[:, i % 2], ACT.Copy).then_inc(kv_ready, 1)
                        act.wait_ge(kv_ready, c * 8 + 8)
                    take_queries(c, 0, 0)
                    take_queries(c, 0, 1) if mix else None
                    take_values(c, 0, 0)
                    if not mix:
                        take_queries(c, 0, 1)
                    exponentials(c, 0, 0)

                    def step(m, b, first, last):
                        nxt = (m, 1) if b == 0 else (m + 1, 0)
                        take_turned(c, m, b)
                        if last == 0:
                            take_queries(c, m + 1, b)
                        if last < 2:
                            if not mix:
                                take_values(c, *nxt)
                            exponentials(c, *nxt)
                            if mix:
                                take_values(c, *nxt)
                        if mix:
                            take_context(c, m, b)

                    steps(act, c, step)

            @block.vector
            def _(dve):
                def sum_squares(c, m, b):
                    t = turn(c, m)
                    dve.wait_ge(acc_zero, c + len(CHANNEL_SHIFTS))
                    dve.wait_ge(qk_biased[b], own(c, m) + 1)
                    dve.wait_ge(*before(summed, b, own(c, m)))
                    nc.vector.tensor_tensor(acc[:, 0], acc[:, 0], sq_q[b][:], ALU.add)
                    nc.vector.tensor_tensor(acc[:, 1], acc[:, 1], sq_k[b][:], ALU.add).then_inc(summed[b], 1)

                def take_queries(c, m, b):
                    t = turn(c, m)
                    dve.wait_ge(q_proj[b], t + 1)
                    dve.wait_ge(scored[b], t)
                    nc.vector.tensor_tensor(qT[b][:], proj[:], inv_rms[:, 0], ALU.mult).then_inc(q_ready[b], 1)
                    h = 2 * m + b
                    nc.vector.scalar_tensor_tensor(out=kT[b][:], in0=k_all[:, h], scalar=vec[:, 4, bass.ds(h, 1)],
                                                   in1=inv_rms[:, 1], op0=ALU.mult, op1=ALU.mult).then_inc(k_ready[b], 1)

                def mask_scores(c, m, b):
                    t = turn(c, m)
                    dve.wait_ge(scored[b], t + 1)
                    dve.wait_ge(turned[b], t)
                    nc.vector.tensor_tensor(probs[b][:].rearrange("p (s i) k -> p s (i k)", s=2), s_ps[:],
                                            mask[:].rearrange("p i k -> p (i k)").unsqueeze(1).to_broadcast([P, 2, CH]),
                                            ALU.add).then_inc(masked[b], 1)
                    dve.wait_ge(masked[b], t + 1)
                    nc.vector.tensor_reduce(peak[b][:], probs[b][:], AX_X, ALU.max).then_inc(peaked[b], 1)
                    dve.wait_ge(peaked[b], t + 1)
                    nc.vector.tensor_scalar(shift[b][:], peak[b][:], -(D ** -0.5), None, ALU.mult).then_inc(shifted[b], 1)

                def normalise(c, m, b):
                    t = turn(c, m)
                    dve.wait_ge(exped[b], t + 1)
                    nc.vector.reciprocal(inverse[b][:], total[b][:]).then_inc(inverted[b], 1)
                    dve.wait_ge(inverted[b], t + 1)
                    nc.vector.tensor_tensor(probs[b][:], probs[b][:], inverse[b][:].unsqueeze(2).to_broadcast([P, 4, SEQ]),
                                            ALU.mult).then_inc(normed[b], 1)

                def take_context(c, m, b):
                    t = turn(c, m)
                    dve.wait_ge(ctx_done[b], t + 1)
                    dve.wait_ge(y_done[b], t)
                    nc.vector.tensor_copy(oT[b][:], ctx_bank[:]).then_inc(o_ready[b], 1)

                dve.wait_ge(const_in, 80 if mix else 32)
                if mix:
                    nc.vector.memset(eps6[:], 1e-6)
                    nc.vector.tensor_scalar(circ[:], shifts[:, 0], w_mix[:, 0:1], None, ALU.mult).then_inc(setup, 1)
                    for i in range(len(CHANNEL_SHIFTS)):
                        dve.wait_ge(setup, 1) if i == 0 else dve.wait_ge(acc_zero, i)
                        last = nc.vector.scalar_tensor_tensor(out=circ[:], in0=shifts[:, i + 1], scalar=w_mix[:, i + 1:i + 2],
                                                              in1=circ[:], op0=ALU.mult, op1=ALU.add)
                        last.then_inc(acc_zero if i + 1 < len(CHANNEL_SHIFTS) else setup, 1)
                else:
                    nc.vector.memset(peak[0][:], 0.0).then_inc(setup, 1)
                with dve.Fori(0, NCH) as c:
                    if mix:
                        nc.vector.memset(acc[:], 0.0).then_inc(acc_zero, 1)
                        with dve.Fori(0, MH) as m:
                            sum_squares(c, m, 0)
                            sum_squares(c, m, 1)
                        dve.wait_ge(rms_done, c + 1)
                        nc.vector.reciprocal(inv_rms[:], rms[:]).then_inc(inv_done, 1)
                        dve.wait_ge(inv_done, c + 1)
                        take_queries(c, 0, 0)
                        take_queries(c, 0, 1)
                    mask_scores(c, 0, 0)
                    normalise(c, 0, 0)

                    def step(m, b, first, last):
                        nxt = (m, 1) if b == 0 else (m + 1, 0)
                        if last < 2:
                            mask_scores(c, *nxt)
                        if mix and last == 0:
                            take_queries(c, m + 1, b)
                        if last < 2:
                            normalise(c, *nxt)
                        if not mix:
                            take_context(c, m, b)

                    steps(dve, c, step)
                    dve.wait_ge(y_done[1], turn(c, MH - 1) + 1)
                    for kt in range(KT):
                        x = k.x[:, kt, bass.ts(c, CH)]
                        if mix:
                            add = nc.vector.scalar_tensor_tensor(out=x, in0=y[kt][:], scalar=b_out[:, kt:kt + 1], in1=x,
                                                                 op0=ALU.add, op1=ALU.add)
                        else:
                            add = nc.vector.tensor_tensor(x, y[kt][:], x, ALU.add)
                    add.then_inc(y_added, 1)


def store_result(nc, k, out):
    stored = k.sem("result_stored")
    block = nc.Block()
    with block:
        @block.sync
        def _(sp):
            sp.dma_start(out, k.x[:]).then_inc(stored, 16)
            sp.wait_ge(stored, 16)


def macaron(nc, a, out):
    w0 = nc.dram_tensor("ffn0_weights", [T0, P, WCOL], F32, kind="Internal").ap()
    with ExitStack() as ctx:
        k = Core(nc, ctx)
        sb = lambda name, shape, dt: ctx.enter_context(nc.sbuf_tensor(name, shape, dt))
        k.x = sb("x", [P, KT, TOK], F32)
        k.mean_mat = sb("mean_mat", [P, P], F32)
        k.eps = sb("eps", [P, 1], F32)
        k.ident = sb("ident", [P, P], F32)
        ps = lambda name, *shape: ctx.enter_context(nc.psum_tensor(name, [P, *shape, CH], F32))
        low, k.pair, high = [ps(f"bank{i}") for i in range(3)], [ps("banks34", 2), ps("banks56", 2)], ps("bank7")
        k.bank = low + [k.pair[0][:, 0], k.pair[0][:, 1], k.pair[1][:, 0], k.pair[1][:, 1], high]
        load_constants(nc, k, a["x"], a)
        dequantise(nc, k, a["ffn0_codes"], a["ffn0_scales"], w0)

        def ffn0(tag):
            with ExitStack() as inner:
                k.xn_high = inner.enter_context(nc.sbuf_tensor(f"xn_high_{tag}", [P, KT, TOK], F32R))
                k.xn_low = inner.enter_context(nc.sbuf_tensor(f"xn_low_{tag}", [P, KT, TOK], F32R))
                layernorm(nc, k, tag, True)
                feed_forward(nc, k, tag, T0, w0, ACT.Gelu_apprx_tanh)

        def ffn1(tag):
            with ExitStack() as inner:
                k.xn_high = inner.enter_context(nc.sbuf_tensor(f"xn_high_{tag}", [P, KT, TOK], F32R))
                k.xn_low = inner.enter_context(nc.sbuf_tensor(f"xn_low_{tag}", [P, KT, TOK], F32R))
                layernorm(nc, k, tag, True)
                comb = [inner.enter_context(nc.sbuf_tensor(f"comb{i}_{tag}", [NE + 1, TOK], F32R)) for i in range(2)]
                route(nc, k, tag, a["router"], a["router_bias"], comb)
                feed_forward(nc, k, tag, T1, a["ffn1_weights"], ACT.Silu, comb)

        def attn(tag, mix):
            with ExitStack() as inner:
                k.xn = inner.enter_context(nc.sbuf_tensor(f"xn_{tag}", [P, KT, TOK], F32))
                layernorm(nc, k, tag, False)
                attention(nc, k, tag, a, mix)

        ffn0("f0")
        attn("a0", False)
        ffn0("f1")
        ffn1("f2")
        attn("a1", True)
        ffn1("f3")
        store_result(nc, k, out)


def planes(w):
    return w.reshape(P, KT, *w.shape[1:])


def lay_out(i):
    a = {}
    tokens = lambda x: np.ascontiguousarray(x)
    a["x"] = tokens(i["L0_attn_x"].reshape(TOK, P, KT).transpose(1, 2, 0))
    units = T0 // 2

    def rows(w):
        return w.reshape(units, P, 2, -1).transpose(0, 3, 2, 1)

    def down(w):
        return w.reshape(P, KT, units, -1).transpose(2, 3, 1, 0)

    join = lambda g, u, d: np.concatenate([z.reshape(units, -1, HID) for z in (g, u, d)], axis=2)
    a["ffn0_codes"] = join(rows(i["L0_ffn_gate_W_packed"]), rows(i["L0_ffn_up_W_packed"]),
                           down(i["L0_ffn_down_W_packed"]))
    a["ffn0_scales"] = join(rows(i["L0_ffn_gate_scales"]), rows(i["L0_ffn_up_scales"]),
                            down(i["L0_ffn_down_scales"]))
    def up(w, shared):
        w = np.concatenate([w.transpose(1, 0, 2).reshape(HID, ROUTED), shared], axis=1)
        return np.pad(w, ((0, 0), (0, T1 * P - w.shape[1]))).reshape(P, KT, T1, P).transpose(2, 0, 1, 3)

    d = np.concatenate([i["L1_ffn_down_w"].reshape(ROUTED, HID), i["L1_ffn_sh_down_w"]])
    d = np.pad(d, ((0, T1 * P - len(d)), (0, 0))).reshape(T1, P, P, KT).transpose(0, 1, 3, 2)
    owner = np.minimum(np.arange(T1 * P) // MI, NE)
    select = np.zeros((P, T1 * P), np.float32)
    select[owner, np.arange(T1 * P)] = 1.0
    a["ffn1_weights"] = np.concatenate(
        [up(i["L1_ffn_gate_w"], i["L1_ffn_sh_gate_w"]).reshape(T1, P, HID),
         up(i["L1_ffn_up_w"], i["L1_ffn_sh_up_w"]).reshape(T1, P, HID),
         select.reshape(P, T1, P).transpose(1, 0, 2), d.reshape(T1, P, HID)], axis=2)
    a["router"] = planes(i["L1_ffn_w_router"])
    a["router_bias"] = i["L1_ffn_corr_bias"].reshape(1, NE)
    by_head = lambda w: planes(w).reshape(P, KT, HEADS, D).transpose(2, 0, 1, 3).reshape(HEADS, P, HID)
    a["attn0_q"] = by_head(i["L0_attn_w_q"])
    a["attn0_kv"] = planes(i["L0_attn_w_kv"]).reshape(P, KT, 2, GROUPS * D).transpose(0, 2, 1, 3)
    outs = lambda w: w.reshape(HEADS, D, P, KT).transpose(0, 1, 3, 2).reshape(HEADS, D, HID)
    a["attn0_o"] = outs(i["L0_attn_w_dense"])
    a["attn1_qk"] = np.concatenate([by_head(i["L1_attn_wq"].T), by_head(i["L1_attn_wk"].T)], axis=2)
    a["attn1_v"] = by_head(i["L1_attn_wv"].T)
    a["attn1_o"] = outs(i["L1_attn_wo"].T)
    a["attn1_vec"] = np.stack([i[f"L1_attn_{n}"].reshape(HEADS, D) for n in ("bq", "bk", "bv", "gq", "gk")]
                              ).transpose(2, 0, 1)
    a["attn1_bo"] = i["L1_attn_bo"].reshape(P, KT)
    a["w_mix"] = i["L1_attn_w_mix"].reshape(1, -1)
    eye = np.eye(P, dtype=np.float32)
    a["shift_mats"] = np.stack([np.roll(eye, s, axis=1) for s in (0,) + CHANNEL_SHIFTS], axis=1)
    q, key = np.arange(SEQ)[:, None], np.arange(SEQ)[None, :]
    near = np.isin((q - key) % SEQ, np.array(SEQ_SHIFTS) % SEQ)
    lay_mask = lambda seen: np.where(seen, 0.0, -BIG).astype(np.float32).reshape(2, P, SEQ).transpose(1, 0, 2)
    a["causal_mask"], a["near_mask"] = lay_mask(q >= key), lay_mask(near)
    a["ident"] = np.eye(P, dtype=np.float32)
    return {n: np.ascontiguousarray(v) for n, v in a.items()}


def kernel(**inputs):
    import concourse.bacc as bacc
    from concourse.bass_utils import run_bass_kernel_spmd

    nc = bacc.Bacc("TRN2", target_bir_lowering=False, num_devices=1)
    arrays = lay_out({n: np.asarray(v) for n, v in inputs.items()})
    aps = {n: nc.dram_tensor(f"in_{n}", v.shape, mybir.dt.from_np(v.dtype), kind="ExternalInput").ap()
           for n, v in arrays.items()}
    out = nc.dram_tensor("out_0_dram", (P, KT, TOK), F32, kind="ExternalOutput").ap()
    macaron(nc, aps, out)
    r = run_bass_kernel_spmd(nc, [{f"in_{n}": v for n, v in arrays.items()}], core_ids=[0])
    y = r.results[0]["out_0_dram"]
    return np.ascontiguousarray(y.transpose(2, 0, 1)).reshape(BATCH, SEQ, HID)
```

```python
from contextlib import ExitStack

import numpy as np

import concourse.bass as bass
from concourse import mybir

F32 = mybir.dt.float32
F32R = mybir.dt.float32r
I32 = mybir.dt.int32
BF16 = mybir.dt.bfloat16
ALU = mybir.AluOpType
ACT = mybir.ActivationFunctionType
AX_X = mybir.AxisListType.X



P = 128
HID = 256
KT = HID // P
BATCH, SEQ = 8, 256
TOK = BATCH * SEQ
CH = 512
NCH = TOK // CH
MLP = 2048
T0 = MLP // P
NE, MI, SHARED = 32, 176, 352
ROUTED = NE * MI
NG, TOPG, TOPK = 8, 4, 6
WCOL = 3 * HID
EX = NE + SHARED // MI
ER = MI // 2
PAIRS_AT, FIRST_AT = (SHARED // MI + NE) * NCH, (SHARED // MI + NE) * NCH + NCH
LAST_AT = FIRST_AT + NCH + 1
PLAN = LAST_AT + NCH
NO_PLACE = 99.0
BIG = 1.0e30
HEADS, D = 16, 128
GROUPS = 4
CHANNEL_SHIFTS = (1, 2, 4, 8)
SEQ_SHIFTS = (0, 1, -1, 2, -2, 4, -4, 8, -8, 16, -16, 32, -32, 64, -64, 128)


class Core:

    def __init__(self, nc, ctx):
        self.nc, self.ctx, self.named, self.passes, self.route_steps, self.primed = nc, ctx, {}, {}, 0, set()

    def sem(self, name):
        if name not in self.named:
            self.named[name] = self.nc.alloc_semaphore(name=name)
        return self.named[name]

    def retire(self, kind):
        gone = [name for name in self.named if kind in name]
        self.nc.clear_and_free_semaphores([self.named.pop(name) for name in gone])
        self.nc.all_engine_barrier()

    def again(self, stage):
        self.passes[stage] = self.passes.get(stage, -1) + 1
        return self.passes[stage]

    def sems(self, name, n=2):
        return [self.sem(f"{name}{i}") for i in range(n)]

    def prime(self, sp, *groups):
        for group in groups:
            for sem in group if isinstance(group, list) else [group]:
                if sem.name not in self.primed:
                    self.primed.add(sem.name)
                    sp.sem_inc(sem, 1)


def load_constants(nc, k, x_t, gather_mats):
    x_in, ones_set = k.sem("x_in"), k.sem("ones_set")
    block = k.nc.Block()
    with block:
        @block.sync
        def _(sp):
            sp.dma_start(k.x[:], x_t).then_inc(x_in, 16)
            sp.dma_start(k.ident[:], gather_mats["ident"]).then_inc(x_in, 16)
            sp.wait_ge(x_in, 32)

        @block.vector
        def _(dve):
            nc.vector.memset(k.mean_mat[:], 1.0 / HID).then_inc(ones_set, 1)
            nc.vector.memset(k.eps[:], 1e-5).then_inc(ones_set, 1)
            nc.vector.memset(k.turns_run[:], 1.0).then_inc(ones_set, 1)
            dve.wait_ge(ones_set, 3)


def dequantise(nc, k, packed, scales, w_out):
    units = T0 // 2
    with ExitStack() as ctx:
        sb = lambda name, shape, dt: ctx.enter_context(nc.sbuf_tensor(name, shape, dt))
        codes = sb("dq_codes", [P, 2, WCOL], I32)
        scale = sb("dq_scale", [P, 2, WCOL], F32)
        mag = sb("dq_mag", [P, 2, WCOL], I32)
        bit = sb("dq_bit", [P, 2, WCOL], I32)
        steep = sb("dq_steep", [P, 2, WCOL], F32)
        sign = sb("dq_sign", [P, 2, WCOL], F32)
        value = sb("dq_value", [P, 2, WCOL], F32)
        done = sb("dq_done", [P, 2, 2, WCOL], F32)
        codes_in, scale_in, bits_done = k.sems("codes_in_dq"), k.sems("scale_in_dq"), k.sem("bits_done_dq")
        steep_done, sign_done = k.sem("steep_done_dq"), k.sem("sign_done_dq")
        step, unit_done, stored = k.sem("dq_step"), k.sem("unit_done_dq"), k.sems("dq_stored")
        block = nc.Block()
        with block:
            @block.sync
            def _(sp):
                for u in range(units):
                    b = u % 2
                    if u >= 2:
                        sp.wait_ge(unit_done, u - 1)
                    sp.dma_start(codes[:, b], packed[u]).then_inc(codes_in[b], 16)
                    for g in range(8):
                        sp.dma_start(scale[16 * g:16 * g + 16, b], scales[u, g:g + 1].to_broadcast([16, WCOL])
                                     ).then_inc(scale_in[b], 16)

            @block.scalar
            def _(act):
                for u in range(units):
                    b = u % 2
                    act.wait_ge(bits_done, u + 1)
                    if u:
                        act.wait_ge(unit_done, u)
                    nc.scalar.activation(steep[:], mag[:], ACT.Copy, bias=-8.0, scale=2.0).then_inc(steep_done, 1)
                    nc.scalar.activation(sign[:], bit[:], ACT.Copy, bias=1.0, scale=-0.25).then_inc(sign_done, 1)
                    act.wait_ge(unit_done, u + 1)
                    act.dma_start(w_out[2 * u:2 * u + 2].rearrange("t p c -> p t c"), done[:, b]
                                  ).then_inc(stored[b], 16)
                for b in range(2):
                    act.wait_ge(stored[b], 16 * (units // 2))

            @block.vector
            def _(dve):
                steps = 0
                for u in range(units):
                    b = u % 2
                    dve.wait_ge(codes_in[b], 16 * (u // 2 + 1))
                    if u:
                        dve.wait_ge(sign_done, u)
                    for nib in range(2):
                        if nib:
                            nc.vector.tensor_scalar(mag[:, 1], codes[:, b], 4, 7, ALU.logical_shift_right,
                                                    ALU.bitwise_and)
                            nc.vector.tensor_scalar(bit[:, 1], codes[:, b], 4, 8, ALU.logical_shift_right,
                                                    ALU.bitwise_and).then_inc(bits_done, 1)
                        else:
                            nc.vector.tensor_scalar(mag[:, 0], codes[:, b], 7, None, ALU.bitwise_and)
                            nc.vector.tensor_scalar(bit[:, 0], codes[:, b], 8, None, ALU.bitwise_and)
                    dve.wait_ge(bits_done, u + 1)
                    dve.wait_ge(steep_done, u + 1)
                    nc.vector.scalar_tensor_tensor(out=value[:], in0=mag[:], scalar=-2.0, in1=steep[:],
                                                   op0=ALU.add, op1=ALU.max).then_inc(step, 1)
                    dve.wait_ge(step, steps + 1)
                    nc.vector.scalar_tensor_tensor(out=value[:], in0=mag[:], scalar=0.5, in1=value[:],
                                                   op0=ALU.mult, op1=ALU.max).then_inc(step, 1)
                    dve.wait_ge(step, steps + 2)
                    dve.wait_ge(sign_done, u + 1)
                    nc.vector.tensor_tensor(value[:], value[:], sign[:], ALU.mult).then_inc(step, 1)
                    dve.wait_ge(step, steps + 3)
                    dve.wait_ge(scale_in[b], 128 * (u // 2 + 1))
                    if u >= 2:
                        dve.wait_ge(stored[b], 16 * (u // 2))
                    for nib in range(2):
                        nc.vector.tensor_tensor(
                            done[:, b, :, 0:2 * HID].rearrange("p t (w k c) -> p w t k c", w=2, k=2)[:, :, :, nib],
                            value[:, nib, 0:2 * HID].rearrange("p (w t c) -> p w t c", w=2, t=2),
                            scale[:, b, 0:2 * HID].rearrange("p (w t c) -> p w t c", w=2, t=2), ALU.mult)
                        last = nc.vector.tensor_tensor(done[:, b, nib, 2 * HID:], value[:, nib, 2 * HID:],
                                                       scale[:, b, 2 * HID:], ALU.mult)
                    last.then_inc(unit_done, 1)
                    steps += 3


def layernorm(nc, k, tag, split):
    with ExitStack() as ctx:
        sb = lambda name, shape, dt: ctx.enter_context(nc.sbuf_tensor(f"{name}_{tag}", shape, dt))
        centred = sb("centred", [P, 2, KT, CH], F32)
        square = sb("square", [P, 2, KT, CH], F32)
        root = sb("root", [P, 2, CH], F32)
        rstd = sb("rstd", [P, 2, CH], F32)
        scaled = sb("scaled", [P, 2, KT, CH], F32) if split else None
        mean_done, var_done = k.sem("mean_done"), k.sem("var_done")
        centred_done, square_done = k.sem("centred_done"), k.sem("square_done")
        root_done, rstd_done, scaled_done = k.sem("root_done"), k.sem("rstd_done"), k.sem("scaled_done")
        if split:
            high_done, low_done = k.sem("xn_high_done"), k.sem("xn_low_done")
        C0, S0 = NCH * k.again("layernorm"), NCH * k.again("split") if split else 0
        mean = [k.bank[0], k.bank[1]]
        var = [k.bank[2], k.bank[3]]
        chunk = lambda c: slice(c * CH, (c + 1) * CH)

        def out_of(c):
            return scaled[:, c % 2] if split else k.xn[:, :, chunk(c)]

        block = nc.Block()
        with block:
            @block.tensor
            def _(pe):
                def sum_mean(c):
                    if c >= 2:
                        pe.wait_ge(centred_done, C0 + c - 1)
                    for kt in range(KT):
                        last = nc.tensor.matmul(mean[c % 2][:], k.mean_mat[:], k.x[:, kt, chunk(c)],
                                                start=kt == 0, stop=kt == KT - 1)
                    last.then_inc(mean_done, 1)

                def sum_var(c):
                    pe.wait_ge(square_done, C0 + c + 1)
                    if c >= 2:
                        pe.wait_ge(root_done, C0 + c - 1)
                    for kt in range(KT):
                        last = nc.tensor.matmul(var[c % 2][:], k.mean_mat[:], square[:, c % 2, kt],
                                                start=kt == 0, stop=kt == KT - 1)
                    last.then_inc(var_done, 1)

                sum_mean(0)
                for c in range(NCH):
                    if c + 1 < NCH:
                        sum_mean(c + 1)
                    sum_var(c)

            @block.scalar
            def _(act):
                def take_square(c):
                    act.wait_ge(centred_done, C0 + c + 1)
                    if c >= 2:
                        act.wait_ge(var_done, C0 + c - 1)
                    nc.scalar.activation(square[:, c % 2], centred[:, c % 2], ACT.Square).then_inc(square_done, 1)

                take_square(0)
                for c in range(NCH):
                    if c + 1 < NCH:
                        take_square(c + 1)
                    act.wait_ge(var_done, C0 + c + 1)
                    if c >= 2:
                        act.wait_ge(rstd_done, C0 + c - 1)
                    nc.scalar.activation(root[:, c % 2], var[c % 2][:], ACT.Sqrt, bias=k.eps[:, 0:1]
                                         ).then_inc(root_done, 1)
                    if split:
                        act.wait_ge(scaled_done, C0 + c + 1)
                        nc.scalar.activation(k.xn_high[:, :, chunk(c)], scaled[:, c % 2], ACT.Copy
                                             ).then_inc(high_done, 1)

            @block.vector
            def _(dve):
                def centre(c):
                    dve.wait_ge(mean_done, C0 + c + 1)
                    if c >= 2:
                        dve.wait_ge(square_done, C0 + c - 1)
                        dve.wait_ge(scaled_done, C0 + c - 1)
                    nc.vector.tensor_tensor(centred[:, c % 2], k.x[:, :, chunk(c)],
                                            mean[c % 2][:].unsqueeze(1).to_broadcast([P, KT, CH]), ALU.subtract
                                            ).then_inc(centred_done, 1)

                def low(c):
                    dve.wait_ge(high_done, S0 + c + 1)
                    nc.vector.tensor_tensor(k.xn_low[:, :, chunk(c)], scaled[:, c % 2],
                                            k.xn_high[:, :, chunk(c)].bitcast(F32), ALU.subtract).then_inc(low_done, 1)

                centre(0)
                for c in range(NCH):
                    if c + 1 < NCH:
                        centre(c + 1)
                    dve.wait_ge(root_done, C0 + c + 1)
                    if c >= 2:
                        dve.wait_ge(scaled_done, C0 + c - 1)
                    nc.vector.reciprocal(rstd[:, c % 2], root[:, c % 2]).then_inc(rstd_done, 1)
                    if split and c:
                        low(c - 1)
                    dve.wait_ge(rstd_done, C0 + c + 1)
                    if split and c >= 2:
                        dve.wait_ge(low_done, S0 + c - 1)
                    nc.vector.tensor_tensor(out_of(c), centred[:, c % 2],
                                            rstd[:, c % 2].unsqueeze(1).to_broadcast([P, KT, CH]), ALU.mult
                                            ).then_inc(scaled_done, 1)
                if split:
                    low(NCH - 1)


def feed_forward(nc, k, tag, rows, w_gu, w_dn, func, combine=None):
    moe = combine is not None
    kind = "moe" if moe else "fp4"
    run = k.again(kind)
    C0 = NCH * run + 1
    gu_cols = 4 * rows

    def begin(eng, c):
        if not moe:
            first = 1 + (NCH * run + c) * (T0 // 2)
            return first, first + (T0 // 2 - 1), T0 // 2
        first = eng.value_load(k.plan[0:1, bass.ds(c + FIRST_AT, 1)], min_val=1, max_val=2 * NCH * EX)
        pairs = eng.value_load(k.plan[0:1, bass.ds(c + PAIRS_AT, 1)], min_val=SHARED // MI + TOPK, max_val=EX)
        last = eng.value_load(k.plan[0:1, bass.ds(c + LAST_AT, 1)], min_val=1, max_val=2 * NCH * EX)
        return first, last, pairs

    with ExitStack() as ctx:
        sb = lambda name, shape, dt: [ctx.enter_context(nc.sbuf_tensor(f"{name}{i}_{tag}", shape, dt)) for i in range(2)]
        gu_raw, gu_high, gu_low = sb("gu_raw", [P, gu_cols], F32), sb("gu_high", [P, gu_cols], F32R), sb("gu_low", [P, gu_cols], F32R)
        dn_raw, dn_high, dn_low = sb("dn_raw", [rows, HID], F32), sb("dn_high", [rows, HID], F32R), sb("dn_low", [rows, HID], F32R)
        acted, prod = sb("acted", [rows, CH], F32), sb("prod", [rows, CH], F32)
        spread = sb("spread", [rows, CH], F32) if moe else None
        weighed = sb("weighed", [rows, CH], F32) if moe else prod
        h_high, h_low = sb("h_high", [rows, CH], F32R), sb("h_low", [rows, CH], F32R)
        y = [k.bank[0], k.bank[1]]
        gate, up = [k.bank[2 + i][0:rows, :] for i in range(2)], [k.bank[4 + i][0:rows, :] for i in range(2)]
        sems = lambda name: k.sems(f"{name}_{kind}")
        gu_in, dn_in = sems("gu_in"), sems("dn_in")
        gu_high_done, gu_split, dn_high_done, dn_split = sems("gu_high_done"), sems("gu_split"), sems("dn_high_done"), sems("dn_split")
        gu_done, acted_done, prod_done = sems("gu_done"), sems("acted_done"), sems("prod_done")
        weighed_done = sems("weighed_done") if moe else prod_done
        spread_in = sems("spread_in") if moe else None
        h_high_done, h_split, down_done = sems("h_high_done"), sems("h_split"), sems("down_done")
        y_added = k.sem(f"y_added_{kind}")

        block = nc.Block()
        with block:
            @block.sync
            def _(sp):
                k.prime(sp, gu_high_done, gu_split, dn_high_done, dn_split, gu_done, acted_done, prod_done, weighed_done,
                        h_high_done, h_split, down_done, y_added)

                with sp.Fori(0, NCH) as c:
                    first, last, pairs = begin(sp, c)
                    with sp.Fori(0, pairs) as h:
                        n = first + h
                        if moe:
                            e = sp.value_load(k.plan[0:1, bass.ds(c * EX + h, 1)], min_val=0, max_val=EX - 1)
                        for b in range(2):
                            tile = 2 * (e if moe else h) + b
                            sp.wait_ge(gu_split[b], n)
                            sp.dma_start(gu_raw[b][:], w_gu[tile]).then_inc(gu_in[b], 16)
                            if moe:
                                sp.wait_ge(weighed_done[b], n)
                                sp.dma_start(spread[b][:], combine[bass.ds(e, 1), bass.ts(c, CH)].to_broadcast([rows, CH])
                                             ).then_inc(spread_in[b], 16)
                            sp.wait_ge(dn_split[b], n)
                            sp.dma_start(dn_raw[b][:], w_dn[tile]).then_inc(dn_in[b], 16)

            @block.gpsimd
            def _(pool):
                def gu_low_part(n, b):
                    pool.wait_ge(gu_high_done[b], n + 1)
                    nc.gpsimd.tensor_tensor(gu_low[b][:], gu_raw[b][:], gu_high[b][:].bitcast(F32),
                                            ALU.subtract).then_inc(gu_split[b], 1)

                def dn_low_part(n, b):
                    pool.wait_ge(dn_high_done[b], n + 1)
                    nc.gpsimd.tensor_tensor(dn_low[b][:], dn_raw[b][:], dn_high[b][:].bitcast(F32),
                                            ALU.subtract).then_inc(dn_split[b], 1)

                with pool.Fori(0, NCH) as c:
                    first, last, pairs = begin(pool, c)
                    for b in range(2):
                        gu_low_part(first, b)
                    with pool.Fori(0, pairs - 1) as h:
                        for b in range(2):
                            dn_low_part(first + h, b)
                            gu_low_part(first + h + 1, b)
                    for b in range(2):
                        dn_low_part(last, b)

            @block.tensor
            def _(pe):
                def gate_up(n, b, c):
                    pe.wait_ge(gu_split[b], n + 1)
                    pe.wait_ge(weighed_done[b], n)
                    cols = bass.ts(c, CH)
                    for out, at in ((gate[b], 0), (up[b], 2 * rows)):
                        for kt in range(KT):
                            w = slice(at + kt * rows, at + kt * rows + rows)
                            nc.tensor.matmul(out, gu_high[b][:, w], k.xn_high[:, kt, cols], start=kt == 0, stop=False)
                            nc.tensor.matmul(out, gu_high[b][:, w], k.xn_low[:, kt, cols], start=False, stop=False)
                            last = nc.tensor.matmul(out, gu_low[b][:, w], k.xn_high[:, kt, cols], start=False,
                                                    stop=kt == KT - 1)
                    last.then_inc(gu_done[b], 1)

                def down(n, b, start=False, final=False):
                    pe.wait_ge(dn_split[b], n + 1)
                    pe.wait_ge(h_split[b], n + 1)
                    for kt in range(KT):
                        w = slice(kt * P, kt * P + P)
                        nc.tensor.matmul(y[kt][:], dn_high[b][:, w], h_high[b][:], start=start, stop=False)
                        nc.tensor.matmul(y[kt][:], dn_high[b][:, w], h_low[b][:], start=False, stop=False)
                        last = nc.tensor.matmul(y[kt][:], dn_low[b][:, w], h_high[b][:], start=False, stop=final)
                    last.then_inc(down_done[b], 1)

                with pe.Fori(0, NCH) as c:
                    first, last, pairs = begin(pe, c)
                    for b in range(2):
                        gate_up(first, b, c)
                    pe.wait_ge(y_added, c + C0)
                    for b in range(2):
                        gate_up(first + 1, b, c)
                        down(first, b, start=b == 0)
                    with pe.Fori(1, pairs - 1) as h:
                        for b in range(2):
                            gate_up(first + h + 1, b, c)
                            down(first + h, b)
                    for b in range(2):
                        down(last, b, final=b == 1)

            @block.scalar
            def _(act):
                def gu_high_part(n, b):
                    act.wait_ge(gu_in[b], 16 * n)
                    act.wait_ge(gu_done[b], n)
                    nc.scalar.activation(gu_high[b][:], gu_raw[b][:], ACT.Copy).then_inc(gu_high_done[b], 1)

                def dn_high_part(n, b):
                    act.wait_ge(dn_in[b], 16 * n)
                    act.wait_ge(down_done[b], n)
                    nc.scalar.activation(dn_high[b][:], dn_raw[b][:], ACT.Copy).then_inc(dn_high_done[b], 1)

                def values(n, b):
                    act.wait_ge(gu_done[b], n + 1)
                    act.wait_ge(prod_done[b], n)
                    nc.scalar.activation(acted[b][:], gate[b], func).then_inc(acted_done[b], 1)
                    dn_high_part(n, b)
                    act.wait_ge(weighed_done[b], n + 1)
                    nc.scalar.activation(h_high[b][:], weighed[b][:], ACT.Copy).then_inc(h_high_done[b], 1)

                with act.Fori(0, NCH) as c:
                    first, last, pairs = begin(act, c)
                    for b in range(2):
                        gu_high_part(first, b)
                    with act.Fori(0, pairs - 1) as h:
                        for b in range(2):
                            values(first + h, b)
                            gu_high_part(first + h + 1, b)
                    for b in range(2):
                        values(last, b)

            @block.vector
            def _(dve):
                def product(n, b):
                    dve.wait_ge(acted_done[b], n + 1)
                    dve.wait_ge(h_split[b], n)
                    nc.vector.tensor_tensor(prod[b][:], acted[b][:], up[b], ALU.mult).then_inc(prod_done[b], 1)
                    if moe:
                        dve.wait_ge(spread_in[b], 16 * n)
                        dve.wait_ge(prod_done[b], n + 1)
                        nc.vector.tensor_tensor(weighed[b][:], prod[b][:], spread[b][:], ALU.mult
                                                ).then_inc(weighed_done[b], 1)
                    dve.wait_ge(h_high_done[b], n + 1)
                    nc.vector.tensor_tensor(h_low[b][:], weighed[b][:], h_high[b][:].bitcast(F32), ALU.subtract
                                            ).then_inc(h_split[b], 1)

                with dve.Fori(0, NCH) as c:
                    first, last, pairs = begin(dve, c)
                    with dve.Fori(0, pairs) as h:
                        product(first + h, 0)
                        product(first + h, 1)
                    dve.wait_ge(down_done[1], last + 1)
                    for kt in range(KT):
                        add = nc.vector.scalar_tensor_tensor(
                            out=k.x[:, kt, bass.ts(c, CH)], in0=y[kt][:], scalar=0.5, in1=k.x[:, kt, bass.ts(c, CH)],
                            op0=ALU.mult, op1=ALU.add)
                    add.then_inc(y_added, 1)


def route(nc, k, tag, w_router, bias, plan_consts, comb_dram):
    NT = TOK // P
    with ExitStack() as ctx:
        sb = lambda name, shape, dt=F32: ctx.enter_context(nc.sbuf_tensor(f"{name}_{tag}", shape, dt))
        w_raw, w_high, w_low = sb("rw_raw", [P, KT, NE]), sb("rw_high", [P, KT, NE], F32R), sb("rw_low", [P, KT, NE], F32R)
        bias_row = sb("bias_row", [P, NE])
        half_tanh = sb("half_tanh", [NE, TOK])
        comb = sb("comb", [EX, TOK])
        consts = sb("plan_consts", [EX, 3 * EX + 3])
        before, ones, place_no = consts[:, 0:EX], consts[:, EX:2 * EX], consts[:, 2 * EX:3 * EX]
        number, is_last, no_place = (consts[:, 3 * EX + i:3 * EX + i + 1] for i in range(3))
        active, place, last_place = sb("active", [EX, NCH]), sb("place", [EX, NCH]), sb("last_place", [EX, NCH])
        at_place = sb("at_place", [EX, NCH, EX])
        plan = sb("plan_row", [1, PLAN])
        score, sfc, masked, weight = sb("score", [P, NT, NE]), sb("sfc", [P, NT, NE]), sb("masked", [P, NT, NE]), sb("weight", [P, NT, NE])
        best2 = sb("best2", [P, NT, NG])
        pair_a, pair_b = sb("pair_a", [P, NT, NG, 2]), sb("pair_b", [P, NT, NG, 2])
        keep = sb("keep", [P, NT, NG])
        chosen = sb("chosen", [P, NT, NE])
        top8 = sb("top8", [P, NT, 8])
        above, equal = sb("above", [P, NT, NE]), sb("equal", [P, NT, NE])
        count = sb("count", [P, NT])
        PAD = 16
        run = [sb(f"run{i}", [P, NT, PAD + NE]) for i in range(2)]
        w_in, bias_in = k.sem("rw_in"), k.sem("rbias_in")
        step, tanh_done, logits_done = k.sem("rstep"), k.sem("tanh_done"), k.sem("logits_done")
        w_ready, turned, weight_done = k.sem("rw_ready"), k.sem("rturned"), k.sem("rweight")
        back, comb_done, comb_out = k.sem("rback"), k.sem("rcomb"), k.sem("rcomb_out")
        placed, one_hot, listed, plan_done = k.sem("placed"), k.sem("one_hot"), k.sem("listed"), k.sem("plan_done")
        R = k.again("route")
        chunk = lambda c: slice(c * CH, (c + 1) * CH)
        logit_bank = [k.bank[c] for c in range(NCH)]
        turn_bank = k.bank[4]
        block = nc.Block()
        with block:
            @block.sync
            def _(sp):
                sp.dma_start(w_raw[:], w_router).then_inc(w_in, 16)
                sp.dma_start(bias_row[:], bias.to_broadcast([P, NE])).then_inc(bias_in, 16)
                sp.dma_start(consts[:], plan_consts).then_inc(bias_in, 16)
                for c in range(NCH):
                    sp.wait_ge(comb_done, NCH * R + c + 1)
                    sp.dma_start(comb_dram[:, chunk(c)], comb[:, chunk(c)]).then_inc(comb_out, 16)
                sp.wait_ge(comb_out, 16 * NCH * (R + 1))

            @block.tensor
            def _(pe):
                pe.wait_ge(w_ready, 2 * R + 2)
                for c in range(NCH):
                    for kt in range(KT):
                        out = logit_bank[c][0:NE, :]
                        nc.tensor.matmul(out, w_high[:, kt], k.xn_high[:, kt, chunk(c)], start=kt == 0, stop=False)
                        nc.tensor.matmul(out, w_high[:, kt], k.xn_low[:, kt, chunk(c)], start=False, stop=False)
                        last = nc.tensor.matmul(out, w_low[:, kt], k.xn_high[:, kt, chunk(c)], start=False, stop=kt == KT - 1)
                    last.then_inc(logits_done, 1)
                for c in range(NCH):
                    pe.wait_ge(tanh_done, NCH * R + c + 1)
                    for t in range(4 * c, 4 * c + 4):
                        last = nc.tensor.transpose(turn_bank[:, t * NE:(t + 1) * NE], half_tanh[:, t * P:(t + 1) * P],
                                                   k.ident[0:NE, 0:NE])
                last.then_inc(turned, 1)
                pe.wait_ge(weight_done, R + 1)
                for c in range(NCH):
                    for t in range(4 * c, 4 * c + 4):
                        last = nc.tensor.transpose(logit_bank[c][0:NE, t % 4 * P:t % 4 * P + P], weight[:, t], k.ident[:])
                    last.then_inc(back, 1)

                pe.wait_ge(placed, R + 1)
                nc.tensor.matmul(turn_bank[0:EX, 0:NCH], before, active[:], start=True, stop=True)
                nc.tensor.matmul(turn_bank[0:EX, NCH:2 * NCH], ones, active[:], start=True, stop=True
                                 ).then_inc(listed, 1)
                pe.wait_ge(one_hot, R + 1)
                nc.tensor.matmul(turn_bank[0:1, 0:NCH * EX], number, at_place[:].rearrange("e c j -> e (c j)"),
                                 start=True, stop=True).then_inc(listed, 1)

            @block.scalar
            def _(act):
                for c in range(NCH):
                    act.wait_ge(logits_done, NCH * R + c + 1)
                    nc.scalar.activation(half_tanh[:, chunk(c)], logit_bank[c][0:NE, :], ACT.Tanh, scale=0.5
                                         ).then_inc(tanh_done, 1)
                for c in range(NCH):
                    act.wait_ge(back, NCH * R + c + 1)
                    nc.scalar.activation(comb[0:NE, chunk(c)], logit_bank[c][0:NE, :], ACT.Copy).then_inc(comb_done, 1)

            @block.vector
            def _(dve):
                steps = [k.route_steps]

                def link(ins):
                    steps[0] += 1
                    ins.then_inc(step, 1)
                    dve.wait_ge(step, steps[0])

                def tt(out, a, b, op):
                    return nc.vector.tensor_tensor(out, a, b, op)

                def choose(mask, values, n, many):
                    for t in range(NT):
                        last = nc.vector.max(top8[:, t], values[:, t])
                    link(last)
                    least = top8[:, :, many - 1:many].to_broadcast([P, NT, n])
                    a, e = above[:, :, 0:n], equal[:, :, 0:n]
                    tt(a, values, least, ALU.is_gt)
                    tt(e, values, least, ALU.is_equal)
                    link(tt(run[0][:, :, PAD:PAD + n], values, least, ALU.is_equal))
                    link(nc.vector.tensor_reduce(count[:], a, AX_X, ALU.add))
                    at, by = 0, 1
                    while by < n:
                        link(tt(run[1 - at][:, :, PAD:PAD + n], run[at][:, :, PAD:PAD + n],
                                run[at][:, :, PAD - by:PAD - by + n], ALU.add))
                        at, by = 1 - at, 2 * by
                    ran = run[at][:, :, PAD:PAD + n]
                    link(tt(ran, ran, count[:].unsqueeze(2).to_broadcast([P, NT, n]), ALU.add))
                    link(nc.vector.scalar_tensor_tensor(out=e, in0=ran, scalar=float(many), in1=e,
                                                        op0=ALU.is_le, op1=ALU.mult))
                    link(tt(mask, a, e, ALU.add))

                nc.vector.memset(comb[NE:EX, :], 1.0)
                nc.vector.memset(active[:], 0.0)
                nc.vector.memset(run[0][:], 0.0)
                link(nc.vector.memset(run[1][:], 0.0))
                dve.wait_ge(w_in, 16 * R + 16)
                nc.vector.tensor_copy(w_high[:], w_raw[:]).then_inc(w_ready, 1)
                dve.wait_ge(w_ready, 2 * R + 1)
                nc.vector.tensor_tensor(w_low[:], w_raw[:], w_high[:].bitcast(F32), ALU.subtract).then_inc(w_ready, 1)
                dve.wait_ge(turned, R + 1)
                link(nc.vector.tensor_scalar(score[:].rearrange("p t e -> p (t e)"), turn_bank[:], 0.5, 0.5,
                                             ALU.mult, ALU.add))
                dve.wait_ge(bias_in, 32 * R + 32)
                link(tt(sfc[:], score[:], bias_row[:].unsqueeze(1).to_broadcast([P, NT, NE]), ALU.add))
                quad = sfc[:].rearrange("p t (g x y) -> p (t g) x y", x=2, y=2)
                a, b = quad[:, :, :, 0], quad[:, :, :, 1]
                sums, maxs = [z[:].rearrange("p t g x -> p (t g) x") for z in (pair_a, pair_b)]
                best = best2[:].rearrange("p t g -> p (t g)")
                tt(sums, a, b, ALU.add)
                link(tt(maxs, a, b, ALU.max))
                link(tt(best, maxs[:, :, 0], maxs[:, :, 1], ALU.add))
                link(tt(best, best, sums[:, :, 0], ALU.max))
                link(tt(best, best, sums[:, :, 1], ALU.max))
                choose(keep[:], best2[:], NG, TOPG)
                kept = keep[:].rearrange("p t g -> p (t g)").unsqueeze(2).to_broadcast([P, NT * NG, NE // NG])
                m4 = masked[:].rearrange("p t (g x) -> p (t g) x", x=NE // NG)
                s4 = sfc[:].rearrange("p t (g x) -> p (t g) x", x=NE // NG)
                link(tt(m4, s4, kept, ALU.mult))
                link(nc.vector.tensor_scalar(keep[:], keep[:], BIG, -BIG, ALU.mult, ALU.add))
                link(tt(m4, m4, kept, ALU.add))
                choose(chosen[:], masked[:], NE, TOPK)
                tt(weight[:], chosen[:], score[:], ALU.mult).then_inc(weight_done, 1)
                for c in range(NCH):
                    dve.wait_ge(comb_done, NCH * R + c + 1)
                    last = nc.vector.tensor_reduce(active[0:NE, c:c + 1], comb[0:NE, chunk(c)], AX_X, ALU.max)
                link(last)
                nc.vector.tensor_scalar(active[0:NE, :], active[0:NE, :], 0.0, None, ALU.is_gt).then_inc(placed, 1)
                dve.wait_ge(listed, 2 * R + 1)
                numbers = turn_bank[0:EX, NCH:2 * NCH]
                link(nc.vector.scalar_tensor_tensor(out=place[:], in0=turn_bank[0:EX, 0:NCH], scalar=1.0 - NO_PLACE,
                                                    in1=active[:], op0=ALU.add, op1=ALU.mult))
                link(nc.vector.tensor_scalar(last_place[:], numbers, 1.0, is_last, ALU.add, ALU.mult))
                link(tt(place[:], place[:], last_place[:], ALU.add))
                link(nc.vector.tensor_scalar(place[:], place[:], no_place, None, ALU.add))
                link(nc.vector.tensor_scalar(plan[:, PAIRS_AT:PAIRS_AT + NCH], numbers[0:1, :], 2.0, None, ALU.add))
                link(nc.vector.tensor_copy(plan[:, FIRST_AT:FIRST_AT + 1], k.turns_run[:]))
                for c in range(NCH):
                    link(tt(plan[:, FIRST_AT + c + 1:FIRST_AT + c + 2], plan[:, FIRST_AT + c:FIRST_AT + c + 1],
                            plan[:, PAIRS_AT + c:PAIRS_AT + c + 1], ALU.add))
                nc.vector.tensor_scalar(plan[:, LAST_AT:LAST_AT + NCH], plan[:, FIRST_AT + 1:FIRST_AT + NCH + 1], -1.0, None,
                                        ALU.add)
                nc.vector.tensor_copy(k.turns_run[:], plan[:, FIRST_AT + NCH:FIRST_AT + NCH + 1])
                tt(at_place[:], place_no.unsqueeze(1).to_broadcast([EX, NCH, EX]),
                   place[:].unsqueeze(2).to_broadcast([EX, NCH, EX]), ALU.is_equal).then_inc(one_hot, 1)
                dve.wait_ge(listed, 2 * R + 2)
                link(nc.vector.tensor_copy(plan[:, 0:NCH * EX], turn_bank[0:1, 0:NCH * EX]))
                nc.vector.tensor_copy(k.plan[:], plan[:]).then_inc(plan_done, 1)
                dve.wait_ge(plan_done, R + 1)
                k.route_steps = steps[0]


def attention(nc, k, tag, a, mix):
    MH = HEADS // 2
    run = k.again("attention")
    C0, X0 = NCH * run, (NCH + 1) * run
    turn = lambda c, m: 1 + (c + C0) * MH + m
    own = lambda c, m: 1 + c * MH + m
    with ExitStack() as ctx:
        one = lambda name, shape, dt=F32: ctx.enter_context(nc.sbuf_tensor(f"{name}_{tag}", shape, dt))
        two = lambda name, shape, dt=F32: [one(f"{name}{i}", shape, dt) for i in range(2)]
        SEEN = (SEQ, SEQ) if mix else (P, SEQ)
        AT, WIDE = (0, SEEN[0]), sum(SEEN)
        Q0, J_AT = ((0, 0), (0, SEQ)) if mix else ((0, P), (0, SEQ))
        xc_high, xc_low = one("xc_high", [P, KT, CH], F32R), one("xc_low", [P, KT, CH], F32R)
        mask = one("mask", [P, WIDE])
        probs = two("probs", [P, 2, WIDE])
        oT_high, oT_low = two("oT_high", [P, CH], F32R), two("oT_low", [P, CH], F32R)
        peak, shift, total, inverse = [two(name, [P, 2, 2]) for name in ("peak", "shift", "total", "inverse")]
        w_out, wo_high, wo_low = two("w_out", [P, HID]), two("wo_high", [P, HID], F32R), two("wo_low", [P, HID], F32R)
        if mix:
            q_all, k_all = one("q_all", [P, HEADS, CH]), one("k_all", [P, HEADS, CH])
            qT, kT = two("qT", [P, CH]), two("kT", [P, CH])
            vs = one("vs", [P, 2, 2, 2 * D])
            w_in, wi_high, wi_low = ([one(name, [P, 2 * HID], dt)] for name, dt in
                                     (("w_in", F32), ("wi_high", F32R), ("wi_low", F32R)))
            pT = two("pT", [P, 2, WIDE])
            w_qk, qk_high, qk_low = two("w_qk", [P, 2 * HID]), two("qk_high", [P, 2 * HID], F32R), two("qk_low", [P, 2 * HID], F32R)
            vec = one("vec", [P, 5, HEADS])
            shifts = one("shifts", [P, 1 + len(CHANNEL_SHIFTS), P])
            w_mix = one("w_mix", [P, 1 + len(CHANNEL_SHIFTS)])
            circ = one("circ", [P, P])
            circ_g = two("circ_g", [P, P])
            sq_q, sq_k = two("sq_q", [P, CH]), two("sq_k", [P, CH])
            acc = one("acc", [P, 2, CH])
            rms = acc
            inv_rms = one("inv_rms", [P, 2, CH])
            eps6, b_out = one("eps6", [P, 1]), one("b_out", [P, KT])
        else:
            w_in, wi_high, wi_low = two("w_in", [P, HID]), two("wi_high", [P, HID], F32R), two("wi_low", [P, HID], F32R)
            qT_high, qT_low = two("qT_high", [P, CH], F32R), two("qT_low", [P, CH], F32R)
            pT_high, pT_low = two("pT_high", [P, 2, WIDE], F32R), two("pT_low", [P, 2, WIDE], F32R)
            vs = two("vs", [P, 4, 2, D], F32R)
            w_kv = one("w_kv", [P, 2, KT, GROUPS * D])
            kv_high, kv_low = one("kv_high", [P, 2, KT, GROUPS * D], F32R), one("kv_low", [P, 2, KT, GROUPS * D], F32R)
            k_high, k_low = one("k_high", [P, GROUPS, CH], F32R), one("k_low", [P, GROUPS, CH], F32R)
            v_all = one("v_all", [P, 4, 2, GROUPS * D], F32R)
        y = [k.bank[0], k.bank[1]]
        proj, ctx_bank = k.bank[2], k.bank[7]
        s_ps, t_ps = k.pair[0], k.pair[1]
        n = lambda s: f"{s}_near_" if mix else f"{s}_gqa_"
        xc_ready, const_in, setup = k.sem("attn_xc_ready"), k.sem(n("const_in")), k.sem(n("setup"))
        xc_high_done = k.sem("attn_xc_high")
        head_in, wo_in = k.sems("head_in"), k.sems("wo_in")
        in_high_done, in_split = k.sems("attn_in_high"), k.sems("attn_in_split")
        wo_high_done, wo_split, o_high_done = k.sems("attn_wo_high"), k.sems("attn_wo_split"), k.sems("attn_o_high")
        q_proj, q_ready, k_ready = k.sems("attn_q_proj"), k.sems("attn_q_ready"), k.sems(n("k_ready"))
        v_proj, v_ready = k.sems(n("v_proj")), k.sems("attn_v_ready")
        scored, masked, peaked, shifted = k.sems("attn_scored"), k.sems("attn_masked"), k.sems("attn_peaked"), k.sems("attn_shifted")
        exped, inverted, normed = k.sems("attn_exped"), k.sems("attn_inverted"), k.sems("attn_normed")
        turned, pt_ready, ctx_done, o_ready, y_done = (k.sems("attn_turned"), k.sems("attn_pt_ready"), k.sems("attn_ctx_done"),
                                                       k.sems("attn_o_ready"), k.sems("attn_y_done"))
        y_added = k.sem("attn_y_added")
        if mix:
            qk_in, qk_proj, qk_biased = k.sems(n("qk_in")), k.sems(n("qk_proj")), k.sems(n("qk_biased"))
            summed, qk_high_done, qk_split = k.sems(n("summed")), k.sems(n("qk_high")), k.sems(n("qk_split"))
            acc_zero, sums_done, rms_done, inv_done = k.sem(n("acc_zero")), k.sem(n("sums_done")), k.sem(n("rms_done")), k.sem(n("inv_done"))
            circ_ready = k.sems(n("circ_ready"))
        else:
            kv_proj, kv_high_done, kv_ready = k.sem(n("kv_proj")), k.sem(n("kv_high")), k.sem(n("kv_ready"))
            q_high_done, pt_high_done = k.sems(n("q_high")), k.sems(n("pt_high"))

        def before(sems, b, t):
            return (sems[1], t) if b == 0 else (sems[0], t + 1)

        def product(out, w, w_low, z, z_low, start=True, stop=True):
            nc.tensor.matmul(out, w, z, start=start, stop=False)
            nc.tensor.matmul(out, w, z_low, start=False, stop=False)
            return nc.tensor.matmul(out, w_low, z, start=False, stop=stop)

        def steps(eng, c, step):
            step(0, 0, True, 0)
            step(0, 1, False, 0)
            with eng.Fori(1, MH - 1) as m:
                step(m, 0, False, 0)
                step(m, 1, False, 0)
            step(MH - 1, 0, False, 1)
            step(MH - 1, 1, False, 2)

        block = nc.Block()
        with block:
            @block.sync
            def _(sp):
                k.prime(sp, q_proj, q_ready, v_ready, scored, masked, peaked, shifted, exped, inverted, normed, turned,
                        pt_ready, ctx_done, o_ready, y_done, y_added, v_proj, k_ready, in_high_done, in_split,
                        wo_high_done, wo_split, o_high_done)
                if mix:
                    k.prime(sp, qk_proj, qk_biased, summed, circ_ready, qk_high_done, qk_split)
                else:
                    k.prime(sp, q_high_done, pt_high_done)
                sp.dma_start(mask[:], a["near_mask" if mix else "causal_mask"]).then_inc(const_in, 16)
                if mix:
                    sp.dma_start(vec[:], a["attn1_vec"]).then_inc(const_in, 16)
                    sp.dma_start(b_out[:], a["attn1_bo"]).then_inc(const_in, 16)
                    sp.dma_start(shifts[:], a["shift_mats"]).then_inc(const_in, 16)
                    sp.dma_start(w_mix[:], a["w_mix"].to_broadcast([P, 1 + len(CHANNEL_SHIFTS)])).then_inc(const_in, 16)
                else:
                    sp.dma_start(w_kv[:], a["attn0_kv"]).then_inc(const_in, 16)

                def load_in(c, m):
                    for b in range(1 if mix else 2):
                        sp.wait_ge(in_split[b], turn(c, m))
                        sp.dma_start(w_in[b][:], a["attn1_v"][m] if mix else a["attn0_q"][2 * m + b]
                                     ).then_inc(head_in[b], 16)

                def load_out(c, m):
                    for b in range(2):
                        sp.wait_ge(wo_split[b], turn(c, m))
                        sp.dma_start(w_out[b][:], a["attn1_o" if mix else "attn0_o"][2 * m + b]).then_inc(wo_in[b], 16)

                with sp.Fori(0, NCH) as c:
                    if mix:
                        with sp.Fori(0, MH) as m:
                            for b in range(2):
                                sp.wait_ge(qk_split[b], own(c, m))
                                sp.dma_start(w_qk[b][:], a["attn1_qk"][2 * m + b]).then_inc(qk_in[b], 16)
                    load_in(c, 0)
                    with sp.Fori(1, MH) as m:
                        load_in(c, m)
                        load_out(c, m - 1)
                    load_out(c, MH - 1)

            @block.gpsimd
            def _(pool):
                def low_part(done, low, raw, high):
                    nc.gpsimd.tensor_tensor(low, raw, high.bitcast(F32), ALU.subtract).then_inc(done, 1)

                def qk_low_part(c, m, b):
                    pool.wait_ge(qk_high_done[b], own(c, m) + 1)
                    low_part(qk_split[b], qk_low[b][:], w_qk[b][:], qk_high[b][:])

                def in_low_part(c, m, b):
                    pool.wait_ge(in_high_done[b], turn(c, m) + 1)
                    low_part(in_split[b], wi_low[b][:], w_in[b][:], wi_high[b][:])

                def out_low_part(c, m, b):
                    pool.wait_ge(wo_high_done[b], turn(c, m) + 1)
                    low_part(wo_split[b], wo_low[b][:], w_out[b][:], wo_high[b][:])

                def chunk_low_part(c, count):
                    pool.wait_ge(xc_high_done, count)
                    low_part(xc_ready, xc_low[:], k.xn[:, :, bass.ts(c, CH)], xc_high[:])

                chunk_low_part(0, X0 + 1)
                with pool.Fori(0, NCH) as c:
                    if not mix:
                        in_low_part(c, 0, 0)
                        in_low_part(c, 0, 1)
                    if mix:
                        with pool.Fori(0, MH) as m:
                            qk_low_part(c, m, 0)
                            qk_low_part(c, m, 1)
                        in_low_part(c, 0, 0)

                    def step(m, b, first, last):
                        if last == 0 and not mix:
                            in_low_part(c, m + 1, b)
                        if last == 0 and mix and b == 1:
                            in_low_part(c, m + 1, 0)
                        out_low_part(c, m, b)
                        if last == 1:
                            chunk_low_part((c + 1) & (NCH - 1), c + X0 + 2)

                    steps(pool, c, step)

            @block.tensor
            def _(pe):
                def query_key(c, m, b):
                    t = turn(c, m)
                    pe.wait_ge(xc_ready, c + X0 + 1)
                    pe.wait_ge(qk_split[b], own(c, m) + 1)
                    pe.wait_ge(qk_biased[b], own(c, m))
                    for out, at in ((s_ps[:, b], 0), (t_ps[:, b], HID)):
                        for kt in range(KT):
                            w = slice(at + kt * P, at + kt * P + P)
                            last = product(out, qk_high[b][:, w], qk_low[b][:, w], xc_high[:, kt], xc_low[:, kt],
                                           kt == 0, kt == KT - 1)
                    last.then_inc(qk_proj[b], 1)

                def queries(c, m, b):
                    t = turn(c, m)
                    pe.wait_ge(*before(q_ready, b, t))
                    if mix:
                        pe.wait_ge(v_ready[1], t)
                        pe.wait_ge(circ_ready[b], own(c, m) + 1)
                        last = nc.tensor.matmul(proj[:], circ_g[b][:], q_all[:, 2 * m + b], start=True, stop=True)
                    else:
                        pe.wait_ge(in_split[b], t + 1)
                        for kt in range(KT):
                            w = slice(kt * P, kt * P + P)
                            last = product(proj[:], wi_high[b][:, w], wi_low[b][:, w], xc_high[:, kt], xc_low[:, kt],
                                           kt == 0, kt == KT - 1)
                    last.then_inc(q_proj[b], 1)

                def values(c, m, b):
                    t = turn(c, m)
                    pe.wait_ge(in_split[0], t + 1)
                    pe.wait_ge(q_ready[1], t + 1)
                    pe.wait_ge(v_ready[0], t + b)
                    pe.wait_ge(v_ready[1], t)
                    for i in range(2):
                        for kt in range(KT):
                            z, w = slice((2 * b + i) * P, (2 * b + i + 1) * P), slice(kt * 2 * D, (kt + 1) * 2 * D)
                            last = product(proj[:, i * 2 * D:(i + 1) * 2 * D], xc_high[:, kt, z], xc_low[:, kt, z],
                                           wi_high[0][:, w], wi_low[0][:, w], kt == 0, kt == KT - 1)
                    last.then_inc(v_proj[b], 1)

                def scores(c, m, b):
                    t = turn(c, m)
                    pe.wait_ge(q_ready[b], t + 1)
                    if mix:
                        pe.wait_ge(k_ready[b], own(c, m) + 1)
                    pe.wait_ge(*before(masked, b, t))
                    for s in range(2):
                        for i in range(2):
                            q, keys = slice(s * SEQ + i * P, s * SEQ + i * P + P), slice(s * SEQ, s * SEQ + SEEN[i])
                            out = s_ps[:, s, AT[i]:AT[i] + SEEN[i]]
                            if mix:
                                last = nc.tensor.matmul(out, qT[b][:, q], kT[b][:, keys], start=True, stop=True)
                            else:
                                last = product(out, qT_high[b][:, q], qT_low[b][:, q],
                                               k_high[:, m // 2, keys], k_low[:, m // 2, keys])
                    last.then_inc(scored[b], 1)

                def turn_probs(c, m, b):
                    t = turn(c, m)
                    pe.wait_ge(normed[b], t + 1)
                    pe.wait_ge(*before(pt_ready, b, t))
                    for s in range(2):
                        for j in range(2):
                            for q in range(Q0[j], SEQ, P):
                                to, key = J_AT[j] + q - Q0[j], AT[q // P] + j * P
                                last = nc.tensor.transpose(t_ps[:, s, to:to + P], probs[b][:, s, key:key + P], k.ident[:])
                    last.then_inc(turned[b], 1)

                def context(c, m, b):
                    t = turn(c, m)
                    pe.wait_ge(pt_ready[b], t + 1)
                    pe.wait_ge(v_ready[0 if mix else b], t + 1)
                    if mix:
                        pe.wait_ge(v_ready[1], t + 1)
                    pe.wait_ge(*before(o_ready, b, t))
                    for s in range(2):
                        for j in range(2):
                            out = ctx_bank[:, s * SEQ + Q0[j]:(s + 1) * SEQ]
                            z = slice(J_AT[j], J_AT[j] + SEQ - Q0[j])
                            if mix:
                                last = nc.tensor.matmul(out, vs[:, s, j, b * D:(b + 1) * D], pT[b][:, s, z], start=j == 0, stop=j == 1)
                            else:
                                last = product(out, vs[b][:, 2 * s + j, 0], vs[b][:, 2 * s + j, 1],
                                               pT_high[b][:, s, z], pT_low[b][:, s, z], j == 0, j == 1)
                    last.then_inc(ctx_done[b], 1)

                def project_out(c, m, b, first, final):
                    t = turn(c, m)
                    if first:
                        pe.wait_ge(y_added, c + C0 + 1)
                    pe.wait_ge(wo_split[b], t + 1)
                    pe.wait_ge(o_ready[b], t + 1)
                    for kt in range(KT):
                        w = slice(kt * P, kt * P + P)
                        last = product(y[kt][:], wo_high[b][:, w], wo_low[b][:, w], oT_high[b][:], oT_low[b][:], first, final)
                    last.then_inc(y_done[b], 1)

                pe.wait_ge(setup, 2)
                with pe.Fori(0, NCH) as c:
                    if mix:
                        with pe.Fori(0, MH) as m:
                            query_key(c, m, 0)
                            query_key(c, m, 1)
                        pe.wait_ge(summed[1], own(c, MH - 1) + 1)
                        for i in range(2):
                            last = nc.tensor.matmul(s_ps[:, i], k.mean_mat[:], acc[:, i], start=True, stop=True)
                        last.then_inc(sums_done, 1)
                    else:
                        pe.wait_ge(xc_ready, c + X0 + 1)
                        def project_kv(i):
                            bank = t_ps[:, i % 2]
                            if i >= 2:
                                pe.wait_ge(kv_ready, c * 8 + i - 1)
                            for kt in range(KT):
                                if i < GROUPS:
                                    g = slice(i * D, (i + 1) * D)
                                    last = product(bank, kv_high[:, 0, kt, g], kv_low[:, 0, kt, g],
                                                   xc_high[:, kt], xc_low[:, kt], kt == 0, kt == KT - 1)
                                else:
                                    z = slice((i - 4) * P, (i - 3) * P)
                                    last = product(bank, xc_high[:, kt, z], xc_low[:, kt, z],
                                                   kv_high[:, 1, kt], kv_low[:, 1, kt], kt == 0, kt == KT - 1)
                            last.then_inc(kv_proj, 1)

                        project_kv(0)
                    queries(c, 0, 0)
                    if mix:
                        queries(c, 0, 1)
                        values(c, 0, 0)
                    else:
                        project_kv(1)
                        pe.wait_ge(kv_ready, c * 8 + 1)
                    scores(c, 0, 0)
                    if not mix:
                        queries(c, 0, 1)
                        for i in range(2, 8):
                            project_kv(i)
                        pe.wait_ge(kv_ready, c * 8 + 8)

                    def step(m, b, first, last):
                        nxt = (m, 1) if b == 0 else (m + 1, 0)
                        if last < 2:
                            scores(c, *nxt)
                        if mix and b == 0:
                            values(c, m, 1)
                        turn_probs(c, m, b)
                        if not first:
                            prev = (m, 0) if b == 1 else (m - 1, 1)
                            project_out(c, *prev, first=isinstance(m, int) and m == 0, final=False)
                        if last == 0:
                            queries(c, m + 1, b)
                        context(c, m, b)
                        if mix and b == 1 and last == 0:
                            values(c, m + 1, 0)

                    steps(pe, c, step)
                    project_out(c, MH - 1, 1, first=False, final=True)

            @block.scalar
            def _(act):
                def bias_qk(c, m, b):
                    t = turn(c, m)
                    act.wait_ge(qk_proj[b], own(c, m) + 1)
                    act.wait_ge(summed[b], own(c, m))
                    h = 2 * m + b
                    nc.scalar.activation(q_all[:, h], s_ps[:, b], ACT.Identity, bias=vec[:, 0, bass.ds(h, 1)])
                    nc.scalar.activation(k_all[:, h], t_ps[:, b], ACT.Identity, bias=vec[:, 1, bass.ds(h, 1)])
                    nc.scalar.activation(sq_q[b][:], s_ps[:, b], ACT.Square, bias=vec[:, 0, bass.ds(h, 1)])
                    nc.scalar.activation(sq_k[b][:], t_ps[:, b], ACT.Square, bias=vec[:, 1, bass.ds(h, 1)]
                                         ).then_inc(qk_biased[b], 1)

                def take_queries(c, m, b):
                    t = turn(c, m)
                    if mix:
                        act.wait_ge(q_proj[b], t)
                        h = 2 * m + b
                        nc.scalar.activation(circ_g[b][:], circ[:], ACT.Copy, scale=vec[:, 3, bass.ds(h, 1)]
                                             ).then_inc(circ_ready[b], 1)
                    else:
                        act.wait_ge(q_proj[b], t + 1)
                        act.wait_ge(scored[b], t)
                        nc.scalar.activation(qT_high[b][:], proj[:], ACT.Copy).then_inc(q_high_done[b], 1)

                def in_high_part(c, m, b):
                    act.wait_ge(head_in[b], 16 * turn(c, m))
                    act.wait_ge(v_proj[1], own(c, m)) if mix else act.wait_ge(q_proj[b], turn(c, m))
                    nc.scalar.activation(wi_high[b][:], w_in[b][:], ACT.Copy).then_inc(in_high_done[b], 1)

                def out_high_part(c, m, b):
                    act.wait_ge(wo_in[b], 16 * turn(c, m))
                    act.wait_ge(y_done[b], turn(c, m))
                    nc.scalar.activation(wo_high[b][:], w_out[b][:], ACT.Copy).then_inc(wo_high_done[b], 1)

                def take_values(c, m, b):
                    t = turn(c, m)
                    if mix:
                        act.wait_ge(v_proj[b], own(c, m) + 1)
                        act.wait_ge(ctx_done[1], t)
                        dst, src = vs[:, b], proj[:].rearrange("p (i z) -> p i z", i=2)
                    else:
                        act.wait_ge(ctx_done[b], t)
                        dst, src = vs[b][:], v_all[:, :, :, bass.ds(m // 2 * D, D)].bitcast(F32)
                    nc.scalar.activation(dst, src, ACT.Copy).then_inc(v_ready[b], 1)

                def take_turned(c, m, b):
                    t = turn(c, m)
                    act.wait_ge(turned[b], t + 1)
                    act.wait_ge(ctx_done[b], t)
                    dst, done = (pT[b], pt_ready[b]) if mix else (pT_high[b], pt_high_done[b])
                    nc.scalar.activation(dst[:], t_ps[:, :, 0:WIDE], ACT.Copy).then_inc(done, 1)

                def exponentials(c, m, b):
                    t = turn(c, m)
                    act.wait_ge(shifted[b], t + 1)
                    for i in range(2):
                        for s in range(2):
                            row = probs[b][:, s, AT[i]:AT[i] + SEEN[i]]
                            last = nc.scalar.activation(row, row, ACT.Exp, bias=shift[b][:, i, s:s + 1],
                                                        scale=D ** -0.5, accum_out=total[b][:, i, s:s + 1])
                    last.then_inc(exped[b], 1)

                def take_context(c, m, b):
                    t = turn(c, m)
                    act.wait_ge(ctx_done[b], t + 1)
                    act.wait_ge(y_done[b], t)
                    if mix:
                        taken = nc.scalar.activation(oT_high[b][:], ctx_bank[:], ACT.Identity,
                                                     bias=vec[:, 2, bass.ds(2 * m + b, 1)])
                    else:
                        taken = nc.scalar.activation(oT_high[b][:], ctx_bank[:], ACT.Copy)
                    taken.then_inc(o_high_done[b], 1)

                if mix:
                    act.wait_ge(setup, 2)
                else:
                    act.wait_ge(const_in, 32)
                    nc.scalar.activation(kv_high[:], w_kv[:], ACT.Copy).then_inc(setup, 1)

                def take_chunk(c):
                    nc.scalar.activation(xc_high[:], k.xn[:, :, bass.ts(c, CH)], ACT.Copy).then_inc(xc_high_done, 1)

                take_chunk(0)
                with act.Fori(0, NCH) as c:
                    if not mix:
                        in_high_part(c, 0, 0)
                        in_high_part(c, 0, 1)
                    if mix:
                        act.wait_ge(qk_in[0], 16 * own(c, 0))
                        act.wait_ge(qk_proj[0], own(c, 0))
                        nc.scalar.activation(qk_high[0][:], w_qk[0][:], ACT.Copy).then_inc(qk_high_done[0], 1)
                        with act.Fori(0, MH) as m:
                            bias_qk(c, m, 0)
                            bias_qk(c, m, 1)
                        act.wait_ge(sums_done, c + 1)
                        nc.scalar.activation(rms[:], s_ps[:], ACT.Sqrt, bias=eps6[:, 0:1], scale=HID / (HEADS * D)
                                             ).then_inc(rms_done, 1)
                        in_high_part(c, 0, 0)
                    else:
                        def kv_high_part(i):
                            act.wait_ge(kv_proj, c * 8 + i + 1)
                            dst = k_high[:, i] if i < GROUPS else v_all[:, i - 4, 0]
                            nc.scalar.activation(dst, t_ps[:, i % 2], ACT.Copy).then_inc(kv_high_done, 1)

                    if mix:
                        take_queries(c, 0, 0)
                        take_queries(c, 0, 1)
                        take_values(c, 0, 0)
                        exponentials(c, 0, 0)
                    else:
                        kv_high_part(0)
                        take_queries(c, 0, 0)
                        kv_high_part(1)
                        take_queries(c, 0, 1)
                        kv_high_part(2)
                        exponentials(c, 0, 0)
                        for i in range(3, 8):
                            kv_high_part(i)
                        act.wait_ge(kv_ready, c * 8 + 8)
                        take_values(c, 0, 0)

                    def step(m, b, first, last):
                        nxt = (m, 1) if b == 0 else (m + 1, 0)
                        if last == 0:
                            if not mix:
                                in_high_part(c, m + 1, b)
                            elif b == 0:
                                take_queries(c, m + 1, b)
                            else:
                                in_high_part(c, m + 1, 0)
                                take_queries(c, m + 1, b)
                        if mix and b == 0:
                            take_values(c, m, 1)
                        take_turned(c, m, b)
                        out_high_part(c, m, b)
                        if last == 0 and not mix:
                            take_queries(c, m + 1, b)
                        if last < 2:
                            exponentials(c, *nxt)
                        if last == 1:
                            take_chunk((c + 1) & (NCH - 1))
                        take_context(c, m, b)
                        if last < 2 and not mix:
                            take_values(c, *nxt)
                        if mix and b == 1 and last == 0:
                            take_values(c, m + 1, 0)

                    steps(act, c, step)

            @block.vector
            def _(dve):
                def sum_squares(c, m, b):
                    t = turn(c, m)
                    dve.wait_ge(acc_zero, c + len(CHANNEL_SHIFTS))
                    dve.wait_ge(qk_biased[b], own(c, m) + 1)
                    dve.wait_ge(*before(summed, b, own(c, m)))
                    nc.vector.tensor_tensor(acc[:, 0], acc[:, 0], sq_q[b][:], ALU.add)
                    nc.vector.tensor_tensor(acc[:, 1], acc[:, 1], sq_k[b][:], ALU.add).then_inc(summed[b], 1)

                def take_queries(c, m, b):
                    t = turn(c, m)
                    dve.wait_ge(q_proj[b], t + 1)
                    dve.wait_ge(scored[b], t)
                    nc.vector.tensor_tensor(qT[b][:], proj[:], inv_rms[:, 0], ALU.mult).then_inc(q_ready[b], 1)
                    h = 2 * m + b
                    nc.vector.scalar_tensor_tensor(out=kT[b][:], in0=k_all[:, h], scalar=vec[:, 4, bass.ds(h, 1)],
                                                   in1=inv_rms[:, 1], op0=ALU.mult, op1=ALU.mult).then_inc(k_ready[b], 1)

                def qk_high_part(c, m, b):
                    dve.wait_ge(qk_in[b], 16 * own(c, m))
                    dve.wait_ge(qk_proj[b], own(c, m))
                    nc.vector.tensor_copy(qk_high[b][:], w_qk[b][:]).then_inc(qk_high_done[b], 1)

                def low_part(done, low, whole, high):
                    nc.vector.tensor_tensor(low, whole, high.bitcast(F32), ALU.subtract).then_inc(done, 1)

                def queries_low(c, m, b):
                    dve.wait_ge(q_high_done[b], turn(c, m) + 1)
                    low_part(q_ready[b], qT_low[b][:], proj[:], qT_high[b][:])

                def turned_low(c, m, b):
                    dve.wait_ge(pt_high_done[b], turn(c, m) + 1)
                    low_part(pt_ready[b], pT_low[b][:], t_ps[:, :, 0:WIDE], pT_high[b][:])

                def mask_scores(c, m, b):
                    t = turn(c, m)
                    dve.wait_ge(scored[b], t + 1)
                    dve.wait_ge(turned[b], t)
                    nc.vector.tensor_tensor(probs[b][:], s_ps[:, :, 0:WIDE], mask[:].unsqueeze(1).to_broadcast([P, 2, WIDE]),
                                            ALU.add).then_inc(masked[b], 1)
                    dve.wait_ge(masked[b], t + 1)
                    for i in range(2):
                        last = nc.vector.tensor_reduce(peak[b][:, i], probs[b][:, :, AT[i]:AT[i] + SEEN[i]], AX_X, ALU.max)
                    last.then_inc(peaked[b], 1)
                    dve.wait_ge(peaked[b], t + 1)
                    nc.vector.tensor_scalar(shift[b][:], peak[b][:], -(D ** -0.5), None, ALU.mult).then_inc(shifted[b], 1)

                def normalise(c, m, b):
                    t = turn(c, m)
                    dve.wait_ge(exped[b], t + 1)
                    nc.vector.reciprocal(inverse[b][:], total[b][:]).then_inc(inverted[b], 1)
                    dve.wait_ge(inverted[b], t + 1)
                    for i in range(2):
                        rows = probs[b][:, :, AT[i]:AT[i] + SEEN[i]]
                        last = nc.vector.tensor_tensor(rows, rows, inverse[b][:, i].unsqueeze(2).to_broadcast([P, 2, SEEN[i]]),
                                                       ALU.mult)
                    last.then_inc(normed[b], 1)

                def take_context(c, m, b):
                    dve.wait_ge(o_high_done[b], turn(c, m) + 1)
                    if mix:
                        nc.vector.scalar_tensor_tensor(out=oT_low[b][:], in0=ctx_bank[:], scalar=vec[:, 2, bass.ds(2 * m + b, 1)],
                                                       in1=oT_high[b][:].bitcast(F32), op0=ALU.add, op1=ALU.subtract
                                                       ).then_inc(o_ready[b], 1)
                    else:
                        low_part(o_ready[b], oT_low[b][:], ctx_bank[:], oT_high[b][:])

                dve.wait_ge(const_in, 80 if mix else 32)
                if mix:
                    nc.vector.memset(eps6[:], 1e-6)
                    nc.vector.tensor_scalar(circ[:], shifts[:, 0], w_mix[:, 0:1], None, ALU.mult).then_inc(setup, 1)
                    for i in range(len(CHANNEL_SHIFTS)):
                        dve.wait_ge(setup, 1) if i == 0 else dve.wait_ge(acc_zero, i)
                        last = nc.vector.scalar_tensor_tensor(out=circ[:], in0=shifts[:, i + 1], scalar=w_mix[:, i + 1:i + 2],
                                                              in1=circ[:], op0=ALU.mult, op1=ALU.add)
                        last.then_inc(acc_zero if i + 1 < len(CHANNEL_SHIFTS) else setup, 1)
                else:
                    dve.wait_ge(setup, 1)
                    nc.vector.tensor_tensor(kv_low[:], w_kv[:], kv_high[:].bitcast(F32), ALU.subtract).then_inc(setup, 1)
                with dve.Fori(0, NCH) as c:
                    if mix:
                        qk_high_part(c, 0, 1)
                        nc.vector.memset(acc[:], 0.0).then_inc(acc_zero, 1)
                        with dve.Fori(0, MH - 1) as m:
                            for b in range(2):
                                qk_high_part(c, m + 1, b)
                                sum_squares(c, m, b)
                        sum_squares(c, MH - 1, 0)
                        sum_squares(c, MH - 1, 1)
                        dve.wait_ge(rms_done, c + 1)
                        nc.vector.reciprocal(inv_rms[:], rms[:]).then_inc(inv_done, 1)
                        dve.wait_ge(inv_done, c + 1)
                        take_queries(c, 0, 0)
                        take_queries(c, 0, 1)
                    else:
                        def kv_low_part(i):
                            dve.wait_ge(kv_high_done, c * 8 + i + 1)
                            dst = (k_low[:, i], k_high[:, i]) if i < GROUPS else (v_all[:, i - 4, 1], v_all[:, i - 4, 0])
                            low_part(kv_ready, dst[0], t_ps[:, i % 2], dst[1])

                        kv_low_part(0)
                        queries_low(c, 0, 0)
                        kv_low_part(1)
                    mask_scores(c, 0, 0)
                    if mix:
                        normalise(c, 0, 0)
                    else:
                        queries_low(c, 0, 1)
                        kv_low_part(2)
                        kv_low_part(3)
                        normalise(c, 0, 0)
                        for i in range(4, 8):
                            kv_low_part(i)

                    def step(m, b, first, last):
                        nxt = (m, 1) if b == 0 else (m + 1, 0)
                        if last < 2:
                            mask_scores(c, *nxt)
                        if not mix:
                            turned_low(c, m, b)
                        if last == 0:
                            (take_queries if mix else queries_low)(c, m + 1, b)
                        if last < 2:
                            normalise(c, *nxt)
                        take_context(c, m, b)

                    steps(dve, c, step)
                    dve.wait_ge(y_done[1], turn(c, MH - 1) + 1)
                    for kt in range(KT):
                        x = k.x[:, kt, bass.ts(c, CH)]
                        if mix:
                            add = nc.vector.scalar_tensor_tensor(out=x, in0=y[kt][:], scalar=b_out[:, kt:kt + 1], in1=x,
                                                                 op0=ALU.add, op1=ALU.add)
                        else:
                            add = nc.vector.tensor_tensor(x, y[kt][:], x, ALU.add)
                    add.then_inc(y_added, 1)


def store_result(nc, k, out):
    stored = k.sem("result_stored")
    block = nc.Block()
    with block:
        @block.sync
        def _(sp):
            sp.dma_start(out, k.x[:]).then_inc(stored, 16)
            sp.wait_ge(stored, 16)


def macaron(nc, a, out):
    w0 = nc.dram_tensor("ffn0_weights", [T0, P, WCOL], F32, kind="Internal").ap()
    comb_dram = nc.dram_tensor("combine_weights", [EX, TOK], F32, kind="Internal").ap()
    with ExitStack() as ctx:
        k = Core(nc, ctx)
        sb = lambda name, shape, dt: ctx.enter_context(nc.sbuf_tensor(name, shape, dt))
        k.x = sb("x", [P, KT, TOK], F32)
        k.mean_mat = sb("mean_mat", [P, P], F32)
        k.eps = sb("eps", [P, 1], F32)
        k.ident = sb("ident", [P, P], F32)
        k.plan = sb("plan", [1, PLAN], I32)
        k.turns_run = sb("turns_run", [1, 1], F32)
        ps = lambda name, *shape: ctx.enter_context(nc.psum_tensor(name, [P, *shape, CH], F32))
        low, k.pair, high = [ps(f"bank{i}") for i in range(3)], [ps("banks34", 2), ps("banks56", 2)], ps("bank7")
        k.bank = low + [k.pair[0][:, 0], k.pair[0][:, 1], k.pair[1][:, 0], k.pair[1][:, 1], high]
        load_constants(nc, k, a["x"], a)
        dequantise(nc, k, a["ffn0_codes"], a["ffn0_scales"], w0)
        k.retire("dq")

        def ffn0(tag):
            with ExitStack() as inner:
                k.xn_high = inner.enter_context(nc.sbuf_tensor(f"xn_high_{tag}", [P, KT, TOK], F32R))
                k.xn_low = inner.enter_context(nc.sbuf_tensor(f"xn_low_{tag}", [P, KT, TOK], F32R))
                layernorm(nc, k, tag, True)
                feed_forward(nc, k, tag, P, w0[:, :, 0:2 * HID], w0[:, :, 2 * HID:], ACT.Gelu_apprx_tanh)

        def ffn1(tag):
            with ExitStack() as inner:
                k.xn_high = inner.enter_context(nc.sbuf_tensor(f"xn_high_{tag}", [P, KT, TOK], F32R))
                k.xn_low = inner.enter_context(nc.sbuf_tensor(f"xn_low_{tag}", [P, KT, TOK], F32R))
                layernorm(nc, k, tag, True)
                route(nc, k, tag, a["router"], a["router_bias"], a["plan_consts"], comb_dram)
                feed_forward(nc, k, tag, ER, a["ffn1_gu"], a["ffn1_down"], ACT.Silu, comb_dram)

        def attn(tag, mix):
            with ExitStack() as inner:
                k.xn = inner.enter_context(nc.sbuf_tensor(f"xn_{tag}", [P, KT, TOK], F32))
                layernorm(nc, k, tag, False)
                attention(nc, k, tag, a, mix)

        ffn0("f0")
        attn("a0", False)
        ffn0("f1")
        k.retire("gqa")
        k.retire("fp4")
        ffn1("f2")
        attn("a1", True)
        ffn1("f3")
        store_result(nc, k, out)


def planes(w):
    return w.reshape(P, KT, *w.shape[1:])


def lay_out(i):
    a = {}
    tokens = lambda x: np.ascontiguousarray(x)
    a["x"] = tokens(i["L0_attn_x"].reshape(TOK, P, KT).transpose(1, 2, 0))
    units = T0 // 2

    def rows(w):
        return w.reshape(units, P, 2, -1).transpose(0, 3, 2, 1)

    def down(w):
        return w.reshape(P, KT, units, -1).transpose(2, 3, 1, 0)

    join = lambda g, u, d: np.concatenate([z.reshape(units, -1, HID) for z in (g, u, d)], axis=2)
    a["ffn0_codes"] = join(rows(i["L0_ffn_gate_W_packed"]), rows(i["L0_ffn_up_W_packed"]),
                           down(i["L0_ffn_down_W_packed"]))
    a["ffn0_scales"] = join(rows(i["L0_ffn_gate_scales"]), rows(i["L0_ffn_up_scales"]),
                            down(i["L0_ffn_down_scales"]))
    def halves(w, shared):
        w = np.concatenate([w.transpose(1, 0, 2).reshape(HID, ROUTED), shared], axis=1)
        return w.reshape(P, KT, 2 * EX, ER).transpose(2, 0, 1, 3).reshape(2 * EX, P, 2 * ER)

    a["ffn1_gu"] = np.concatenate([halves(i["L1_ffn_gate_w"], i["L1_ffn_sh_gate_w"]),
                                   halves(i["L1_ffn_up_w"], i["L1_ffn_sh_up_w"])], axis=2)
    d = np.concatenate([i["L1_ffn_down_w"].reshape(ROUTED, HID), i["L1_ffn_sh_down_w"]])
    a["ffn1_down"] = d.reshape(2 * EX, ER, P, KT).transpose(0, 1, 3, 2).reshape(2 * EX, ER, HID)
    e = np.arange(EX)
    a["plan_consts"] = np.concatenate([e[:, None] < e, np.ones((EX, EX)), np.tile(e, (EX, 1)), e[:, None],
                                       e[:, None] == EX - 1, NO_PLACE * (e[:, None] < NE)], axis=1).astype(np.float32)
    a["router"] = planes(i["L1_ffn_w_router"])
    a["router_bias"] = i["L1_ffn_corr_bias"].reshape(1, NE)
    by_head = lambda w: planes(w).reshape(P, KT, HEADS, D).transpose(2, 0, 1, 3).reshape(HEADS, P, HID)
    a["attn0_q"] = by_head(i["L0_attn_w_q"])
    a["attn0_kv"] = planes(i["L0_attn_w_kv"]).reshape(P, KT, 2, GROUPS * D).transpose(0, 2, 1, 3)
    outs = lambda w: w.reshape(HEADS, D, P, KT).transpose(0, 1, 3, 2).reshape(HEADS, D, HID)
    a["attn0_o"] = outs(i["L0_attn_w_dense"])
    a["attn1_qk"] = np.concatenate([by_head(i["L1_attn_wq"].T), by_head(i["L1_attn_wk"].T)], axis=2)
    a["attn1_v"] = (by_head(i["L1_attn_wv"].T).reshape(HEADS // 2, 2, P, KT, D).transpose(0, 2, 3, 1, 4)
                    .reshape(HEADS // 2, P, 2 * HID))
    a["attn1_o"] = outs(i["L1_attn_wo"].T)
    a["attn1_vec"] = np.stack([i[f"L1_attn_{n}"].reshape(HEADS, D) for n in ("bq", "bk", "bv", "gq", "gk")]
                              ).transpose(2, 0, 1)
    a["attn1_bo"] = i["L1_attn_bo"].reshape(P, KT)
    a["w_mix"] = i["L1_attn_w_mix"].reshape(1, -1)
    eye = np.eye(P, dtype=np.float32)
    a["shift_mats"] = np.stack([np.roll(eye, s, axis=1) for s in (0,) + CHANNEL_SHIFTS], axis=1)
    q, key = np.arange(SEQ)[:, None], np.arange(SEQ)[None, :]
    near = np.isin((q - key) % SEQ, np.array(SEQ_SHIFTS) % SEQ)
    lay_mask = lambda seen: np.where(seen, 0.0, -BIG).astype(np.float32).reshape(2, P, SEQ).transpose(1, 0, 2).reshape(P, 2 * SEQ)
    a["near_mask"] = lay_mask(near)
    a["causal_mask"] = np.delete(lay_mask(q >= key), np.s_[P:SEQ], axis=1)
    a["ident"] = np.eye(P, dtype=np.float32)
    return {n: np.ascontiguousarray(v) for n, v in a.items()}


def kernel(**inputs):
    import concourse.bacc as bacc
    from concourse.bass_utils import run_bass_kernel_spmd

    nc = bacc.Bacc("TRN2", target_bir_lowering=False, num_devices=1)
    arrays = lay_out({n: np.asarray(v) for n, v in inputs.items()})
    aps = {n: nc.dram_tensor(f"in_{n}", v.shape, mybir.dt.from_np(v.dtype), kind="ExternalInput").ap()
           for n, v in arrays.items()}
    out = nc.dram_tensor("out_0_dram", (P, KT, TOK), F32, kind="ExternalOutput").ap()
    macaron(nc, aps, out)
    r = run_bass_kernel_spmd(nc, [{f"in_{n}": v for n, v in arrays.items()}], core_ids=[0])
    y = r.results[0]["out_0_dram"]
    return np.ascontiguousarray(y.transpose(2, 0, 1)).reshape(BATCH, SEQ, HID)
```

```python
from contextlib import ExitStack

import numpy as np

import concourse.bass as bass
from concourse import mybir

F32 = mybir.dt.float32
F32R = mybir.dt.float32r
I32 = mybir.dt.int32
BF16 = mybir.dt.bfloat16
ALU = mybir.AluOpType
ACT = mybir.ActivationFunctionType
AX_X = mybir.AxisListType.X



P = 128
HID = 256
KT = HID // P
BATCH, SEQ = 8, 256
TOK = BATCH * SEQ
CH = 512
NCH = TOK // CH
MLP = 2048
T0 = MLP // P
NE, MI, SHARED = 32, 176, 352
ROUTED = NE * MI
NG, TOPG, TOPK = 8, 4, 6
WCOL = 3 * HID
EX = NE + SHARED // MI
ER = MI // 2
PAIRS_AT, FIRST_AT = (SHARED // MI + NE) * NCH, (SHARED // MI + NE) * NCH + NCH
LAST_AT = FIRST_AT + NCH + 1
PLAN = LAST_AT + NCH
NO_PLACE = 99.0
BIG = 1.0e30
HEADS, D = 16, 128
GROUPS = 4
CHANNEL_SHIFTS = (1, 2, 4, 8)
SEQ_SHIFTS = (0, 1, -1, 2, -2, 4, -4, 8, -8, 16, -16, 32, -32, 64, -64, 128)


class Core:

    def __init__(self, nc, ctx):
        self.nc, self.ctx, self.named, self.passes, self.route_steps, self.primed = nc, ctx, {}, {}, 0, set()

    def sem(self, name):
        if name not in self.named:
            self.named[name] = self.nc.alloc_semaphore(name=name)
        return self.named[name]

    def retire(self, kind):
        gone = [name for name in self.named if kind in name]
        self.nc.clear_and_free_semaphores([self.named.pop(name) for name in gone])
        self.nc.all_engine_barrier()

    def again(self, stage):
        self.passes[stage] = self.passes.get(stage, -1) + 1
        return self.passes[stage]

    def sems(self, name, n=2):
        return [self.sem(f"{name}{i}") for i in range(n)]

    def prime(self, sp, *groups, by=1):
        for group in groups:
            for sem in group if isinstance(group, list) else [group]:
                if sem.name not in self.primed:
                    self.primed.add(sem.name)
                    sp.sem_inc(sem, by)


def set_constants(nc, k):
    ones_set = k.sem("ones_set")
    block = k.nc.Block()
    with block:
        @block.vector
        def _(dve):
            nc.vector.memset(k.mean_mat[:], 1.0 / HID).then_inc(ones_set, 1)
            nc.vector.memset(k.eps[:], 1e-5 / HID ** 2).then_inc(ones_set, 1)
            nc.vector.memset(k.turns_run[:], 1.0).then_inc(ones_set, 1)
            dve.wait_ge(ones_set, 3)


def dequantise(nc, k, packed, scales, w_out, x_t, ident):
    units = T0 // 2
    with ExitStack() as ctx:
        sb = lambda name, shape, dt: ctx.enter_context(nc.sbuf_tensor(name, shape, dt))
        codes = sb("dq_codes", [P, 2, WCOL], I32)
        scale = sb("dq_scale", [P, 2, WCOL], F32)
        two = lambda name, dt: [sb(f"dq_{name}{i}", [P, 2, WCOL], dt) for i in range(2)]
        mag, bit, steep, sign, value = two("mag", I32), two("bit", I32), two("steep", F32), two("sign", F32), two("value", F32)
        signed_scale = two("signed_scale", F32)
        done = sb("dq_done", [P, 2, 2, WCOL], F32)
        codes_in, scale_in, bits_done = k.sems("codes_in_dq"), k.sems("scale_in_dq"), k.sem("bits_done_dq")
        steep_done, sign_done, signed_done = k.sem("steep_done_dq"), k.sem("sign_done_dq"), k.sem("signed_done_dq")
        step, stored, x_in = k.sem("dq_step"), k.sems("dq_stored"), k.sem("x_in")
        nibble_done = k.sems("nibble_done_dq")
        block = nc.Block()

        def scaled(eng, u, nib):
            b = u % 2
            eng.wait_ge(step, 2 * u + 2)
            eng.wait_ge(signed_done, u + 1)
            if u >= 2:
                eng.wait_ge(stored[b], 16 * (u // 2))
            eng.tensor_tensor(
                done[:, b, :, 0:2 * HID].rearrange("p t (w k c) -> p w t k c", w=2, k=2)[:, :, :, nib],
                value[b][:, nib, 0:2 * HID].rearrange("p (w t c) -> p w t c", w=2, t=2),
                signed_scale[b][:, nib, 0:2 * HID].rearrange("p (w t c) -> p w t c", w=2, t=2), ALU.mult)
            eng.tensor_tensor(done[:, b, nib, 2 * HID:], value[b][:, nib, 2 * HID:], signed_scale[b][:, nib, 2 * HID:],
                              ALU.mult).then_inc(nibble_done[nib], 1)

        with block:
            @block.sync
            def _(sp):
                def load_codes(u):
                    if u >= 2:
                        sp.wait_ge(bits_done, u - 1)
                    sp.dma_start(codes[:, u % 2], packed[u]).then_inc(codes_in[u % 2], 16)

                load_codes(0)
                for u in range(units):
                    b = u % 2
                    if u + 1 < units:
                        load_codes(u + 1)
                    if u >= 2:
                        sp.wait_ge(signed_done, u - 1)
                    for g in range(8):
                        sp.dma_start(scale[16 * g:16 * g + 16, b], scales[u, g:g + 1].to_broadcast([16, WCOL])
                                     ).then_inc(scale_in[b], 16)
                    if u == 1:
                        sp.dma_start(k.x[:], x_t).then_inc(x_in, 16)
                        sp.dma_start(k.ident[:], ident).then_inc(x_in, 16)
                sp.wait_ge(x_in, 32)

            @block.scalar
            def _(act):
                def store(u):
                    act.wait_ge(nibble_done[0], u + 1)
                    act.wait_ge(nibble_done[1], u + 1)
                    act.dma_start(w_out[2 * u:2 * u + 2].rearrange("t p c -> p t c"), done[:, u % 2]
                                  ).then_inc(stored[u % 2], 16)

                for u in range(units):
                    b = u % 2
                    act.wait_ge(bits_done, u + 1)
                    if u >= 2:
                        act.wait_ge(signed_done, u - 1)
                        act.wait_ge(step, 2 * (u - 1))
                    nc.scalar.activation(sign[b][:], bit[b][:], ACT.Copy, bias=1.0, scale=-0.25).then_inc(sign_done, 1)
                    nc.scalar.activation(steep[b][:], mag[b][:], ACT.Copy, bias=-8.0, scale=2.0).then_inc(steep_done, 1)
                    if u >= 2:
                        store(u - 2)
                store(units - 2)
                store(units - 1)
                for b in range(2):
                    act.wait_ge(stored[b], 16 * (units // 2))

            @block.gpsimd
            def _(pool):
                def sign_scales(u):
                    b = u % 2
                    pool.wait_ge(scale_in[b], 128 * (u // 2 + 1))
                    pool.wait_ge(sign_done, u + 1)
                    if u >= 2:
                        pool.wait_ge(nibble_done[0], u - 1)
                        pool.wait_ge(nibble_done[1], u - 1)
                    nc.gpsimd.tensor_tensor(signed_scale[b][:], sign[b][:],
                                            scale[:, b:b + 1].to_broadcast([P, 2, WCOL]), ALU.mult
                                            ).then_inc(signed_done, 1)

                sign_scales(0)
                for u in range(units):
                    if u + 1 < units:
                        sign_scales(u + 1)
                    scaled(nc.gpsimd, u, 1)

            @block.vector
            def _(dve):
                def take_bits(u):
                    b = u % 2
                    dve.wait_ge(codes_in[b], 16 * (u // 2 + 1))
                    if u >= 2:
                        dve.wait_ge(steep_done, u - 1)
                    nc.vector.tensor_scalar(mag[b][:, 0], codes[:, b], 7, None, ALU.bitwise_and)
                    nc.vector.tensor_scalar(bit[b][:, 0], codes[:, b], 8, None, ALU.bitwise_and)
                    nc.vector.tensor_scalar(mag[b][:, 1], codes[:, b], 4, 7, ALU.logical_shift_right, ALU.bitwise_and)
                    nc.vector.tensor_scalar(bit[b][:, 1], codes[:, b], 4, 8, ALU.logical_shift_right, ALU.bitwise_and
                                            ).then_inc(bits_done, 1)

                take_bits(0)
                for u in range(units):
                    b = u % 2
                    if u + 1 < units:
                        take_bits(u + 1)
                    dve.wait_ge(bits_done, u + 1)
                    dve.wait_ge(steep_done, u + 1)
                    if u >= 2:
                        dve.wait_ge(nibble_done[0], u - 1)
                        dve.wait_ge(nibble_done[1], u - 1)
                    nc.vector.scalar_tensor_tensor(out=value[b][:], in0=mag[b][:], scalar=-2.0, in1=steep[b][:],
                                                   op0=ALU.add, op1=ALU.max).then_inc(step, 1)
                    dve.wait_ge(step, 2 * u + 1)
                    nc.vector.scalar_tensor_tensor(out=value[b][:], in0=mag[b][:], scalar=0.5, in1=value[b][:],
                                                   op0=ALU.mult, op1=ALU.max).then_inc(step, 1)
                    scaled(nc.vector, u, 0)


def layernorm(nc, k, tag, split):
    NT = CH // P
    with ExitStack() as ctx:
        sb = lambda name, shape, dt: ctx.enter_context(nc.sbuf_tensor(f"{name}_{tag}", shape, dt))
        centred, square = sb("centred", [P, NCH, KT, CH], F32), sb("square", [P, NCH, KT, CH], F32)
        root, rstd = sb("root", [P, NCH, NT], F32), sb("rstd", [P, NCH, NT], F32)
        diag = sb("diag", [P, NCH, NT, P], F32)
        scaled = sb("scaled", [P, 2, KT, CH], F32) if split else None
        mean_done, var_done = k.sem("mean_done"), k.sem("var_done")
        centred_done, square_done = k.sem("centred_done"), k.sem("square_done")
        root_done, rstd_done, scaled_done = k.sem("root_done"), k.sem("rstd_done"), k.sem("scaled_done")
        diag_done, spread_done = k.sem("diag_done"), k.sem("rstd_spread")
        if split:
            high_done, low_done, last_low_done = k.sem("xn_high_done"), k.sem("xn_low_done"), k.sem("xn_last_low")
            L0 = (NCH - 1) * (k.passes.get("split", -1) + 1)
        C0, S0 = NCH * k.again("layernorm"), NCH * k.again("split") if split else 0
        mean, var, spread = k.bank[0:NCH], [k.bank[NCH], k.bank[NCH + 1]], [k.bank[NCH + 2], k.bank[NCH + 3]]
        chunk = lambda c: slice(c * CH, (c + 1) * CH)

        def low_part(eng, c):
            eng.wait_ge(high_done, S0 + c + 1)
            eng.tensor_tensor(k.xn_low[:, :, chunk(c)], scaled[:, c % 2], k.xn_high[:, :, chunk(c)].bitcast(F32),
                              ALU.subtract).then_inc(low_done if c + 1 < NCH else last_low_done, 1)

        block = nc.Block()
        with block:
            @block.tensor
            def _(pe):
                def sum_mean(c):
                    for kt in range(KT):
                        last = nc.tensor.matmul(mean[c][:], k.mean_mat[:], k.x[:, kt, chunk(c)],
                                                start=kt == 0, stop=kt == KT - 1)
                    last.then_inc(mean_done, 1)

                def sum_var(c):
                    pe.wait_ge(square_done, C0 + c + 1)
                    if c >= 2:
                        pe.wait_ge(root_done, C0 + c - 1)
                    for t in range(NT):
                        for kt in range(KT):
                            last = nc.tensor.matmul(var[c % 2][:, t:t + 1], square[:, c, kt, t * P:(t + 1) * P],
                                                    k.mean_mat[:, 0:1], start=kt == 0, stop=kt == KT - 1)
                    last.then_inc(var_done, 1)

                def spread_rstd(c):
                    pe.wait_ge(diag_done, C0 + c + 1)
                    if c >= 2:
                        pe.wait_ge(scaled_done, C0 + c - 1)
                    nc.tensor.matmul(spread[c % 2][:], k.mean_mat[:], diag[:, c].rearrange("p t q -> p (t q)"),
                                     start=True, stop=True).then_inc(spread_done, 1)

                sum_mean(0)
                sum_mean(1)
                sum_var(0)
                sum_mean(2)
                sum_mean(3)
                for c in range(NCH):
                    if c + 1 < NCH:
                        sum_var(c + 1)
                    spread_rstd(c)

            @block.scalar
            def _(act):
                def take_square(c):
                    act.wait_ge(centred_done, C0 + c + 1)
                    nc.scalar.activation(square[:, c], centred[:, c], ACT.Square).then_inc(square_done, 1)

                def take_root(c):
                    act.wait_ge(var_done, C0 + c + 1)
                    nc.scalar.activation(root[:, c], var[c % 2][:, 0:NT], ACT.Sqrt, bias=k.eps[:, 0:1],
                                         scale=1.0 / HID ** 2).then_inc(root_done, 1)

                take_square(0)
                take_square(1)
                take_root(0)
                for c in range(NCH):
                    if c + 2 < NCH:
                        take_square(c + 2)
                    if c + 1 < NCH:
                        take_root(c + 1)
                    if split:
                        act.wait_ge(scaled_done, C0 + c + 1)
                        nc.scalar.activation(k.xn_high[:, :, chunk(c)], scaled[:, c % 2], ACT.Copy
                                             ).then_inc(high_done, 1)

            @block.vector
            def _(dve):
                def centre(c):
                    dve.wait_ge(mean_done, C0 + c + 1)
                    nc.vector.tensor_tensor(centred[:, c], k.x[:, :, chunk(c)],
                                            mean[c][:].unsqueeze(1).to_broadcast([P, KT, CH]), ALU.subtract
                                            ).then_inc(centred_done, 1)

                def make_diag(c):
                    dve.wait_ge(root_done, C0 + c + 1)
                    nc.vector.reciprocal(rstd[:, c], root[:, c]).then_inc(rstd_done, 1)
                    dve.wait_ge(rstd_done, C0 + c + 1)
                    nc.vector.tensor_tensor(diag[:, c], k.ident[:].unsqueeze(1).to_broadcast([P, NT, P]),
                                            rstd[:, c].unsqueeze(2).to_broadcast([P, NT, P]), ALU.mult
                                            ).then_inc(diag_done, 1)

                centre(0)
                centre(1)
                centre(2)
                make_diag(0)
                centre(3)
                for c in range(NCH):
                    if c + 1 < NCH:
                        make_diag(c + 1)
                    dve.wait_ge(spread_done, C0 + c + 1)
                    if split and c >= 2:
                        dve.wait_ge(low_done, L0 + c - 1)
                    out = scaled[:, c % 2] if split else k.xn[:, :, chunk(c)]
                    nc.vector.tensor_tensor(out, centred[:, c],
                                            spread[c % 2][:].unsqueeze(1).to_broadcast([P, KT, CH]), ALU.mult
                                            ).then_inc(scaled_done, 1)
                if split:
                    low_part(dve, NCH - 1)

            if split:
                @block.gpsimd
                def _(pool):
                    for c in range(NCH - 1):
                        low_part(pool, c)


def feed_forward(nc, k, tag, rows, w_gu, w_dn, func):
    kind, pairs = "fp4", T0 // 2
    run = k.again(kind)
    C0 = NCH * run + 1
    gu_cols = 4 * rows

    def begin(c):
        first = 1 + (NCH * run + c) * pairs
        return first, first + (pairs - 1)

    with ExitStack() as ctx:
        sb = lambda name, shape, dt: [ctx.enter_context(nc.sbuf_tensor(f"{name}{i}_{tag}", shape, dt)) for i in range(2)]
        gu_raw, gu_high, gu_low = sb("gu_raw", [P, gu_cols], F32), sb("gu_high", [P, gu_cols], F32R), sb("gu_low", [P, gu_cols], F32R)
        dn_raw, dn_high, dn_low = sb("dn_raw", [rows, HID], F32), sb("dn_high", [rows, HID], F32R), sb("dn_low", [rows, HID], F32R)
        acted, prod = sb("acted", [rows, CH], F32), sb("prod", [rows, CH], F32)
        h_high, h_low = sb("h_high", [rows, CH], F32R), sb("h_low", [rows, CH], F32R)
        y = [k.bank[0], k.bank[1]]
        gate, up = [k.bank[2 + i][0:rows, :] for i in range(2)], [k.bank[4 + i][0:rows, :] for i in range(2)]
        sems = lambda name: k.sems(f"{name}_{kind}")
        gu_in, dn_in = sems("gu_in"), sems("dn_in")
        gu_high_done, gu_split, dn_high_done, dn_split = sems("gu_high_done"), sems("gu_split"), sems("dn_high_done"), sems("dn_split")
        gu_done, acted_done, prod_done = sems("gu_done"), sems("acted_done"), sems("prod_done")
        h_high_done, h_split, down_done = sems("h_high_done"), sems("h_split"), sems("down_done")
        y_added = k.sem(f"y_added_{kind}")

        block = nc.Block()
        with block:
            @block.sync
            def _(sp):
                k.prime(sp, gu_high_done, gu_split, dn_high_done, dn_split, gu_done, acted_done, prod_done,
                        h_high_done, h_split, down_done, y_added)

                with sp.Fori(0, NCH) as c:
                    first, last = begin(c)
                    with sp.Fori(0, pairs) as h:
                        n = first + h
                        for b in range(2):
                            tile = 2 * h + b
                            sp.wait_ge(gu_split[b], n)
                            sp.dma_start(gu_raw[b][:], w_gu[tile]).then_inc(gu_in[b], 16)
                            sp.wait_ge(dn_split[b], n)
                            sp.dma_start(dn_raw[b][:], w_dn[tile]).then_inc(dn_in[b], 16)

            @block.gpsimd
            def _(pool):
                def gu_low_part(n, b):
                    pool.wait_ge(gu_high_done[b], n + 1)
                    nc.gpsimd.tensor_tensor(gu_low[b][:], gu_raw[b][:], gu_high[b][:].bitcast(F32),
                                            ALU.subtract).then_inc(gu_split[b], 1)

                def dn_low_part(n, b):
                    pool.wait_ge(dn_high_done[b], n + 1)
                    nc.gpsimd.tensor_tensor(dn_low[b][:], dn_raw[b][:], dn_high[b][:].bitcast(F32),
                                            ALU.subtract).then_inc(dn_split[b], 1)

                with pool.Fori(0, NCH) as c:
                    first, last = begin(c)
                    for b in range(2):
                        gu_low_part(first, b)
                    with pool.Fori(0, pairs - 1) as h:
                        for b in range(2):
                            dn_low_part(first + h, b)
                            gu_low_part(first + h + 1, b)
                    for b in range(2):
                        dn_low_part(last, b)

            @block.tensor
            def _(pe):
                def gate_up(n, b, c):
                    pe.wait_ge(gu_split[b], n + 1)
                    pe.wait_ge(prod_done[b], n)
                    cols = bass.ts(c, CH)
                    for out, at in ((gate[b], 0), (up[b], 2 * rows)):
                        for kt in range(KT):
                            w = slice(at + kt * rows, at + kt * rows + rows)
                            nc.tensor.matmul(out, gu_high[b][:, w], k.xn_high[:, kt, cols], start=kt == 0, stop=False)
                            nc.tensor.matmul(out, gu_high[b][:, w], k.xn_low[:, kt, cols], start=False, stop=False)
                            last = nc.tensor.matmul(out, gu_low[b][:, w], k.xn_high[:, kt, cols], start=False,
                                                    stop=kt == KT - 1)
                    last.then_inc(gu_done[b], 1)

                def down(n, b, start=False, final=False):
                    pe.wait_ge(dn_split[b], n + 1)
                    pe.wait_ge(h_split[b], n + 1)
                    for kt in range(KT):
                        w = slice(kt * P, kt * P + P)
                        nc.tensor.matmul(y[kt][:], dn_high[b][:, w], h_high[b][:], start=start, stop=False)
                        nc.tensor.matmul(y[kt][:], dn_high[b][:, w], h_low[b][:], start=False, stop=False)
                        last = nc.tensor.matmul(y[kt][:], dn_low[b][:, w], h_high[b][:], start=False, stop=final)
                    last.then_inc(down_done[b], 1)

                with pe.Fori(0, NCH) as c:
                    first, last = begin(c)
                    for b in range(2):
                        gate_up(first, b, c)
                    pe.wait_ge(y_added, c + C0)
                    for b in range(2):
                        gate_up(first + 1, b, c)
                        down(first, b, start=b == 0)
                    with pe.Fori(1, pairs - 1) as h:
                        for b in range(2):
                            gate_up(first + h + 1, b, c)
                            down(first + h, b)
                    for b in range(2):
                        down(last, b, final=b == 1)

            @block.scalar
            def _(act):
                def gu_high_part(n, b):
                    act.wait_ge(gu_in[b], 16 * n)
                    act.wait_ge(gu_done[b], n)
                    nc.scalar.activation(gu_high[b][:], gu_raw[b][:], ACT.Copy).then_inc(gu_high_done[b], 1)

                def dn_high_part(n, b):
                    act.wait_ge(dn_in[b], 16 * n)
                    act.wait_ge(down_done[b], n)
                    nc.scalar.activation(dn_high[b][:], dn_raw[b][:], ACT.Copy).then_inc(dn_high_done[b], 1)

                def values(n, b):
                    act.wait_ge(gu_done[b], n + 1)
                    act.wait_ge(prod_done[b], n)
                    nc.scalar.activation(acted[b][:], gate[b], func).then_inc(acted_done[b], 1)
                    dn_high_part(n, b)
                    act.wait_ge(prod_done[b], n + 1)
                    nc.scalar.activation(h_high[b][:], prod[b][:], ACT.Copy).then_inc(h_high_done[b], 1)

                with act.Fori(0, NCH) as c:
                    first, last = begin(c)
                    for b in range(2):
                        gu_high_part(first, b)
                    with act.Fori(0, pairs - 1) as h:
                        for b in range(2):
                            values(first + h, b)
                            gu_high_part(first + h + 1, b)
                    for b in range(2):
                        values(last, b)

            @block.vector
            def _(dve):
                def product(n, b):
                    dve.wait_ge(acted_done[b], n + 1)
                    dve.wait_ge(h_split[b], n)
                    nc.vector.tensor_tensor(prod[b][:], acted[b][:], up[b], ALU.mult).then_inc(prod_done[b], 1)
                    dve.wait_ge(h_high_done[b], n + 1)
                    nc.vector.tensor_tensor(h_low[b][:], prod[b][:], h_high[b][:].bitcast(F32), ALU.subtract
                                            ).then_inc(h_split[b], 1)

                with dve.Fori(0, NCH) as c:
                    first, last = begin(c)
                    with dve.Fori(0, pairs) as h:
                        product(first + h, 0)
                        product(first + h, 1)
                    dve.wait_ge(down_done[1], last + 1)
                    for kt in range(KT):
                        add = nc.vector.scalar_tensor_tensor(
                            out=k.x[:, kt, bass.ts(c, CH)], in0=y[kt][:], scalar=0.5, in1=k.x[:, kt, bass.ts(c, CH)],
                            op0=ALU.mult, op1=ALU.add)
                    add.then_inc(y_added, 1)


def experts(nc, k, tag, w_gu, w_dn):
    NB = CH // P
    run = k.again("moe")
    C0, X0 = NCH * run + 1, (NCH + 1) * run

    def first_turn(eng, c):
        return eng.value_load(k.plan[0:1, bass.ds(c + FIRST_AT, 1)], min_val=1, max_val=2 * NCH * EX)

    def last_and_number(eng, c):
        last = eng.value_load(k.plan[0:1, bass.ds(c + LAST_AT, 1)], min_val=1, max_val=2 * NCH * EX)
        number = eng.value_load(k.plan[0:1, bass.ds(c + PAIRS_AT, 1)], min_val=SHARED // MI + TOPK, max_val=EX)
        return last, number

    def expert(eng, c, h):
        return eng.value_load(k.plan[0:1, bass.ds(c * EX + h, 1)], min_val=0, max_val=EX - 1)

    with ExitStack() as ctx:
        sb = lambda name, shape, dt=F32: ctx.enter_context(nc.sbuf_tensor(f"{name}_{tag}", shape, dt))
        xc_high, xc_low = sb("xc_high", [P, KT, CH], F32R), sb("xc_low", [P, KT, CH], F32R)
        gu_raw, gu_high, gu_low = (sb(name, [P, KT, 2 * MI], dt) for name, dt in
                                   (("gu_raw", F32), ("gu_high", F32R), ("gu_low", F32R)))
        dn_raw, dn_high, dn_low = (sb(name, [ER, 2, HID], dt) for name, dt in
                                   (("dn_raw", F32), ("dn_high", F32R), ("dn_low", F32R)))
        acted, prod = sb("acted", [P, NB, MI]), sb("prod", [P, NB, MI])
        h_high, h_low = sb("h_high", [ER, 2, CH], F32R), sb("h_low", [ER, 2, CH], F32R)
        y = [k.bank[0], k.bank[1]]
        gu_ps = k.bank[2:5] + k.bank[7:8]
        h_ps = k.pair[1]
        sem = lambda name: k.sem(f"{name}_moe")
        xc_ready, gu_in, dn_in = sem("xc_ready"), sem("gu_in"), sem("dn_in")
        gu_high_done, gu_split, dn_high_done, dn_split = sem("gu_high_done"), sem("gu_split"), sem("dn_high_done"), sem("dn_split")
        gu_done, acted_done, prod_done = sem("gu_done"), sem("acted_done"), sem("prod_done")
        turned, h_high_done, h_split, down_done = sem("turned"), sem("h_high_done"), sem("h_split"), sem("down_done")
        y_added = sem("y_added")

        block = nc.Block()
        with block:
            @block.sync
            def _(sp):
                k.prime(sp, gu_high_done, gu_split, dn_high_done, dn_split, turned, h_high_done, h_split, down_done, y_added)
                k.prime(sp, gu_done, acted_done, prod_done, by=2 * NB - 1)
                def load_gate_up(n, e):
                    sp.wait_ge(gu_split, n)
                    sp.dma_start(gu_raw[:], w_gu[e]).then_inc(gu_in, 16)

                def load_down(n, e):
                    sp.wait_ge(dn_split, n)
                    sp.dma_start(dn_raw[:], w_dn[e]).then_inc(dn_in, 16)

                with sp.Fori(0, NCH) as c:
                    first = first_turn(sp, c)
                    load_gate_up(first, NE)
                    last, number = last_and_number(sp, c)
                    with sp.Fori(0, number - 1) as h:
                        load_gate_up(first + h + 1, expert(sp, c, h + 1))
                        load_down(first + h, expert(sp, c, h))
                    load_down(last, EX - 1)

            @block.gpsimd
            def _(pool):
                with pool.Fori(0, NCH) as c:
                    first = first_turn(pool, c)
                    pool.wait_ge(gu_high_done, first + 1)
                    nc.gpsimd.tensor_tensor(gu_low[:], gu_raw[:], gu_high[:].bitcast(F32), ALU.subtract).then_inc(gu_split, 1)
                    last, number = last_and_number(pool, c)
                    with pool.Fori(0, number) as h:
                        pool.wait_ge(dn_high_done, first + h + 1)
                        nc.gpsimd.tensor_tensor(dn_low[:], dn_raw[:], dn_high[:].bitcast(F32), ALU.subtract
                                                ).then_inc(dn_split, 1)

            @block.tensor
            def _(pe):
                def gate_up(n):
                    pe.wait_ge(gu_split, n + 1)
                    for i in range(NB):
                        z, out = slice(i * P, (i + 1) * P), gu_ps[i][:, 0:2 * MI]
                        pe.wait_ge(prod_done, n * NB + i)
                        for kt in range(KT):
                            nc.tensor.matmul(out, xc_high[:, kt, z], gu_high[:, kt], start=kt == 0, stop=False)
                            nc.tensor.matmul(out, xc_high[:, kt, z], gu_low[:, kt], start=False, stop=False)
                            last = nc.tensor.matmul(out, xc_low[:, kt, z], gu_high[:, kt], start=False, stop=kt == KT - 1)
                        last.then_inc(gu_done, 1)

                def turn(n):
                    pe.wait_ge(h_split, n)
                    for i in range(NB):
                        pe.wait_ge(prod_done, n * NB + NB + i)
                        for half in range(2):
                            last = nc.tensor.transpose(h_ps[0:ER, half, i * P:(i + 1) * P],
                                                       prod[:, i, half * ER:(half + 1) * ER], k.ident[:])
                    last.then_inc(turned, 1)

                def down(n, start=False, final=False):
                    pe.wait_ge(dn_split, n + 1)
                    pe.wait_ge(h_split, n + 1)
                    for half in range(2):
                        s, f = start and half == 0, final and half == 1
                        for kt in range(KT):
                            w = slice(kt * P, kt * P + P)
                            nc.tensor.matmul(y[kt][:], dn_high[:, half, w], h_high[:, half], start=s, stop=False)
                            nc.tensor.matmul(y[kt][:], dn_high[:, half, w], h_low[:, half], start=False, stop=False)
                            last = nc.tensor.matmul(y[kt][:], dn_low[:, half, w], h_high[:, half], start=False, stop=f)
                    last.then_inc(down_done, 1)

                with pe.Fori(0, NCH) as c:
                    first = first_turn(pe, c)
                    pe.wait_ge(xc_ready, c + X0 + 1)
                    gate_up(first)
                    last, number = last_and_number(pe, c)
                    turn(first)
                    gate_up(first + 1)
                    pe.wait_ge(y_added, c + C0)
                    down(first, start=True)
                    turn(first + 1)
                    with pe.Fori(1, number - 1) as h:
                        gate_up(first + h + 1)
                        down(first + h)
                        turn(first + h + 1)
                    down(last, final=True)

            @block.scalar
            def _(act):
                def gu_high_part(n):
                    act.wait_ge(gu_in, 16 * n)
                    act.wait_ge(gu_done, n * NB + NB - 1)
                    nc.scalar.activation(gu_high[:], gu_raw[:], ACT.Copy).then_inc(gu_high_done, 1)

                def gates(n):
                    for i in range(NB):
                        act.wait_ge(gu_done, n * NB + NB + i)
                        act.wait_ge(prod_done, n * NB + i)
                        nc.scalar.activation(acted[:, i], gu_ps[i][:, 0:MI], ACT.Silu).then_inc(acted_done, 1)

                def down_parts(n):
                    act.wait_ge(dn_in, 16 * n)
                    act.wait_ge(down_done, n)
                    nc.scalar.activation(dn_high[:], dn_raw[:], ACT.Copy).then_inc(dn_high_done, 1)
                    act.wait_ge(turned, n + 1)
                    nc.scalar.activation(h_high[:], h_ps[0:ER], ACT.Copy).then_inc(h_high_done, 1)

                with act.Fori(0, NCH) as c:
                    first = first_turn(act, c)
                    gu_high_part(first)
                    last, number = last_and_number(act, c)
                    with act.Fori(0, number - 1) as h:
                        gates(first + h)
                        gu_high_part(first + h + 1)
                        down_parts(first + h)
                    gates(last)
                    down_parts(last)

            @block.vector
            def _(dve):
                def gu_low_part(n):
                    dve.wait_ge(gu_high_done, n + 1)
                    nc.vector.tensor_tensor(gu_low[:], gu_raw[:], gu_high[:].bitcast(F32), ALU.subtract).then_inc(gu_split, 1)

                def products(n, c, h):
                    e = expert(dve, c, h)
                    dve.wait_ge(turned, n)
                    for i in range(NB):
                        dve.wait_ge(acted_done, n * NB + NB + i)
                        nc.vector.scalar_tensor_tensor(
                            out=prod[:, i], in0=acted[:, i], scalar=k.weights[:, bass.ds(c * (NB * EX) + e + i * EX, 1)],
                            in1=gu_ps[i][:, MI:2 * MI], op0=ALU.mult, op1=ALU.mult).then_inc(prod_done, 1)

                def h_low_part(n):
                    dve.wait_ge(h_high_done, n + 1)
                    nc.vector.tensor_tensor(h_low[:], h_ps[0:ER], h_high[:].bitcast(F32), ALU.subtract).then_inc(h_split, 1)

                def take_chunk(c):
                    cols = bass.ts(c, CH)
                    nc.vector.tensor_copy(xc_high[:], k.xn_high[:, :, cols])
                    nc.vector.tensor_copy(xc_low[:], k.xn_low[:, :, cols]).then_inc(xc_ready, 1)

                take_chunk(0)
                with dve.Fori(0, NCH) as c:
                    first = first_turn(dve, c)
                    last, number = last_and_number(dve, c)
                    with dve.Fori(0, number - 1) as h:
                        products(first + h, c, h)
                        gu_low_part(first + h + 1)
                        h_low_part(first + h)
                    products(last, c, number - 1)
                    take_chunk((c + 1) & (NCH - 1))
                    h_low_part(last)
                    dve.wait_ge(down_done, last + 1)
                    for kt in range(KT):
                        add = nc.vector.scalar_tensor_tensor(
                            out=k.x[:, kt, bass.ts(c, CH)], in0=y[kt][:], scalar=0.5, in1=k.x[:, kt, bass.ts(c, CH)],
                            op0=ALU.mult, op1=ALU.add)
                    add.then_inc(y_added, 1)


def route(nc, k, tag, w_router, bias, plan_consts):
    NT = TOK // P
    with ExitStack() as ctx:
        sb = lambda name, shape, dt=F32: ctx.enter_context(nc.sbuf_tensor(f"{name}_{tag}", shape, dt))
        w_raw, w_high, w_low = sb("rw_raw", [P, KT, NE]), sb("rw_high", [P, KT, NE], F32R), sb("rw_low", [P, KT, NE], F32R)
        bias_row = sb("bias_row", [P, NE])
        half_tanh = sb("half_tanh", [NE, TOK])
        consts = sb("plan_consts", [EX, 3 * EX + 3])
        before, ones, place_no = consts[:, 0:EX], consts[:, EX:2 * EX], consts[:, 2 * EX:3 * EX]
        number, is_last, no_place = (consts[:, 3 * EX + i:3 * EX + i + 1] for i in range(3))
        active, place, last_place = sb("active", [EX, NCH]), sb("place", [EX, NCH]), sb("last_place", [EX, NCH])
        at_place = sb("at_place", [EX, NCH, EX])
        plan = sb("plan_row", [1, PLAN])
        score, sfc, masked = sb("score", [P, NT, NE]), sb("sfc", [P, NT, NE]), sb("masked", [P, NT, NE])
        weight = k.weights[:].rearrange("p (t e) -> p t e", e=EX)
        best2 = sb("best2", [P, NT, NG])
        pair_a, pair_b = sb("pair_a", [P, NT, NG, 2]), sb("pair_b", [P, NT, NG, 2])
        keep = sb("keep", [P, NT, NG])
        chosen = sb("chosen", [P, NT, NE])
        top8 = sb("top8", [P, NT, 8])
        above, equal = sb("above", [P, NT, NE]), sb("equal", [P, NT, NE])
        count = sb("count", [P, NT])
        PAD = 16
        run = [sb(f"run{i}", [P, NT, PAD + NE]) for i in range(2)]
        w_in, bias_in = k.sem("rw_in"), k.sem("rbias_in")
        step, tanh_done, logits_done = k.sem("rstep"), k.sem("tanh_done"), k.sem("logits_done")
        w_ready, turned, weight_done = k.sem("rw_ready"), k.sem("rturned"), k.sem("rweight")
        back = k.sem("rback")
        placed, one_hot, listed, plan_done = k.sem("placed"), k.sem("one_hot"), k.sem("listed"), k.sem("plan_done")
        R = k.again("route")
        chunk = lambda c: slice(c * CH, (c + 1) * CH)
        logit_bank = [k.bank[c] for c in range(NCH)]
        turn_bank = k.bank[4]
        block = nc.Block()
        with block:
            @block.sync
            def _(sp):
                sp.dma_start(w_raw[:], w_router).then_inc(w_in, 16)
                sp.dma_start(bias_row[:], bias.to_broadcast([P, NE])).then_inc(bias_in, 16)
                sp.dma_start(consts[:], plan_consts).then_inc(bias_in, 16)

            @block.tensor
            def _(pe):
                pe.wait_ge(w_ready, 2 * R + 2)
                for c in range(NCH):
                    for kt in range(KT):
                        out = logit_bank[c][0:NE, :]
                        nc.tensor.matmul(out, w_high[:, kt], k.xn_high[:, kt, chunk(c)], start=kt == 0, stop=False)
                        nc.tensor.matmul(out, w_high[:, kt], k.xn_low[:, kt, chunk(c)], start=False, stop=False)
                        last = nc.tensor.matmul(out, w_low[:, kt], k.xn_high[:, kt, chunk(c)], start=False, stop=kt == KT - 1)
                    last.then_inc(logits_done, 1)
                for c in range(NCH):
                    pe.wait_ge(tanh_done, NCH * R + c + 1)
                    for t in range(4 * c, 4 * c + 4):
                        last = nc.tensor.transpose(turn_bank[:, t * NE:(t + 1) * NE], half_tanh[:, t * P:(t + 1) * P],
                                                   k.ident[0:NE, 0:NE])
                last.then_inc(turned, 1)
                pe.wait_ge(weight_done, R + 1)
                for c in range(NCH):
                    for t in range(4 * c, 4 * c + 4):
                        last = nc.tensor.transpose(logit_bank[c][0:NE, t % 4 * P:t % 4 * P + P], weight[:, t, 0:NE], k.ident[:])
                    last.then_inc(back, 1)

                pe.wait_ge(placed, R + 1)
                nc.tensor.matmul(turn_bank[0:EX, 0:NCH], before, active[:], start=True, stop=True)
                nc.tensor.matmul(turn_bank[0:EX, NCH:2 * NCH], ones, active[:], start=True, stop=True
                                 ).then_inc(listed, 1)
                pe.wait_ge(one_hot, R + 1)
                nc.tensor.matmul(turn_bank[0:1, 0:NCH * EX], number, at_place[:].rearrange("e c j -> e (c j)"),
                                 start=True, stop=True).then_inc(listed, 1)

            @block.scalar
            def _(act):
                for c in range(NCH):
                    act.wait_ge(logits_done, NCH * R + c + 1)
                    nc.scalar.activation(half_tanh[:, chunk(c)], logit_bank[c][0:NE, :], ACT.Tanh, scale=0.5
                                         ).then_inc(tanh_done, 1)

            @block.vector
            def _(dve):
                steps = [k.route_steps]

                def link(ins):
                    steps[0] += 1
                    ins.then_inc(step, 1)
                    dve.wait_ge(step, steps[0])

                def tt(out, a, b, op):
                    return nc.vector.tensor_tensor(out, a, b, op)

                def choose(mask, values, n, many):
                    for t in range(NT):
                        last = nc.vector.max(top8[:, t], values[:, t])
                    link(last)
                    least = top8[:, :, many - 1:many].to_broadcast([P, NT, n])
                    a, e = above[:, :, 0:n], equal[:, :, 0:n]
                    tt(a, values, least, ALU.is_gt)
                    tt(e, values, least, ALU.is_equal)
                    link(tt(run[0][:, :, PAD:PAD + n], values, least, ALU.is_equal))
                    link(nc.vector.tensor_reduce(count[:], a, AX_X, ALU.add))
                    at, by = 0, 1
                    while by < n:
                        link(tt(run[1 - at][:, :, PAD:PAD + n], run[at][:, :, PAD:PAD + n],
                                run[at][:, :, PAD - by:PAD - by + n], ALU.add))
                        at, by = 1 - at, 2 * by
                    ran = run[at][:, :, PAD:PAD + n]
                    link(tt(ran, ran, count[:].unsqueeze(2).to_broadcast([P, NT, n]), ALU.add))
                    link(nc.vector.scalar_tensor_tensor(out=e, in0=ran, scalar=float(many), in1=e,
                                                        op0=ALU.is_le, op1=ALU.mult))
                    link(tt(mask, a, e, ALU.add))

                nc.vector.memset(weight[:, :, NE:EX], 1.0)
                nc.vector.memset(active[:], 0.0)
                nc.vector.memset(run[0][:], 0.0)
                link(nc.vector.memset(run[1][:], 0.0))
                dve.wait_ge(w_in, 16 * R + 16)
                nc.vector.tensor_copy(w_high[:], w_raw[:]).then_inc(w_ready, 1)
                dve.wait_ge(w_ready, 2 * R + 1)
                nc.vector.tensor_tensor(w_low[:], w_raw[:], w_high[:].bitcast(F32), ALU.subtract).then_inc(w_ready, 1)
                dve.wait_ge(turned, R + 1)
                link(nc.vector.tensor_scalar(score[:].rearrange("p t e -> p (t e)"), turn_bank[:], 0.5, 0.5,
                                             ALU.mult, ALU.add))
                dve.wait_ge(bias_in, 32 * R + 32)
                link(tt(sfc[:], score[:], bias_row[:].unsqueeze(1).to_broadcast([P, NT, NE]), ALU.add))
                quad = sfc[:].rearrange("p t (g x y) -> p (t g) x y", x=2, y=2)
                a, b = quad[:, :, :, 0], quad[:, :, :, 1]
                sums, maxs = [z[:].rearrange("p t g x -> p (t g) x") for z in (pair_a, pair_b)]
                best = best2[:].rearrange("p t g -> p (t g)")
                tt(sums, a, b, ALU.add)
                link(tt(maxs, a, b, ALU.max))
                link(tt(best, maxs[:, :, 0], maxs[:, :, 1], ALU.add))
                link(tt(best, best, sums[:, :, 0], ALU.max))
                link(tt(best, best, sums[:, :, 1], ALU.max))
                choose(keep[:], best2[:], NG, TOPG)
                kept = keep[:].rearrange("p t g -> p (t g)").unsqueeze(2).to_broadcast([P, NT * NG, NE // NG])
                m4 = masked[:].rearrange("p t (g x) -> p (t g) x", x=NE // NG)
                s4 = sfc[:].rearrange("p t (g x) -> p (t g) x", x=NE // NG)
                link(tt(m4, s4, kept, ALU.mult))
                link(nc.vector.tensor_scalar(keep[:], keep[:], BIG, -BIG, ALU.mult, ALU.add))
                link(tt(m4, m4, kept, ALU.add))
                choose(chosen[:], masked[:], NE, TOPK)
                tt(weight[:, :, 0:NE], chosen[:], score[:], ALU.mult).then_inc(weight_done, 1)
                for c in range(NCH):
                    dve.wait_ge(back, NCH * R + c + 1)
                    last = nc.vector.tensor_reduce(active[0:NE, c:c + 1], logit_bank[c][0:NE, :], AX_X, ALU.max)
                link(last)
                nc.vector.tensor_scalar(active[0:NE, :], active[0:NE, :], 0.0, None, ALU.is_gt).then_inc(placed, 1)
                dve.wait_ge(listed, 2 * R + 1)
                numbers = turn_bank[0:EX, NCH:2 * NCH]
                link(nc.vector.scalar_tensor_tensor(out=place[:], in0=turn_bank[0:EX, 0:NCH], scalar=1.0 - NO_PLACE,
                                                    in1=active[:], op0=ALU.add, op1=ALU.mult))
                link(nc.vector.tensor_scalar(last_place[:], numbers, 1.0, is_last, ALU.add, ALU.mult))
                link(tt(place[:], place[:], last_place[:], ALU.add))
                link(nc.vector.tensor_scalar(place[:], place[:], no_place, None, ALU.add))
                link(nc.vector.tensor_scalar(plan[:, PAIRS_AT:PAIRS_AT + NCH], numbers[0:1, :], 2.0, None, ALU.add))
                link(nc.vector.tensor_copy(plan[:, FIRST_AT:FIRST_AT + 1], k.turns_run[:]))
                for c in range(NCH):
                    link(tt(plan[:, FIRST_AT + c + 1:FIRST_AT + c + 2], plan[:, FIRST_AT + c:FIRST_AT + c + 1],
                            plan[:, PAIRS_AT + c:PAIRS_AT + c + 1], ALU.add))
                nc.vector.tensor_scalar(plan[:, LAST_AT:LAST_AT + NCH], plan[:, FIRST_AT + 1:FIRST_AT + NCH + 1], -1.0, None,
                                        ALU.add)
                nc.vector.tensor_copy(k.turns_run[:], plan[:, FIRST_AT + NCH:FIRST_AT + NCH + 1])
                tt(at_place[:], place_no.unsqueeze(1).to_broadcast([EX, NCH, EX]),
                   place[:].unsqueeze(2).to_broadcast([EX, NCH, EX]), ALU.is_equal).then_inc(one_hot, 1)
                dve.wait_ge(listed, 2 * R + 2)
                link(nc.vector.tensor_copy(plan[:, 0:NCH * EX], turn_bank[0:1, 0:NCH * EX]))
                nc.vector.tensor_copy(k.plan[:], plan[:]).then_inc(plan_done, 1)
                dve.wait_ge(plan_done, R + 1)
                k.route_steps = steps[0]


def attention(nc, k, tag, a, mix):
    MH = HEADS // 2
    run = k.again("attention")
    C0, X0 = NCH * run, (NCH + 1) * run
    turn = lambda c, m: 1 + (c + C0) * MH + m
    own = lambda c, m: 1 + c * MH + m
    with ExitStack() as ctx:
        one = lambda name, shape, dt=F32: ctx.enter_context(nc.sbuf_tensor(f"{name}_{tag}", shape, dt))
        two = lambda name, shape, dt=F32: [one(f"{name}{i}", shape, dt) for i in range(2)]
        SEEN = (SEQ, SEQ) if mix else (P, SEQ)
        AT, WIDE = (0, SEEN[0]), sum(SEEN)
        Q0, J_AT = ((0, 0), (0, SEQ)) if mix else ((0, P), (0, SEQ))
        xc_high, xc_low = one("xc_high", [P, KT, CH], F32R), one("xc_low", [P, KT, CH], F32R)
        mask = one("mask", [P, WIDE])
        probs = two("probs", [P, 2, WIDE])
        oT_high, oT_low = two("oT_high", [P, CH], F32R), two("oT_low", [P, CH], F32R)
        minus_peak, total, inverse = [two(name, [P, 2, 2]) for name in ("minus_peak", "total", "inverse")]
        w_out, wo_high, wo_low = two("w_out", [P, HID]), two("wo_high", [P, HID], F32R), two("wo_low", [P, HID], F32R)
        if mix:
            q_all, k_all = one("q_all", [P, HEADS, CH]), one("k_all", [P, HEADS, CH])
            qT, kT = two("qT", [P, CH]), two("kT", [P, CH])
            vs = one("vs", [P, 2, 2, 2 * D])
            w_in, wi_high, wi_low = ([one(name, [P, 2 * HID], dt)] for name, dt in
                                     (("w_in", F32), ("wi_high", F32R), ("wi_low", F32R)))
            pT = two("pT", [P, 2, WIDE])
            w_qk, qk_high, qk_low = two("w_qk", [P, 2 * HID]), two("qk_high", [P, 2 * HID], F32R), two("qk_low", [P, 2 * HID], F32R)
            vec = one("vec", [P, 5, HEADS])
            shifts = one("shifts", [P, 1 + len(CHANNEL_SHIFTS), P])
            w_mix = one("w_mix", [P, 1 + len(CHANNEL_SHIFTS)])
            circ = one("circ", [P, P])
            circ_g = two("circ_g", [P, P])
            sq_q, sq_k = two("sq_q", [P, CH]), two("sq_k", [P, CH])
            acc = one("acc", [P, 2, CH])
            rms, inverse_rms = one("rms", [P, 2 * CH // P]), one("inverse_rms", [P, 2 * CH // P])
            diag = acc
            inv_rms = one("inv_rms", [P, 2, CH])
            eps6, b_out = one("eps6", [P, 1]), one("b_out", [P, KT])
        else:
            w_in, wi_high, wi_low = two("w_in", [P, HID]), two("wi_high", [P, HID], F32R), two("wi_low", [P, HID], F32R)
            qT_high, qT_low = two("qT_high", [P, CH], F32R), two("qT_low", [P, CH], F32R)
            pT_high, pT_low = two("pT_high", [P, 2, WIDE], F32R), two("pT_low", [P, 2, WIDE], F32R)
            vs = two("vs", [P, 4, 2, D], F32R)
            w_kv = one("w_kv", [P, 2, KT, GROUPS * D])
            kv_high, kv_low = one("kv_high", [P, 2, KT, GROUPS * D], F32R), one("kv_low", [P, 2, KT, GROUPS * D], F32R)
            k_high, k_low = one("k_high", [P, GROUPS, CH], F32R), one("k_low", [P, GROUPS, CH], F32R)
            v_all = one("v_all", [P, 4, 2, GROUPS * D], F32R)
        y = [k.bank[0], k.bank[1]]
        proj, ctx_bank = k.bank[2], k.bank[7]
        s_ps, t_ps = k.pair[0], k.pair[1]
        n = lambda s: f"{s}_near_" if mix else f"{s}_gqa_"
        xc_ready, const_in, setup = k.sem("attn_xc_ready"), k.sem(n("const_in")), k.sem(n("setup"))
        xc_high_done = k.sem("attn_xc_high")
        head_in, wo_in = k.sems(n("head_in")), k.sems("wo_in")
        in_high_done, in_split = k.sems(n("in_high")), k.sems(n("in_split"))
        wo_high_done, wo_split, o_high_done = k.sems("attn_wo_high"), k.sems("attn_wo_split"), k.sems("attn_o_high")
        q_proj, q_ready, k_ready = k.sems("attn_q_proj"), k.sems("attn_q_ready"), k.sems(n("k_ready"))
        v_proj, v_ready = k.sems(n("v_proj")), k.sems("attn_v_ready")
        scored, masked, peaked = k.sems("attn_scored"), k.sems("attn_masked"), k.sems("attn_peaked")
        exped, inverted, normed = k.sems("attn_exped"), k.sems("attn_inverted"), k.sems("attn_normed")
        turned, pt_ready, ctx_done, o_ready, y_done = (k.sems("attn_turned"), k.sems("attn_pt_ready"), k.sems("attn_ctx_done"),
                                                       k.sems("attn_o_ready"), k.sems("attn_y_done"))
        y_added = k.sem("attn_y_added")
        if mix:
            qk_in, qk_proj, qk_biased = k.sems(n("qk_in")), k.sems(n("qk_proj")), k.sems(n("qk_biased"))
            summed, qk_high_done, qk_split = k.sems(n("summed")), k.sems(n("qk_high")), k.sems(n("qk_split"))
            acc_zero, sums_done, rms_done, inv_done = k.sem(n("acc_zero")), k.sem(n("sums_done")), k.sem(n("rms_done")), k.sem(n("inv_done"))
            inverse_done, diag_done, inv_spread = k.sem(n("inverse_done")), k.sem(n("diag_done")), k.sem(n("inv_spread"))
            circ_ready = k.sems(n("circ_ready"))
        else:
            kv_proj, kv_high_done, kv_ready = k.sem(n("kv_proj")), k.sem(n("kv_high")), k.sem(n("kv_ready"))
            q_high_done, pt_high_done = k.sems(n("q_high")), k.sems(n("pt_high"))

        def before(sems, b, t):
            return (sems[1], t) if b == 0 else (sems[0], t + 1)

        def product(out, w, w_low, z, z_low, start=True, stop=True):
            nc.tensor.matmul(out, w, z, start=start, stop=False)
            nc.tensor.matmul(out, w, z_low, start=False, stop=False)
            return nc.tensor.matmul(out, w_low, z, start=False, stop=stop)

        def steps(eng, c, step):
            step(0, 0, True, 0)
            step(0, 1, False, 0)
            with eng.Fori(1, MH - 1) as m:
                step(m, 0, False, 0)
                step(m, 1, False, 0)
            step(MH - 1, 0, False, 1)
            step(MH - 1, 1, False, 2)

        block = nc.Block()
        with block:
            @block.sync
            def _(sp):
                k.prime(sp, q_proj, q_ready, v_ready, scored, masked, peaked, exped, inverted, normed, turned,
                        pt_ready, ctx_done, o_ready, y_done, y_added, v_proj, k_ready, in_high_done, in_split,
                        wo_high_done, wo_split, o_high_done)
                if mix:
                    k.prime(sp, qk_proj, qk_biased, summed, circ_ready, qk_high_done, qk_split)
                else:
                    k.prime(sp, q_high_done, pt_high_done)
                sp.dma_start(mask[:], a["near_mask" if mix else "causal_mask"]).then_inc(const_in, 16)
                if mix:
                    sp.dma_start(vec[:], a["attn1_vec"]).then_inc(const_in, 16)
                    sp.dma_start(b_out[:], a["attn1_bo"]).then_inc(const_in, 16)
                    sp.dma_start(shifts[:], a["shift_mats"]).then_inc(const_in, 16)
                    sp.dma_start(w_mix[:], a["w_mix"].to_broadcast([P, 1 + len(CHANNEL_SHIFTS)])).then_inc(const_in, 16)
                else:
                    sp.dma_start(w_kv[:], a["attn0_kv"]).then_inc(const_in, 16)

                def load_in(c, m, b):
                    sp.wait_ge(in_split[b], own(c, m))
                    sp.dma_start(w_in[b][:], a["attn1_v"][m] if mix else a["attn0_q"][2 * m + b]
                                 ).then_inc(head_in[b], 16)

                def load_out(c, m):
                    for b in range(2):
                        sp.wait_ge(wo_split[b], turn(c, m))
                        sp.dma_start(w_out[b][:], a["attn1_o" if mix else "attn0_o"][2 * m + b]).then_inc(wo_in[b], 16)

                if not mix:
                    load_in(0, 0, 0)
                    load_in(0, 0, 1)
                with sp.Fori(0, NCH) as c:
                    if mix:
                        with sp.Fori(0, MH) as m:
                            for b in range(2):
                                sp.wait_ge(qk_split[b], own(c, m))
                                sp.dma_start(w_qk[b][:], a["attn1_qk"][2 * m + b]).then_inc(qk_in[b], 16)
                    if mix:
                        load_in(c, 0, 0)
                        with sp.Fori(1, MH) as m:
                            load_in(c, m, 0)
                            load_out(c, m - 1)
                        load_out(c, MH - 1)
                    else:
                        load_in(c, 1, 0)
                        with sp.Fori(0, MH - 1) as m:
                            load_in(c, m + 1, 1)
                            load_in(c, m + 2, 0)
                            load_out(c, m)
                        load_in(c, MH, 1)
                        load_out(c, MH - 1)

            @block.gpsimd
            def _(pool):
                def low_part(done, low, raw, high):
                    nc.gpsimd.tensor_tensor(low, raw, high.bitcast(F32), ALU.subtract).then_inc(done, 1)

                def qk_low_part(c, m, b):
                    pool.wait_ge(qk_high_done[b], own(c, m) + 1)
                    low_part(qk_split[b], qk_low[b][:], w_qk[b][:], qk_high[b][:])

                def in_low_part(c, m, b):
                    pool.wait_ge(in_high_done[b], own(c, m) + 1)
                    low_part(in_split[b], wi_low[b][:], w_in[b][:], wi_high[b][:])

                def out_low_part(c, m, b):
                    pool.wait_ge(wo_high_done[b], turn(c, m) + 1)
                    low_part(wo_split[b], wo_low[b][:], w_out[b][:], wo_high[b][:])

                def chunk_low_part(c, count):
                    pool.wait_ge(xc_high_done, count)
                    low_part(xc_ready, xc_low[:], k.xn[:, :, bass.ts(c, CH)], xc_high[:])

                chunk_low_part(0, X0 + 1)
                if not mix:
                    in_low_part(0, 0, 0)
                    in_low_part(0, 0, 1)
                with pool.Fori(0, NCH) as c:
                    if not mix:
                        in_low_part(c, 1, 0)
                    if mix:
                        with pool.Fori(0, MH) as m:
                            qk_low_part(c, m, 0)
                            qk_low_part(c, m, 1)
                        in_low_part(c, 0, 0)

                    def step(m, b, first, last):
                        if not mix and last < 2:
                            in_low_part(c, m + 1 + b, 1 - b)
                        if last == 0 and mix and b == 1:
                            in_low_part(c, m + 1, 0)
                        out_low_part(c, m, b)
                        if last == 1:
                            chunk_low_part((c + 1) & (NCH - 1), c + X0 + 2)

                    steps(pool, c, step)

            @block.tensor
            def _(pe):
                def query_key(c, m, b):
                    t = turn(c, m)
                    pe.wait_ge(xc_ready, c + X0 + 1)
                    pe.wait_ge(qk_split[b], own(c, m) + 1)
                    pe.wait_ge(qk_biased[b], own(c, m))
                    for out, at in ((s_ps[:, b], 0), (t_ps[:, b], HID)):
                        for kt in range(KT):
                            w = slice(at + kt * P, at + kt * P + P)
                            last = product(out, qk_high[b][:, w], qk_low[b][:, w], xc_high[:, kt], xc_low[:, kt],
                                           kt == 0, kt == KT - 1)
                    last.then_inc(qk_proj[b], 1)

                def queries(c, m, b):
                    t = turn(c, m)
                    pe.wait_ge(*before(q_ready, b, t))
                    if mix:
                        pe.wait_ge(v_ready[1], t)
                        pe.wait_ge(circ_ready[b], own(c, m) + 1)
                        last = nc.tensor.matmul(proj[:], circ_g[b][:], q_all[:, 2 * m + b], start=True, stop=True)
                    else:
                        pe.wait_ge(in_split[b], own(c, m) + 1)
                        for kt in range(KT):
                            w = slice(kt * P, kt * P + P)
                            last = product(proj[:], wi_high[b][:, w], wi_low[b][:, w], xc_high[:, kt], xc_low[:, kt],
                                           kt == 0, kt == KT - 1)
                    last.then_inc(q_proj[b], 1)

                def values(c, m, b, bank):
                    t = turn(c, m)
                    pe.wait_ge(in_split[0], own(c, m) + 1)
                    if bank is proj:
                        pe.wait_ge(q_ready[1], t + 1)
                    pe.wait_ge(v_ready[0], t + b)
                    pe.wait_ge(v_ready[1], t)
                    for i in range(2):
                        for kt in range(KT):
                            z, w = slice((2 * b + i) * P, (2 * b + i + 1) * P), slice(kt * 2 * D, (kt + 1) * 2 * D)
                            last = product(bank[:, i * 2 * D:(i + 1) * 2 * D], xc_high[:, kt, z], xc_low[:, kt, z],
                                           wi_high[0][:, w], wi_low[0][:, w], kt == 0, kt == KT - 1)
                    last.then_inc(v_proj[b], 1)

                def scores(c, m, b):
                    t = turn(c, m)
                    pe.wait_ge(q_ready[b], t + 1)
                    if mix:
                        pe.wait_ge(k_ready[b], own(c, m) + 1)
                    pe.wait_ge(*before(masked, b, t))
                    for s in range(2):
                        for i in range(2):
                            q, keys = slice(s * SEQ + i * P, s * SEQ + i * P + P), slice(s * SEQ, s * SEQ + SEEN[i])
                            out = s_ps[:, s, AT[i]:AT[i] + SEEN[i]]
                            if mix:
                                last = nc.tensor.matmul(out, qT[b][:, q], kT[b][:, keys], start=True, stop=True)
                            else:
                                last = product(out, qT_high[b][:, q], qT_low[b][:, q],
                                               k_high[:, m // 2, keys], k_low[:, m // 2, keys])
                    last.then_inc(scored[b], 1)

                def turn_probs(c, m, b):
                    t = turn(c, m)
                    pe.wait_ge(normed[b], t + 1)
                    pe.wait_ge(*before(pt_ready, b, t))
                    for s in range(2):
                        for j in range(2):
                            for q in range(Q0[j], SEQ, P):
                                to, key = J_AT[j] + q - Q0[j], AT[q // P] + j * P
                                last = nc.tensor.transpose(t_ps[:, s, to:to + P], probs[b][:, s, key:key + P], k.ident[:])
                    last.then_inc(turned[b], 1)

                def context(c, m, b):
                    t = turn(c, m)
                    pe.wait_ge(pt_ready[b], t + 1)
                    pe.wait_ge(v_ready[0 if mix else b], t + 1)
                    if mix:
                        pe.wait_ge(v_ready[1], t + 1)
                    pe.wait_ge(*before(o_ready, b, t))
                    for s in range(2):
                        for j in range(2):
                            out = ctx_bank[:, s * SEQ + Q0[j]:(s + 1) * SEQ]
                            z = slice(J_AT[j], J_AT[j] + SEQ - Q0[j])
                            if mix:
                                last = nc.tensor.matmul(out, vs[:, s, j, b * D:(b + 1) * D], pT[b][:, s, z], start=j == 0, stop=j == 1)
                            else:
                                last = product(out, vs[b][:, 2 * s + j, 0], vs[b][:, 2 * s + j, 1],
                                               pT_high[b][:, s, z], pT_low[b][:, s, z], j == 0, j == 1)
                    last.then_inc(ctx_done[b], 1)

                def project_out(c, m, b, first, final):
                    t = turn(c, m)
                    if first:
                        pe.wait_ge(y_added, c + C0 + 1)
                    pe.wait_ge(wo_split[b], t + 1)
                    pe.wait_ge(o_ready[b], t + 1)
                    for kt in range(KT):
                        w = slice(kt * P, kt * P + P)
                        last = product(y[kt][:], wo_high[b][:, w], wo_low[b][:, w], oT_high[b][:], oT_low[b][:], first, final)
                    last.then_inc(y_done[b], 1)

                pe.wait_ge(setup, 2)
                with pe.Fori(0, NCH) as c:
                    if mix:
                        with pe.Fori(0, MH) as m:
                            query_key(c, m, 0)
                            query_key(c, m, 1)
                        pe.wait_ge(summed[1], own(c, MH - 1) + 1)
                        for t in range(2 * CH // P):
                            last = nc.tensor.matmul(s_ps[:, 0, t:t + 1], acc[:, t // 4, t % 4 * P:(t % 4 + 1) * P],
                                                    k.mean_mat[:, 0:1], start=True, stop=True)
                        last.then_inc(sums_done, 1)
                        pe.wait_ge(diag_done, c + 1)
                        for i in range(2):
                            last = nc.tensor.matmul(t_ps[:, i], k.mean_mat[:], diag[:, i], start=True, stop=True)
                        last.then_inc(inv_spread, 1)
                    else:
                        pe.wait_ge(xc_ready, c + X0 + 1)
                        def project_kv(i):
                            bank = t_ps[:, i % 2]
                            if i >= 2:
                                pe.wait_ge(kv_ready, c * 8 + i - 1)
                            for kt in range(KT):
                                if i < GROUPS:
                                    g = slice(i * D, (i + 1) * D)
                                    last = product(bank, kv_high[:, 0, kt, g], kv_low[:, 0, kt, g],
                                                   xc_high[:, kt], xc_low[:, kt], kt == 0, kt == KT - 1)
                                else:
                                    z = slice((i - 4) * P, (i - 3) * P)
                                    last = product(bank, xc_high[:, kt, z], xc_low[:, kt, z],
                                                   kv_high[:, 1, kt], kv_low[:, 1, kt], kt == 0, kt == KT - 1)
                            last.then_inc(kv_proj, 1)

                        project_kv(0)
                    queries(c, 0, 0)
                    if mix:
                        values(c, 0, 0, ctx_bank)
                        queries(c, 0, 1)
                    else:
                        project_kv(1)
                        pe.wait_ge(kv_ready, c * 8 + 1)
                    scores(c, 0, 0)
                    if not mix:
                        queries(c, 0, 1)
                        for i in range(2, 8):
                            project_kv(i)
                        pe.wait_ge(kv_ready, c * 8 + 8)

                    def step(m, b, first, last):
                        nxt = (m, 1) if b == 0 else (m + 1, 0)
                        if last < 2:
                            scores(c, *nxt)
                        if mix and b == 0:
                            values(c, m, 1, proj)
                        if not mix and last == 0:
                            queries(c, m + 1, b)
                        turn_probs(c, m, b)
                        if not first:
                            prev = (m, 0) if b == 1 else (m - 1, 1)
                            project_out(c, *prev, first=isinstance(m, int) and m == 0, final=False)
                        if mix and last == 0:
                            queries(c, m + 1, b)
                        context(c, m, b)
                        if mix and b == 1 and last == 0:
                            values(c, m + 1, 0, proj)

                    steps(pe, c, step)
                    project_out(c, MH - 1, 1, first=False, final=True)

            @block.scalar
            def _(act):
                def bias_qk(c, m, b):
                    t = turn(c, m)
                    act.wait_ge(qk_proj[b], own(c, m) + 1)
                    act.wait_ge(summed[b], own(c, m))
                    h = 2 * m + b
                    nc.scalar.activation(q_all[:, h], s_ps[:, b], ACT.Identity, bias=vec[:, 0, bass.ds(h, 1)])
                    nc.scalar.activation(k_all[:, h], t_ps[:, b], ACT.Identity, bias=vec[:, 1, bass.ds(h, 1)])
                    nc.scalar.activation(sq_q[b][:], s_ps[:, b], ACT.Square, bias=vec[:, 0, bass.ds(h, 1)])
                    nc.scalar.activation(sq_k[b][:], t_ps[:, b], ACT.Square, bias=vec[:, 1, bass.ds(h, 1)]
                                         ).then_inc(qk_biased[b], 1)

                def take_queries(c, m, b):
                    t = turn(c, m)
                    if mix:
                        act.wait_ge(q_proj[b], t)
                        h = 2 * m + b
                        nc.scalar.activation(circ_g[b][:], circ[:], ACT.Copy, scale=vec[:, 3, bass.ds(h, 1)]
                                             ).then_inc(circ_ready[b], 1)
                    else:
                        act.wait_ge(q_proj[b], t + 1)
                        act.wait_ge(scored[b], t)
                        nc.scalar.activation(qT_high[b][:], proj[:], ACT.Copy, scale=D ** -0.5).then_inc(q_high_done[b], 1)

                def in_high_part(c, m, b):
                    act.wait_ge(head_in[b], 16 * own(c, m))
                    act.wait_ge(v_proj[1], own(c, m)) if mix else act.wait_ge(q_proj[b], turn(c, m))
                    nc.scalar.activation(wi_high[b][:], w_in[b][:], ACT.Copy).then_inc(in_high_done[b], 1)

                def out_high_part(c, m, b):
                    act.wait_ge(wo_in[b], 16 * turn(c, m))
                    act.wait_ge(y_done[b], turn(c, m))
                    nc.scalar.activation(wo_high[b][:], w_out[b][:], ACT.Copy).then_inc(wo_high_done[b], 1)

                def take_values(c, m, b, bank=None):
                    t = turn(c, m)
                    if mix:
                        act.wait_ge(v_proj[b], own(c, m) + 1)
                        act.wait_ge(ctx_done[1], t)
                        dst, src = vs[:, b], (bank or proj)[:].rearrange("p (i z) -> p i z", i=2)
                    else:
                        act.wait_ge(ctx_done[b], t)
                        dst, src = vs[b][:], v_all[:, :, :, bass.ds(m // 2 * D, D)].bitcast(F32)
                    nc.scalar.activation(dst, src, ACT.Copy).then_inc(v_ready[b], 1)

                def take_turned(c, m, b):
                    t = turn(c, m)
                    act.wait_ge(turned[b], t + 1)
                    act.wait_ge(ctx_done[b], t)
                    dst, done = (pT[b], pt_ready[b]) if mix else (pT_high[b], pt_high_done[b])
                    nc.scalar.activation(dst[:], t_ps[:, :, 0:WIDE], ACT.Copy).then_inc(done, 1)

                def exponentials(c, m, b):
                    t = turn(c, m)
                    act.wait_ge(peaked[b], t + 1)
                    for i in range(2):
                        for s in range(2):
                            row = probs[b][:, s, AT[i]:AT[i] + SEEN[i]]
                            last = nc.scalar.activation(row, row, ACT.Exp, bias=minus_peak[b][:, i, s:s + 1],
                                                        accum_out=total[b][:, i, s:s + 1])
                    last.then_inc(exped[b], 1)

                def take_context(c, m, b):
                    t = turn(c, m)
                    act.wait_ge(ctx_done[b], t + 1)
                    act.wait_ge(y_done[b], t)
                    if mix:
                        taken = nc.scalar.activation(oT_high[b][:], ctx_bank[:], ACT.Identity,
                                                     bias=vec[:, 2, bass.ds(2 * m + b, 1)])
                    else:
                        taken = nc.scalar.activation(oT_high[b][:], ctx_bank[:], ACT.Copy)
                    taken.then_inc(o_high_done[b], 1)

                if mix:
                    act.wait_ge(setup, 2)
                else:
                    act.wait_ge(const_in, 32)
                    nc.scalar.activation(kv_high[:], w_kv[:], ACT.Copy).then_inc(setup, 1)

                def take_chunk(c):
                    nc.scalar.activation(xc_high[:], k.xn[:, :, bass.ts(c, CH)], ACT.Copy).then_inc(xc_high_done, 1)

                take_chunk(0)
                if not mix:
                    in_high_part(0, 0, 0)
                    in_high_part(0, 0, 1)
                with act.Fori(0, NCH) as c:
                    if mix:
                        act.wait_ge(qk_in[0], 16 * own(c, 0))
                        act.wait_ge(qk_proj[0], own(c, 0))
                        nc.scalar.activation(qk_high[0][:], w_qk[0][:], ACT.Copy).then_inc(qk_high_done[0], 1)
                        with act.Fori(0, MH) as m:
                            bias_qk(c, m, 0)
                            bias_qk(c, m, 1)
                        act.wait_ge(sums_done, c + 1)
                        nc.scalar.activation(rms[:], s_ps[:, 0, 0:2 * CH // P], ACT.Sqrt, bias=eps6[:, 0:1],
                                             scale=1.0 / (HID * HEADS * D)).then_inc(rms_done, 1)
                        in_high_part(c, 0, 0)
                        act.wait_ge(inv_spread, c + 1)
                        nc.scalar.activation(inv_rms[:], t_ps[:], ACT.Copy).then_inc(inv_done, 1)
                    else:
                        def kv_high_part(i):
                            act.wait_ge(kv_proj, c * 8 + i + 1)
                            dst = k_high[:, i] if i < GROUPS else v_all[:, i - 4, 0]
                            nc.scalar.activation(dst, t_ps[:, i % 2], ACT.Copy).then_inc(kv_high_done, 1)

                    if mix:
                        take_queries(c, 0, 0)
                        take_queries(c, 0, 1)
                        take_values(c, 0, 0, ctx_bank)
                        exponentials(c, 0, 0)
                    else:
                        kv_high_part(0)
                        take_queries(c, 0, 0)
                        in_high_part(c, 1, 0)
                        kv_high_part(1)
                        take_queries(c, 0, 1)
                        kv_high_part(2)
                        exponentials(c, 0, 0)
                        for i in range(3, 8):
                            kv_high_part(i)
                        act.wait_ge(kv_ready, c * 8 + 8)
                        take_values(c, 0, 0)

                    def step(m, b, first, last):
                        nxt = (m, 1) if b == 0 else (m + 1, 0)
                        if not mix:
                            if last == 0:
                                take_queries(c, m + 1, b)
                        elif last == 0:
                            if b == 0:
                                take_queries(c, m + 1, b)
                            else:
                                in_high_part(c, m + 1, 0)
                                take_queries(c, m + 1, b)
                        if mix and b == 0:
                            take_values(c, m, 1)
                        take_turned(c, m, b)
                        if mix:
                            out_high_part(c, m, b)
                        if last < 2:
                            exponentials(c, *nxt)
                        if not mix:
                            if last < 2:
                                in_high_part(c, m + 1 + b, 1 - b)
                            out_high_part(c, m, b)
                        if last == 1:
                            take_chunk((c + 1) & (NCH - 1))
                        take_context(c, m, b)
                        if last < 2 and not mix:
                            take_values(c, *nxt)
                        if mix and b == 1 and last == 0:
                            take_values(c, m + 1, 0)

                    steps(act, c, step)

            @block.vector
            def _(dve):
                def sum_squares(c, m, b):
                    t = turn(c, m)
                    dve.wait_ge(acc_zero, c + len(CHANNEL_SHIFTS))
                    dve.wait_ge(qk_biased[b], own(c, m) + 1)
                    dve.wait_ge(*before(summed, b, own(c, m)))
                    nc.vector.tensor_tensor(acc[:, 0], acc[:, 0], sq_q[b][:], ALU.add)
                    nc.vector.tensor_tensor(acc[:, 1], acc[:, 1], sq_k[b][:], ALU.add).then_inc(summed[b], 1)

                def take_queries(c, m, b):
                    t = turn(c, m)
                    dve.wait_ge(q_proj[b], t + 1)
                    dve.wait_ge(scored[b], t)
                    nc.vector.scalar_tensor_tensor(out=qT[b][:], in0=proj[:], scalar=D ** -0.5, in1=inv_rms[:, 0],
                                                   op0=ALU.mult, op1=ALU.mult).then_inc(q_ready[b], 1)
                    h = 2 * m + b
                    nc.vector.scalar_tensor_tensor(out=kT[b][:], in0=k_all[:, h], scalar=vec[:, 4, bass.ds(h, 1)],
                                                   in1=inv_rms[:, 1], op0=ALU.mult, op1=ALU.mult).then_inc(k_ready[b], 1)

                def qk_high_part(c, m, b):
                    dve.wait_ge(qk_in[b], 16 * own(c, m))
                    dve.wait_ge(qk_proj[b], own(c, m))
                    nc.vector.tensor_copy(qk_high[b][:], w_qk[b][:]).then_inc(qk_high_done[b], 1)

                def low_part(done, low, whole, high):
                    nc.vector.tensor_tensor(low, whole, high.bitcast(F32), ALU.subtract).then_inc(done, 1)

                def queries_low(c, m, b):
                    dve.wait_ge(q_high_done[b], turn(c, m) + 1)
                    nc.vector.scalar_tensor_tensor(out=qT_low[b][:], in0=proj[:], scalar=D ** -0.5,
                                                   in1=qT_high[b][:].bitcast(F32), op0=ALU.mult, op1=ALU.subtract
                                                   ).then_inc(q_ready[b], 1)

                def turned_low(c, m, b):
                    dve.wait_ge(pt_high_done[b], turn(c, m) + 1)
                    low_part(pt_ready[b], pT_low[b][:], t_ps[:, :, 0:WIDE], pT_high[b][:])

                def mask_scores(c, m, b):
                    t = turn(c, m)
                    dve.wait_ge(scored[b], t + 1)
                    dve.wait_ge(turned[b], t)
                    nc.vector.tensor_tensor(probs[b][:], s_ps[:, :, 0:WIDE], mask[:].unsqueeze(1).to_broadcast([P, 2, WIDE]),
                                            ALU.add).then_inc(masked[b], 1)
                    dve.wait_ge(masked[b], t + 1)
                    for i in range(2):
                        last = nc.vector.tensor_reduce(minus_peak[b][:, i], probs[b][:, :, AT[i]:AT[i] + SEEN[i]], AX_X,
                                                       ALU.max, negate=True)
                    last.then_inc(peaked[b], 1)

                def normalise(c, m, b):
                    t = turn(c, m)
                    dve.wait_ge(exped[b], t + 1)
                    nc.vector.reciprocal(inverse[b][:], total[b][:]).then_inc(inverted[b], 1)
                    dve.wait_ge(inverted[b], t + 1)
                    for i in range(2):
                        rows = probs[b][:, :, AT[i]:AT[i] + SEEN[i]]
                        last = nc.vector.tensor_tensor(rows, rows, inverse[b][:, i].unsqueeze(2).to_broadcast([P, 2, SEEN[i]]),
                                                       ALU.mult)
                    last.then_inc(normed[b], 1)

                def take_context(c, m, b):
                    dve.wait_ge(o_high_done[b], turn(c, m) + 1)
                    if mix:
                        nc.vector.scalar_tensor_tensor(out=oT_low[b][:], in0=ctx_bank[:], scalar=vec[:, 2, bass.ds(2 * m + b, 1)],
                                                       in1=oT_high[b][:].bitcast(F32), op0=ALU.add, op1=ALU.subtract
                                                       ).then_inc(o_ready[b], 1)
                    else:
                        low_part(o_ready[b], oT_low[b][:], ctx_bank[:], oT_high[b][:])

                dve.wait_ge(const_in, 80 if mix else 32)
                if mix:
                    nc.vector.memset(eps6[:], 1e-6 / HID ** 2)
                    nc.vector.tensor_scalar(circ[:], shifts[:, 0], w_mix[:, 0:1], None, ALU.mult).then_inc(setup, 1)
                    for i in range(len(CHANNEL_SHIFTS)):
                        dve.wait_ge(setup, 1) if i == 0 else dve.wait_ge(acc_zero, i)
                        last = nc.vector.scalar_tensor_tensor(out=circ[:], in0=shifts[:, i + 1], scalar=w_mix[:, i + 1:i + 2],
                                                              in1=circ[:], op0=ALU.mult, op1=ALU.add)
                        last.then_inc(acc_zero if i + 1 < len(CHANNEL_SHIFTS) else setup, 1)
                else:
                    dve.wait_ge(setup, 1)
                    nc.vector.tensor_tensor(kv_low[:], w_kv[:], kv_high[:].bitcast(F32), ALU.subtract).then_inc(setup, 1)
                with dve.Fori(0, NCH) as c:
                    if mix:
                        qk_high_part(c, 0, 1)
                        nc.vector.memset(acc[:], 0.0).then_inc(acc_zero, 1)
                        with dve.Fori(0, MH - 1) as m:
                            for b in range(2):
                                qk_high_part(c, m + 1, b)
                                sum_squares(c, m, b)
                        sum_squares(c, MH - 1, 0)
                        sum_squares(c, MH - 1, 1)
                        dve.wait_ge(rms_done, c + 1)
                        nc.vector.reciprocal(inverse_rms[:], rms[:]).then_inc(inverse_done, 1)
                        dve.wait_ge(inverse_done, c + 1)
                        nc.vector.tensor_tensor(diag[:].rearrange("p i (t q) -> p (i t) q", q=P),
                                                k.ident[:].unsqueeze(1).to_broadcast([P, 2 * CH // P, P]),
                                                inverse_rms[:].unsqueeze(2).to_broadcast([P, 2 * CH // P, P]), ALU.mult
                                                ).then_inc(diag_done, 1)
                        dve.wait_ge(inv_done, c + 1)
                        take_queries(c, 0, 0)
                        take_queries(c, 0, 1)
                    else:
                        def kv_low_part(i):
                            dve.wait_ge(kv_high_done, c * 8 + i + 1)
                            dst = (k_low[:, i], k_high[:, i]) if i < GROUPS else (v_all[:, i - 4, 1], v_all[:, i - 4, 0])
                            low_part(kv_ready, dst[0], t_ps[:, i % 2], dst[1])

                        kv_low_part(0)
                        queries_low(c, 0, 0)
                        kv_low_part(1)
                    mask_scores(c, 0, 0)
                    if mix:
                        normalise(c, 0, 0)
                    else:
                        queries_low(c, 0, 1)
                        kv_low_part(2)
                        kv_low_part(3)
                        normalise(c, 0, 0)
                        for i in range(4, 8):
                            kv_low_part(i)

                    def step(m, b, first, last):
                        nxt = (m, 1) if b == 0 else (m + 1, 0)
                        if last < 2:
                            mask_scores(c, *nxt)
                        if not mix:
                            turned_low(c, m, b)
                        if last == 0:
                            (take_queries if mix else queries_low)(c, m + 1, b)
                        if last < 2:
                            normalise(c, *nxt)
                        take_context(c, m, b)

                    steps(dve, c, step)
                    dve.wait_ge(y_done[1], turn(c, MH - 1) + 1)
                    for kt in range(KT):
                        x = k.x[:, kt, bass.ts(c, CH)]
                        if mix:
                            add = nc.vector.scalar_tensor_tensor(out=x, in0=y[kt][:], scalar=b_out[:, kt:kt + 1], in1=x,
                                                                 op0=ALU.add, op1=ALU.add)
                        else:
                            add = nc.vector.tensor_tensor(x, y[kt][:], x, ALU.add)
                    add.then_inc(y_added, 1)


def store_result(nc, k, out):
    stored = k.sem("result_stored")
    block = nc.Block()
    with block:
        @block.sync
        def _(sp):
            sp.dma_start(out, k.x[:]).then_inc(stored, 16)
            sp.wait_ge(stored, 16)


def macaron(nc, a, out):
    w0 = nc.dram_tensor("ffn0_weights", [T0, P, WCOL], F32, kind="Internal").ap()
    with ExitStack() as ctx:
        k = Core(nc, ctx)
        sb = lambda name, shape, dt: ctx.enter_context(nc.sbuf_tensor(name, shape, dt))
        k.x = sb("x", [P, KT, TOK], F32)
        k.mean_mat = sb("mean_mat", [P, P], F32)
        k.eps = sb("eps", [P, 1], F32)
        k.ident = sb("ident", [P, P], F32)
        k.weights = sb("combine_weights", [P, TOK // P * EX], F32)
        k.plan = sb("plan", [1, PLAN], I32)
        k.turns_run = sb("turns_run", [1, 1], F32)
        ps = lambda name, *shape: ctx.enter_context(nc.psum_tensor(name, [P, *shape, CH], F32))
        low, k.pair, high = [ps(f"bank{i}") for i in range(3)], [ps("banks34", 2), ps("banks56", 2)], ps("bank7")
        k.bank = low + [k.pair[0][:, 0], k.pair[0][:, 1], k.pair[1][:, 0], k.pair[1][:, 1], high]
        set_constants(nc, k)
        dequantise(nc, k, a["ffn0_codes"], a["ffn0_scales"], w0, a["x"], a["ident"])
        k.retire("dq")

        def ffn0(tag):
            with ExitStack() as inner:
                k.xn_high = inner.enter_context(nc.sbuf_tensor(f"xn_high_{tag}", [P, KT, TOK], F32R))
                k.xn_low = inner.enter_context(nc.sbuf_tensor(f"xn_low_{tag}", [P, KT, TOK], F32R))
                layernorm(nc, k, tag, True)
                feed_forward(nc, k, tag, P, w0[:, :, 0:2 * HID], w0[:, :, 2 * HID:], ACT.Gelu_apprx_tanh)

        def ffn1(tag):
            with ExitStack() as inner:
                k.xn_high = inner.enter_context(nc.sbuf_tensor(f"xn_high_{tag}", [P, KT, TOK], F32R))
                k.xn_low = inner.enter_context(nc.sbuf_tensor(f"xn_low_{tag}", [P, KT, TOK], F32R))
                layernorm(nc, k, tag, True)
                route(nc, k, tag, a["router"], a["router_bias"], a["plan_consts"])
                experts(nc, k, tag, a["ffn1_gu"], a["ffn1_down"])

        def attn(tag, mix):
            with ExitStack() as inner:
                k.xn = inner.enter_context(nc.sbuf_tensor(f"xn_{tag}", [P, KT, TOK], F32))
                layernorm(nc, k, tag, False)
                attention(nc, k, tag, a, mix)

        ffn0("f0")
        attn("a0", False)
        ffn0("f1")
        k.retire("gqa")
        k.retire("fp4")
        ffn1("f2")
        attn("a1", True)
        ffn1("f3")
        store_result(nc, k, out)


def planes(w):
    return w.reshape(P, KT, *w.shape[1:])


def lay_out(i):
    a = {}
    tokens = lambda x: np.ascontiguousarray(x)
    a["x"] = tokens(i["L0_attn_x"].reshape(TOK, P, KT).transpose(1, 2, 0))
    units = T0 // 2

    def rows(w):
        return w.reshape(units, P, 2, -1).transpose(0, 3, 2, 1)

    def down(w):
        return w.reshape(P, KT, units, -1).transpose(2, 3, 1, 0)

    join = lambda g, u, d: np.concatenate([z.reshape(units, -1, HID) for z in (g, u, d)], axis=2)
    a["ffn0_codes"] = join(rows(i["L0_ffn_gate_W_packed"]), rows(i["L0_ffn_up_W_packed"]),
                           down(i["L0_ffn_down_W_packed"]))
    a["ffn0_scales"] = join(rows(i["L0_ffn_gate_scales"]), rows(i["L0_ffn_up_scales"]),
                            down(i["L0_ffn_down_scales"]))
    def columns(w, shared):
        w = np.concatenate([w, shared.reshape(HID, EX - NE, MI).transpose(1, 0, 2)])
        return w.reshape(EX, P, KT, MI)

    a["ffn1_gu"] = np.concatenate([columns(i["L1_ffn_gate_w"], i["L1_ffn_sh_gate_w"]),
                                   columns(i["L1_ffn_up_w"], i["L1_ffn_sh_up_w"])], axis=3)
    d = np.concatenate([i["L1_ffn_down_w"].reshape(ROUTED, HID), i["L1_ffn_sh_down_w"]])
    a["ffn1_down"] = d.reshape(EX, 2, ER, P, KT).transpose(0, 2, 1, 4, 3).reshape(EX, ER, 2, HID)
    e = np.arange(EX)
    a["plan_consts"] = np.concatenate([e[:, None] < e, np.ones((EX, EX)), np.tile(e, (EX, 1)), e[:, None],
                                       e[:, None] == EX - 1, NO_PLACE * (e[:, None] < NE)], axis=1).astype(np.float32)
    a["router"] = planes(i["L1_ffn_w_router"])
    a["router_bias"] = i["L1_ffn_corr_bias"].reshape(1, NE)
    by_head = lambda w: planes(w).reshape(P, KT, HEADS, D).transpose(2, 0, 1, 3).reshape(HEADS, P, HID)
    q = by_head(i["L0_attn_w_q"])
    a["attn0_q"] = np.concatenate([q, q[0:2]])
    a["attn0_kv"] = planes(i["L0_attn_w_kv"]).reshape(P, KT, 2, GROUPS * D).transpose(0, 2, 1, 3)
    outs = lambda w: w.reshape(HEADS, D, P, KT).transpose(0, 1, 3, 2).reshape(HEADS, D, HID)
    a["attn0_o"] = outs(i["L0_attn_w_dense"])
    a["attn1_qk"] = np.concatenate([by_head(i["L1_attn_wq"].T), by_head(i["L1_attn_wk"].T)], axis=2)
    a["attn1_v"] = (by_head(i["L1_attn_wv"].T).reshape(HEADS // 2, 2, P, KT, D).transpose(0, 2, 3, 1, 4)
                    .reshape(HEADS // 2, P, 2 * HID))
    a["attn1_o"] = outs(i["L1_attn_wo"].T)
    a["attn1_vec"] = np.stack([i[f"L1_attn_{n}"].reshape(HEADS, D) for n in ("bq", "bk", "bv", "gq", "gk")]
                              ).transpose(2, 0, 1)
    a["attn1_bo"] = i["L1_attn_bo"].reshape(P, KT)
    a["w_mix"] = i["L1_attn_w_mix"].reshape(1, -1)
    eye = np.eye(P, dtype=np.float32)
    a["shift_mats"] = np.stack([np.roll(eye, s, axis=1) for s in (0,) + CHANNEL_SHIFTS], axis=1)
    q, key = np.arange(SEQ)[:, None], np.arange(SEQ)[None, :]
    near = np.isin((q - key) % SEQ, np.array(SEQ_SHIFTS) % SEQ)
    lay_mask = lambda seen: np.where(seen, 0.0, -BIG).astype(np.float32).reshape(2, P, SEQ).transpose(1, 0, 2).reshape(P, 2 * SEQ)
    a["near_mask"] = lay_mask(near)
    a["causal_mask"] = np.delete(lay_mask(q >= key), np.s_[P:SEQ], axis=1)
    a["ident"] = np.eye(P, dtype=np.float32)
    return {n: np.ascontiguousarray(v) for n, v in a.items()}


def kernel(**inputs):
    import concourse.bacc as bacc
    from concourse.bass_utils import run_bass_kernel_spmd

    nc = bacc.Bacc("TRN2", target_bir_lowering=False, num_devices=1)
    arrays = lay_out({n: np.asarray(v) for n, v in inputs.items()})
    aps = {n: nc.dram_tensor(f"in_{n}", v.shape, mybir.dt.from_np(v.dtype), kind="ExternalInput").ap()
           for n, v in arrays.items()}
    out = nc.dram_tensor("out_0_dram", (P, KT, TOK), F32, kind="ExternalOutput").ap()
    macaron(nc, aps, out)
    r = run_bass_kernel_spmd(nc, [{f"in_{n}": v for n, v in arrays.items()}], core_ids=[0])
    y = r.results[0]["out_0_dram"]
    return np.ascontiguousarray(y.transpose(2, 0, 1)).reshape(BATCH, SEQ, HID)
```
